# Optimizing a Trainium2 kernel written in Bass

```python
import numpy as np
import jax
import jax.numpy as jnp

def _softmax(x, axis=-1):
    return jax.nn.softmax(x, axis=axis)

def _gelu(x):
    return jax.nn.gelu(x, approximate=True)

def _silu(x):
    return jax.nn.silu(x)

def _sigmoid(x):
    return jax.nn.sigmoid(x)

def _layernorm(x, axis=-1, eps=1e-05):
    m = jnp.mean(x, axis=axis, keepdims=True)
    v = jnp.var(x, axis=axis, keepdims=True)
    return (x - m) / jnp.sqrt(v + eps)

def _scatter_add(tgt, idx, src, axis=0):
    return tgt.at[idx].add(src)

def _segment_sum(src, seg, n):
    return jax.ops.segment_sum(src, seg, n)
kernel_name = 'mk_xattn_ffn_d2_seqx_r8_58f21c'

def setup_inputs(seed: int=0):
    np.random.seed(seed)
    _w = jnp.asarray

    def _rec_inputs():
        import jax
        import jax.numpy as jnp
        _rk = jax.random.key(seed)
        x = -0.0003929 + 0.9999 * jax.random.normal(jax.random.fold_in(_rk, 1), (4, 256, 256), jnp.float32)
        _lenS = 256 - jax.random.randint(jax.random.fold_in(_rk, 7), (4,), 0, max(1, 256 // 4) + 1, jnp.int32)
        _lenS2 = 1601 - jax.random.randint(jax.random.fold_in(_rk, 8), (4,), 0, max(1, 1601 // 4) + 1, jnp.int32)
        _ctx_2048P = jax.random.normal(jax.random.fold_in(_rk, 11), (4, 16, 256), jnp.float32)
        _ctx_2048c = jax.random.dirichlet(jax.random.fold_in(_rk, 511), 0.3 * jnp.ones((16,), jnp.float32), (4, 1601))
        _ctx_2048t = jnp.einsum('bsk,bkd->bsd', _ctx_2048c, _ctx_2048P)
        _ctx_2048t = _ctx_2048t * jax.lax.rsqrt(jnp.mean(jnp.square(_ctx_2048t)) + 1e-12) * 0.953939
        ctx_2048 = -1.39393e-06 + 0.999914 * (_ctx_2048t + 0.3 * jax.random.normal(jax.random.fold_in(_rk, 611), (4, 1601, 256), jnp.float32))
        itok_BxS_0_1023 = jax.random.randint(jax.random.fold_in(_rk, 12), (4, 256), 0, 128, jnp.int32)
        return (x, ctx_2048, itok_BxS_0_1023)
    x, ctx_2048, itok_BxS_0_1023 = _rec_inputs()

    def _L0_xattn_setup():
        import jax, jax.numpy as jnp
        import numpy as np
        B, Lq, Lk = (2, 512, 128)
        Q_DIM, KV_DIM = (256, 256)
        H, HD = (16, 128)
        KVC, QC, R = (64, 96, 64)
        LOOKBACK = 8
        NEG = -1e+30

        def _rope(x, L):
            half = x.shape[-1] // 2
            inv_freq = 1.0 / 10000.0 ** (jnp.arange(half, dtype=jnp.float32) / half)
            ang = jnp.arange(L, dtype=jnp.float32)[:, None] * inv_freq
            cos, sin = (jnp.cos(ang), jnp.sin(ang))
            x1, x2 = (x[..., :half], x[..., half:])
            return jnp.concatenate([x1 * cos - x2 * sin, x1 * sin + x2 * cos], axis=-1)
        key = jax.random.key(seed)
        ks = jax.random.split(key, 11)

        def w(k, shape, fan_in):
            return jax.random.normal(k, shape, jnp.float32) / np.sqrt(fan_in).astype(np.float32)
        return {'q': jax.random.normal(ks[0], (B, Lq, Q_DIM), jnp.float32), 'kv': jax.random.normal(ks[1], (B, Lk, KV_DIM), jnp.float32), 'seg_id': jnp.sort(jax.random.randint(ks[2], (B, Lq), 0, Lk), axis=-1), 'W_kvc': w(ks[3], (KV_DIM, KVC), KV_DIM), 'W_dq': w(ks[4], (Q_DIM, QC), Q_DIM), 'W_uq': w(ks[5], (QC, H * HD), QC), 'W_qr': w(ks[6], (QC, H * R), QC), 'W_uk': w(ks[7], (KVC, H * HD), KVC), 'W_kr': w(ks[8], (KVC, R), KVC), 'W_uv': w(ks[9], (KVC, H * HD), KVC), 'W_o': w(ks[10], (H * HD, Q_DIM), H * HD)}
    _L0_xattn_all = _L0_xattn_setup()
    _L0_xattn_in = {k: v for k, v in _L0_xattn_all.items() if k in ('W_kvc', 'W_dq', 'W_uq', 'W_qr', 'W_uk', 'W_kr', 'W_uv', 'W_o')}
    del _L0_xattn_all

    def _L0_ffn_setup():
        import jax, jax.numpy as jnp
        import numpy as np
        B, S, D, I, E, K = (4, 128, 256, 128, 8, 2)
        key = jax.random.key(seed)
        ks = jax.random.split(key, 7)

        def w(k, shape, fan_in):
            return jax.random.normal(k, shape, dtype=jnp.float32) * fan_in ** (-0.5)
        return {'hidden_states': jax.random.normal(ks[0], (B, S, D), dtype=jnp.float32), 'router_w': w(ks[1], (D, E), D), 'gate_up_w': w(ks[2], (E, D, 2 * I), D), 'down_w': w(ks[3], (E, I, D), I), 'shared_gate_w': w(ks[4], (D, I), D), 'shared_up_w': w(ks[5], (D, I), D), 'shared_down_w': w(ks[6], (I, D), I)}
    _L0_ffn_all = _L0_ffn_setup()
    _L0_ffn_in = {k: v for k, v in _L0_ffn_all.items() if k in ('router_w', 'gate_up_w', 'down_w', 'shared_gate_w', 'shared_up_w', 'shared_down_w')}
    del _L0_ffn_all

    def _L1_xattn_setup():
        import jax, jax.numpy as jnp
        import numpy as np
        NUM_HEADS = 16

        def _qdq(x):
            s = jnp.maximum(jnp.max(jnp.abs(x), axis=-1, keepdims=True) / 127.0, 1e-08)
            return jnp.clip(jnp.round(x / s), -127.0, 127.0) * s
        key = jax.random.key(seed)
        ks = jax.random.split(key, 8)
        B, N, M, D = (2, 512, 64, 256)
        w_std = 0.02
        return {'x': jax.random.normal(ks[0], (B, N, D), jnp.float32), 'cond': jax.random.normal(ks[1], (B, M, D), jnp.float32), 'wq': jax.random.normal(ks[2], (D, D), jnp.float32) * w_std, 'bq': jax.random.normal(ks[3], (D,), jnp.float32) * w_std, 'wkv': jax.random.normal(ks[4], (2 * D, D), jnp.float32) * w_std, 'bkv': jax.random.normal(ks[5], (2 * D,), jnp.float32) * w_std, 'wp': jax.random.normal(ks[6], (D, D), jnp.float32) * w_std, 'bp': jax.random.normal(ks[7], (D,), jnp.float32) * w_std}
    _L1_xattn_all = _L1_xattn_setup()
    _L1_xattn_in = {k: v for k, v in _L1_xattn_all.items() if k in ('wq', 'bq', 'wkv', 'bkv', 'wp', 'bp')}
    del _L1_xattn_all

    def _L1_ffn_setup():
        import jax, jax.numpy as jnp
        import numpy as np
        DIM = 256
        N_EXPERTS = 8
        TOP_K = 2
        key = jax.random.key(seed)
        ks = jax.random.split(key, 5)
        x = jax.random.normal(ks[0], (4, 512, DIM), dtype=jnp.float32)
        W_up = jax.random.normal(ks[1], (DIM, DIM), dtype=jnp.float32) * (1.0 / np.sqrt(DIM))
        W_down = jax.random.normal(ks[2], (DIM, DIM), dtype=jnp.float32) * (1.0 / np.sqrt(DIM))
        W_gate = jax.random.normal(ks[3], (N_EXPERTS, DIM), dtype=jnp.float32) * (1.0 / np.sqrt(DIM))
        W_expert = jax.random.normal(ks[4], (DIM, DIM), dtype=jnp.float32) * (1.0 / np.sqrt(DIM))
        return {'x': x, 'W_up': W_up, 'W_down': W_down, 'W_gate': W_gate, 'W_expert': W_expert}
    _L1_ffn_all = _L1_ffn_setup()
    _L1_ffn_in = {k: v for k, v in _L1_ffn_all.items() if k in ('W_up', 'W_down', 'W_gate', 'W_expert')}
    del _L1_ffn_all
    return {'x': x, 'ctx_2048': ctx_2048, 'itok_BxS_0_1023': itok_BxS_0_1023, 'L0_xattn_W_kvc': _L0_xattn_in['W_kvc'], 'L0_xattn_W_dq': _L0_xattn_in['W_dq'], 'L0_xattn_W_uq': _L0_xattn_in['W_uq'], 'L0_xattn_W_qr': _L0_xattn_in['W_qr'], 'L0_xattn_W_uk': _L0_xattn_in['W_uk'], 'L0_xattn_W_kr': _L0_xattn_in['W_kr'], 'L0_xattn_W_uv': _L0_xattn_in['W_uv'], 'L0_xattn_W_o': _L0_xattn_in['W_o'], 'L0_ffn_router_w': _L0_ffn_in['router_w'], 'L0_ffn_gate_up_w': _L0_ffn_in['gate_up_w'], 'L0_ffn_down_w': _L0_ffn_in['down_w'], 'L0_ffn_shared_gate_w': _L0_ffn_in['shared_gate_w'], 'L0_ffn_shared_up_w': _L0_ffn_in['shared_up_w'], 'L0_ffn_shared_down_w': _L0_ffn_in['shared_down_w'], 'L1_xattn_wq': _L1_xattn_in['wq'], 'L1_xattn_bq': _L1_xattn_in['bq'], 'L1_xattn_wkv': _L1_xattn_in['wkv'], 'L1_xattn_bkv': _L1_xattn_in['bkv'], 'L1_xattn_wp': _L1_xattn_in['wp'], 'L1_xattn_bp': _L1_xattn_in['bp'], 'L1_ffn_W_up': _L1_ffn_in['W_up'], 'L1_ffn_W_down': _L1_ffn_in['W_down'], 'L1_ffn_W_gate': _L1_ffn_in['W_gate'], 'L1_ffn_W_expert': _L1_ffn_in['W_expert']}

def reference(x, ctx_2048, itok_BxS_0_1023, L0_xattn_W_kvc, L0_xattn_W_dq, L0_xattn_W_uq, L0_xattn_W_qr, L0_xattn_W_uk, L0_xattn_W_kr, L0_xattn_W_uv, L0_xattn_W_o, L0_ffn_router_w, L0_ffn_gate_up_w, L0_ffn_down_w, L0_ffn_shared_gate_w, L0_ffn_shared_up_w, L0_ffn_shared_down_w, L1_xattn_wq, L1_xattn_bq, L1_xattn_wkv, L1_xattn_bkv, L1_xattn_wp, L1_xattn_bp, L1_ffn_W_up, L1_ffn_W_down, L1_ffn_W_gate, L1_ffn_W_expert):
    import jax
    import jax.numpy as jnp

    def _L0_xattn_ref(q, kv, seg_id, W_kvc, W_dq, W_uq, W_qr, W_uk, W_kr, W_uv, W_o):
        import jax, jax.numpy as jnp
        import numpy as np
        B, Lq, Lk = (2, 512, 128)
        Q_DIM, KV_DIM = (256, 256)
        H, HD = (16, 128)
        KVC, QC, R = (64, 96, 64)
        LOOKBACK = 8
        NEG = -1e+30

        def _rope(x, L):
            half = x.shape[-1] // 2
            inv_freq = 1.0 / 10000.0 ** (jnp.arange(half, dtype=jnp.float32) / half)
            ang = jnp.arange(L, dtype=jnp.float32)[:, None] * inv_freq
            cos, sin = (jnp.cos(ang), jnp.sin(ang))
            x1, x2 = (x[..., :half], x[..., half:])
            return jnp.concatenate([x1 * cos - x2 * sin, x1 * sin + x2 * cos], axis=-1)
        b, lq, _ = q.shape
        lk = kv.shape[1]
        kv_c = kv @ W_kvc
        q_c = q @ W_dq
        q_nope = (q_c @ W_uq).reshape(b, lq, H, HD).transpose(0, 2, 1, 3)
        q_rope = (q_c @ W_qr).reshape(b, lq, H, R).transpose(0, 2, 1, 3)
        k_nope = (kv_c @ W_uk).reshape(b, lk, H, HD)
        v = (kv_c @ W_uv).reshape(b, lk, H, HD)
        k_rope = kv_c @ W_kr
        q_rope = _rope(q_rope, lq)
        k_rope = _rope(k_rope, lk)
        scale = 1.0 / np.sqrt(HD + R).astype(np.float32)
        scores = (jnp.einsum('bhqd,bkhd->bhqk', q_nope, k_nope) + jnp.einsum('bhqr,bkr->bhqk', q_rope, k_rope)) * scale
        k_ids = jnp.arange(lk)[None, None, :]
        qs = seg_id[:, :, None]
        good = (k_ids <= qs) & (k_ids >= qs - LOOKBACK)
        scores = jnp.where(good[:, None, :, :], scores, NEG)
        attn = jax.nn.softmax(scores, axis=-1)
        out = jnp.einsum('bhqk,bkhd->bqhd', attn, v).reshape(b, lq, H * HD)
        return out @ W_o

    def _L0_ffn_ref(hidden_states, router_w, gate_up_w, down_w, shared_gate_w, shared_up_w, shared_down_w):
        import jax, jax.numpy as jnp
        import numpy as np
        B, S, D, I, E, K = (4, 128, 256, 128, 8, 2)
        Bb, Ss, Dd = hidden_states.shape
        x = hidden_states.reshape(-1, Dd)
        T = x.shape[0]
        shared = jax.nn.silu(x @ shared_gate_w) * (x @ shared_up_w) @ shared_down_w
        logits = x @ router_w
        top_val, top_idx = jax.lax.top_k(logits, K)
        probs = jnp.zeros_like(logits).at[jnp.arange(T)[:, None], top_idx].set(jax.nn.sigmoid(top_val))
        xin = probs.T[:, :, None] * x[None]
        gu = jnp.einsum('etd,edf->etf', xin, gate_up_w)
        gate, up = jnp.split(gu, 2, axis=-1)
        h = jax.nn.silu(gate) * up
        expert_out = jnp.einsum('eti,eid->etd', h, down_w)
        combined = shared + expert_out.sum(axis=0)
        return combined.reshape(Bb, Ss, Dd)

    def _L1_xattn_ref(x, cond, wq, bq, wkv, bkv, wp, bp):
        import jax, jax.numpy as jnp
        import numpy as np
        NUM_HEADS = 16

        def _qdq(x):
            s = jnp.maximum(jnp.max(jnp.abs(x), axis=-1, keepdims=True) / 127.0, 1e-08)
            return jnp.clip(jnp.round(x / s), -127.0, 127.0) * s
        B, N, C = x.shape
        M = cond.shape[1]
        H = NUM_HEADS
        Dh = C // H
        q = _qdq(x) @ _qdq(wq).T + bq
        kv = cond @ wkv.T + bkv
        k, v = jnp.split(kv, 2, axis=-1)
        q = q.reshape(B, N, H, Dh)
        k = k.reshape(B, M, H, Dh)
        v = v.reshape(B, M, H, Dh)
        scale = 1.0 / np.sqrt(Dh)
        attn = jax.nn.softmax(jnp.einsum('bnhd,bmhd->bhnm', q, k) * scale, axis=-1)
        o = jnp.einsum('bhnm,bmhd->bnhd', attn, v).reshape(B, N, C)
        out = _qdq(o) @ _qdq(wp).T + bp
        return out

    def _L1_ffn_ref(x, W_up, W_down, W_gate, W_expert):
        import jax, jax.numpy as jnp
        import numpy as np
        DIM = 256
        N_EXPERTS = 8
        TOP_K = 2
        logits = jnp.einsum('bsd,ed->bse', x, W_gate)
        routing_weights, selected_experts = jax.lax.top_k(logits, TOP_K)
        shared_out = jnp.einsum('bsd,od->bso', jax.nn.relu(jnp.einsum('bsd,od->bso', x, W_up)), W_down)
        rw = jax.nn.softmax(routing_weights, axis=-1)
        expert_out = jnp.einsum('bsd,do->bso', x, W_expert)
        moe_out = jnp.sum(rw, axis=-1, keepdims=True) * expert_out
        return shared_out + moe_out
    x = x + _L0_xattn_ref(_layernorm(x, axis=-1), ctx_2048, itok_BxS_0_1023, L0_xattn_W_kvc, L0_xattn_W_dq, L0_xattn_W_uq, L0_xattn_W_qr, L0_xattn_W_uk, L0_xattn_W_kr, L0_xattn_W_uv, L0_xattn_W_o)
    x = x + _L0_ffn_ref(_layernorm(x, axis=-1), L0_ffn_router_w, L0_ffn_gate_up_w, L0_ffn_down_w, L0_ffn_shared_gate_w, L0_ffn_shared_up_w, L0_ffn_shared_down_w)
    x = x + _L1_xattn_ref(_layernorm(x, axis=-1), ctx_2048, L1_xattn_wq, L1_xattn_bq, L1_xattn_wkv, L1_xattn_bkv, L1_xattn_wp, L1_xattn_bp)
    x = x + _L1_ffn_ref(_layernorm(x, axis=-1), L1_ffn_W_up, L1_ffn_W_down, L1_ffn_W_gate, L1_ffn_W_expert)
    return x

_drawn_inputs = setup_inputs


def setup_inputs(seed=0):
    import zlib

    import numpy as np

    out = dict(_drawn_inputs(seed))
    spreads = {}
    factors = {'L1_xattn_wq': 40.985,
     'L1_xattn_bq': 200.0,
     'L1_xattn_bkv': 8.0,
     'L1_xattn_bp': 3.826,
     'L1_ffn_W_gate': 200.0}
    for name, (base, spread) in spreads.items():
        noise = np.random.default_rng([zlib.crc32(name.encode()), seed]).standard_normal(out[name].shape)
        drawn = base * np.exp(spread * noise) if base else spread * noise
        out[name] = jnp.asarray(drawn.astype(out[name].dtype))
    for name, factor in factors.items():
        out[name] = (out[name] * factor).astype(out[name].dtype)
    return out
```

```python
from contextlib import ExitStack

import numpy as np

import concourse.bass as bass
from concourse import mybir

F32 = mybir.dt.float32
BF16 = mybir.dt.bfloat16
I32 = mybir.dt.int32
U32 = mybir.dt.uint32
ACT = mybir.ActivationFunctionType
ALU = mybir.AluOpType
AX_X = mybir.AxisListType.X

P = 128
B, LQ, D = 4, 256, 256
KEYS = 1601
TOK = B * LQ
TILES = TOK // P
FC = D // P
H = 16
HD, KVC, QC, R = 128, 64, 96, 64
LOOKBACK = 8
K0 = 128
MASK = float(2.0 ** 99)
SCALE0 = float(1.0 / np.sqrt(HD + R).astype(np.float32))
E, I = 8, 128
HB = E + 1
DH = D // H
SCALE1 = float(1.0 / np.sqrt(DH))
KT = (KEYS + P - 1) // P
KLAST = KEYS - (KT - 1) * P
HALF = H // 2
STAGES = B * 2
QUADS = STAGES * 2
STEPS = QUADS * KT
STACK_Q = (0, 0, 1, 0, 2, 1)
STACK_K = (0, 1, 0, 2, 0, 1)
SROWS = len(STACK_Q) * DH
VW = DH + 1
CH = [(0, 401), (401, 400), (801, 400), (1201, 400)]
MAGIC = float(1.5 * 2 ** 23)
LN_EPS = 1e-5


def schedule():
    beside = {}

    def put(quad, kt, job):
        beside.setdefault((quad, kt), []).append(job)

    for quad in range(QUADS + 1):
        if quad + 1 < QUADS:
            for n in range(8 * len(CH)):
                put(quad, n * 10 // (8 * len(CH)), ("max", quad + 1, n))
            put(quad, 11, ("shift", quad + 1))
        s = (quad + 3) // 2
        if quad % 2 == 1 and 2 <= s < STAGES:
            for c in range(len(CH)):
                put(quad, 3 + c, ("k", s, c))
            if s % 2 == 0:
                for j in range((KT + 1) // 2):
                    put(quad + j // 4, (8 + j) if j < 4 else j, ("v", s // 2, j))
        if quad >= 1:
            put(quad, 2, ("out", quad - 1))
        if quad >= 4 and quad % 4 == 0:
            for n in range(10):
                put(quad, 3 + n, ("tail", 2 * (quad // 4 - 1) + n // 5, n % 5))
    return beside


BESIDE = schedule()


def program(nc, x_in, ctx_in, ctx0_in, seg_in, ident_in, tabs_in, kk_in, ones_in, wkvc_in, wkr_in, wkrs_in,
            wdq_in, wuq_in, wuk_in, wqr_in, wqrs_in, wuv_in, wo_in, router_in, gu_in, sgu_in, down_in, sdown_in,
            wq_in, wp_in, wkv_in, bk_in, rows_in, wup_in, wdn_in, wex_in, wg_in, out):
    with ExitStack() as ctx:
        def sb(name, cols, dt=F32):
            return ctx.enter_context(nc.sbuf_tensor(name, [P, cols], dt))

        def sem(name):
            return ctx.enter_context(nc.semaphore(name))

        ps = ctx.enter_context(nc.psum_tensor("ps", [P, 8 * 512], F32))

        def bank(i, n=1):
            return ps[:, i * 512:(i + n) * 512]

        r1 = sb("r1", 13 * TOK)
        r2 = sb("r2", H * TOK // 2)
        r3 = sb("r3", 7168)
        r4 = sb("r4", FC * KEYS)
        r5 = sb("r5", 4096)
        r6 = sb("r6", 6912)
        x = sb("x", TILES * D)[:, :].rearrange("p (t d) -> p t d", t=TILES)
        ident = sb("ident", P)
        identb = sb("identb", P, BF16)
        wkvT = sb("wkvT", FC * 2 * D)[:, :].rearrange("p (c n) -> p c n", c=FC)
        bk = sb("bk", FC)
        rows = sb("rows", 5 * D)[:, :].rearrange("p (r d) -> p r d", r=5)
        BQ, BV, BP, SWQ, SWP = (rows[:, i, :] for i in range(5))
        wintT = sb("wintT", 2 * FC * D, BF16)[:, :].rearrange("p (m c n) -> p m c n", m=2, c=FC)
        router = sb("router", FC * E)[:, :].rearrange("p (c n) -> p c n", c=FC)
        kk = sb("kk", P)
        segi = sb("segi", TILES, I32)
        small = sb("small", 512)
        def qf(h):
            return r1[:, h * TOK:(h + 1) * TOK] if h < 13 else r6[:, 3584 + (h - 13) * TOK:3584 + (h - 12) * TOK]
        wuq = r2[:, 0:1536].rearrange("p (h n) -> p h n", h=H)
        wuk = r2[:, 1536:2560].rearrange("p (h n) -> p h n", h=H)
        wuv = r2[:, 2560:3584].rearrange("p (h n) -> p h n", h=H)
        wo = r2[:, 3584:7680].rearrange("p (h n) -> p h n", h=H)
        weff = r3[0:QC, 0:2048].rearrange("p (h n) -> p h n", h=H)
        wqrs = r3[0:QC, 2048:3072].rearrange("p (h n) -> p h n", h=H // 2)
        wuvo = r3[:, 3072:5120].rearrange("p (h n) -> p h n", h=H // 2)
        pT = r3[:, 5120:7168].rearrange("p (h n) -> p h n", h=H)
        ctx0 = r3[:, 5120:6144].rearrange("p (c n) -> p c n", c=FC)
        xnT = r5[:, 0:2048].rearrange("p (c t) -> p c t", c=FC)
        qcT = r5[0:QC, 2048:3072]
        tabs = r5[:, 3072:4096].rearrange("p (k t) -> p k t", k=4)
        sm = [r5[:, i * 2048:(i + 1) * 2048].rearrange("p (h n) -> p h n", h=H) for i in range(2)]
        kf0 = [r6[:, i * 512:(i + 1) * 512] for i in range(2)]
        kvtok = r6[:, 1024:1280].rearrange("p (b n) -> p b n", b=B)
        ropet = [r6[:, 1280 + i * 512:1792 + i * 512] for i in range(2)]
        olat = r6[:, 2304:3328].rearrange("p (h n) -> p h n", h=H // 2)
        maskb = [r6[:, 3328 + 64 * i:3392 + 64 * i].bitcast(BF16) for i in range(2)]
        wkvc = r4[:, 0:256].rearrange("p (c n) -> p c n", c=FC)
        wkr = r4[0:KVC, 256:384]
        wkrs = r4[0:KVC, 384:512]
        wdq = r4[:, 512:704].rearrange("p (c n) -> p c n", c=FC)
        wnat = r4[:, 1024:2048].rearrange("p (m c n) -> p m c n", m=2, c=FC)
        wmag = r4[:, 2048:3072].rearrange("p (m c n) -> p m c n", m=2, c=FC)
        wint = r4[:, 704:960].bitcast(BF16).rearrange("p (c n) -> p c n", c=FC)
        wint2 = sb("wint2", FC * D, BF16)[:, :].rearrange("p (c n) -> p c n", c=FC)
        xn = [sb(f"xn{i}", D) for i in range(2)]
        hT = [sb(f"hT{i}", D)[:, :].rearrange("p (c t) -> p c t", c=FC) for i in range(2)]
        gu = r6[:, 0:4096].rearrange("p (c n) -> p c n", c=FC)
        sgu = r6[:, 4096:4608].rearrange("p (c n) -> p c n", c=FC)
        down = r6[:, 4608:6912].rearrange("p (e n) -> p e n", e=HB)
        hid = [r5[:, i * 1152:(i + 1) * 1152].rearrange("p (e n) -> p e n", e=HB) for i in range(2)]
        hidT = r5[:, 2304:3456].rearrange("p (e n) -> p e n", e=HB)
        sg = [r5[:, 3456 + 256 * i:3712 + 256 * i].rearrange("p (e n) -> p e n", e=2) for i in range(2)]
        xq = [sb(f"xq{i}", D, BF16) for i in range(2)]
        xqT = sb("xqT", D, BF16)[:, :].rearrange("p (c t) -> p c t", c=FC)
        xmag = sb("xmag", D)
        qtok = sb("qtok", D)
        qTf = sb("qTf", D)
        qpart = [sb(f"qpart{i}", 3 * D, BF16)[:, :].rearrange("p (j n) -> p j n", j=3) for i in range(2)]
        kst = r1[:, 0:HALF * KEYS].bitcast(BF16).rearrange("p (r h k) -> p r h k", r=2, h=HALF)
        qst = r2[:, :].bitcast(BF16).rearrange("p (h t) -> p h t", h=H)
        vx = r3[:, 0:2 * KT * H * VW].rearrange("p (r k h n) -> p r k h n", r=2, k=KT, h=H)
        ctxT = r4[:, :].rearrange("p (c k) -> p c k", c=FC)
        kf = r5[:, 0:KEYS]
        kpart = [r5[:, 1602 + 802 * j:2404 + 802 * j].bitcast(BF16)[:, 0:KEYS] for j in range(3)]
        pr = [r6[:, i * 1024:(i + 1) * 1024] for i in range(3)]
        wup = r6[:, 3072:3584].rearrange("p (c n) -> p c n", c=FC)
        wdn = r6[:, 3584:4096].rearrange("p (c n) -> p c n", c=FC)
        wex = r6[:, 4096:4608].rearrange("p (c n) -> p c n", c=FC)
        wg = r6[:, 4608:4624].rearrange("p (c n) -> p c n", c=FC)
        poS = [r6[:, 4624 + 256 * i:4880 + 256 * i] for i in range(2)]
        otok = [r6[:, 5136 + 512 * i:5648 + 512 * i].rearrange("p (t d) -> p t d", t=2) for i in range(2)]
        ob = r6[:, 6160:6416]
        upT = r6[:, 6416:6672].rearrange("p (c t) -> p c t", c=FC)
        ystore = [r6[:, 6672:6912], None]
        y = [sb(f"y{i}", D) for i in range(2)]
        nst = [sb(f"nst{i}", 24, BF16)[:, :].rearrange("p (u j) -> p u j", u=8) for i in range(2)]

        cols = iter(range(0, 512))

        def col(n=1):
            a = next(cols)
            for _ in range(n - 1):
                next(cols)
            return small[:, a:a + n]

        segf, seglo = col(TILES), col(TILES)
        stats, mv, rstd = col(6), [col(2), col(2)], [col(1), col(1)]
        neghalf, eul = col(1), col(1)
        mx0, den0, rec0 = col(H), col(H), [col(H), col(H)]
        wam, wsc, wrs = col(4), col(4), col(4)
        lg, top8, idf, sig = col(E), col(E), col(E), [col(2), col(2)]
        sigd, sigr, ntop = col(2), col(2), col(2)
        pe0, pe1 = col(E), col(E)
        probs = [col(E), col(E)]
        top8i = sb("top8i", 8, U32)
        xam, xrs, xsc = col(1), col(1), [col(1), col(1), col(1)]
        mxc, mx1, nrem = [col(32), col(32)], col(8), col(8)
        recd = col(8)
        oam, ors, osc = col(1), col(1), [col(1), col(1)]
        lg1, top1, dtop, etop, rden, rsum = col(E), col(E), col(1), col(1), col(1), col(1)

        kscr = nc.dram_tensor("kscr", (2, 3, P, KEYS), BF16, kind="Internal").ap()
        qscr = nc.dram_tensor("qscr", (3, D, TOK), BF16, kind="Internal").ap()

        ld_const, ld_x, ld_key, ld_q, ld_vo, ld_w1, ld_ctx, ld_ffn, ld_ffn1, ld_ones = (
            sem(n) for n in ("ld_const", "ld_x", "ld_key", "ld_q", "ld_vo", "ld_w1", "ld_ctx", "ld_ffn", "ld_ffn1",
                             "ld_ones"))
        dve_chain, act_chain, pool_chain = sem("dve_chain"), sem("act_chain"), sem("pool_chain")
        (m_mm, m_ev, kv_mm, kv_ev, rope_mm, rope_done, kvt_mm, kvt_ev, eps_rdy, rstd_rdy, xn_rdy, xnT_mm, xnT_ev,
         qc_mm, qc_ev, qa_mm, qa_ev, qb_mm, qb_ev, q_rdy, mask_rdy, s_mm, s_sub, s_exp, s_rec, s_norm, pt_mm, pt_ev,
         pv_mm, pv_ev, ao_mm, x1_rdy) = (sem(n) for n in (
             "m_mm", "m_ev", "kv_mm", "kv_ev", "rope_mm", "rope_done", "kvt_mm", "kvt_ev", "eps_rdy", "rstd_rdy",
             "xn_rdy", "xnT_mm", "xnT_ev", "qc_mm", "qc_ev", "qa_mm", "qa_ev", "qb_mm", "qb_ev", "q_rdy", "mask_rdy",
             "s_mm", "s_sub", "s_exp", "s_rec", "s_norm", "pt_mm", "pt_ev", "pv_mm", "pv_ev", "ao_mm", "x1_rdy"))
        (hT_mm, hT_ev, rt_mm, lg_rdy, ntop_rdy, pow_rdy, p_rdy, gu_mm, silu_rdy, hid_rdy, ht_mm, ht_ev, dn_mm,
         x2_rdy) = (sem(n) for n in ("hT_mm", "hT_ev", "rt_mm", "lg_rdy", "ntop_rdy", "pow_rdy", "p_rdy", "gu_mm",
                                     "silu_rdy", "hid_rdy", "ht_mm", "ht_ev", "dn_mm", "x2_rdy"))
        (wint_rdy, wt_mm, wt_ev, sw_mm, sw_ev, xq_rdy, xqT_mm, xqT_ev, q1_mm, q1_rdy, q1T_mm, q1T_ev, qs_a, qs_b,
         qs_c, qpart_rdy) = (sem(n) for n in (
             "wint_rdy", "wt_mm", "wt_ev", "sw_mm", "sw_ev", "xq_rdy", "xqT_mm", "xqT_ev", "q1_mm", "q1_rdy",
             "q1T_mm", "q1T_ev", "qs_a", "qs_b", "qs_c", "qpart_rdy"))
        (k_mm, k_ev, ks_a, ks_b, ks_c, kpart_rdy, k_wr, v_mm, v_ev, vone_rdy, mx_mm, mx_rdy, nst_rdy, sh_mm,
         sh_rdy, sc_mm, ex_rdy, av_mm, po_rdy, po_zero, ot_mm, o_rdy, oi_rdy, oiT_mm, oiT_ev, wp_mm, x3_rdy, x3T_mm,
         x3T_ev, up_mm, up_rdy, dtop_rdy, etop_rdy, y_mm, y_ev, y_rdy) = (sem(n) for n in (
             "k_mm", "k_ev", "ks_a", "ks_b", "ks_c", "kpart_rdy", "k_wr", "v_mm", "v_ev", "vone_rdy",
             "mx_mm", "mx_rdy", "nst_rdy", "sh_mm", "sh_rdy", "sc_mm", "ex_rdy", "av_mm", "po_rdy", "po_zero",
             "ot_mm", "o_rdy", "oi_rdy", "oiT_mm", "oiT_ev", "wp_mm", "x3_rdy", "x3T_mm", "x3T_ev", "up_mm",
             "up_rdy", "dtop_rdy", "etop_rdy", "y_mm", "y_ev", "y_rdy"))
        q_wr = [sem(f"q_wr{i}") for i in range(2)]
        k_stk = [sem(f"k_stk{i}") for i in range(2)]
        stored = [sem(f"stored{i}") for i in range(2)]
        q_stk = [sem(f"q_stk{b}") for b in range(B)]

        block = ctx.enter_context(nc.Block())

        @block.sync
        def _(sp):
            def load(s, *pairs):
                for dst, src in pairs:
                    sp.dma_start(dst, src).then_inc(s, 16)

            load(ld_key, (ctx0, ctx0_in), (wkvc, wkvc_in), (wkr, wkr_in), (wkrs, wkrs_in))
            load(ld_x, (x, x_in.rearrange("(t p) d -> p t d", p=P)), (segi[:, :], seg_in))
            load(ld_const, (ident[:, :], ident_in), (tabs, tabs_in), (kk[:, :], kk_in))
            load(ld_q, (wuq, wuq_in), (wuk, wuk_in), (weff[:, 0::2, 0:R], wqr_in[:, 0::2, :]),
                 (weff[:, 1::2, KVC:P], wqr_in[:, 1::2, :]), (wqrs, wqrs_in), (wdq, wdq_in))
            load(ld_w1, (wnat[:, 0], wq_in), (wnat[:, 1], wp_in), (rows[:, 0:3, :], rows_in), (wkvT, wkv_in),
                 (bk[:, :], bk_in), (router, router_in))
            load(ld_vo, (wuv, wuv_in), (wo, wo_in))
            sp.wait_ge(wt_mm, 2)
            sp.wait_ge(qc_mm, 2)
            sp.wait_ge(rope_mm, 2)
            sp.wait_ge(kvt_mm, 1)
            load(ld_ctx, (ctxT, ctx_in[0]))
            sp.wait_ge(x1_rdy, TILES)
            load(ld_ones, (kst[SROWS:SROWS + 3], ones_in))
            load(ld_ffn, (gu, gu_in), (sgu, sgu_in), (down[:, 0:E, :], down_in), (down[:, E, :], sdown_in))

            def stack_keys(s):
                sp.wait_ge(kpart_rdy, s + 1)
                if s >= 2:
                    sp.wait_ge(k_stk[s % 2], 96 * (s // 2))
                for j in range(3):
                    sp.dma_start(kscr[s % 2, j], kpart[j]).then_inc(k_wr, 16)
                sp.wait_ge(k_wr, 48 * (s + 1))
                if s >= 2:
                    sp.wait_ge(sc_mm, 2 * KT * (s - 1))
                for g, j in enumerate(STACK_K):
                    sp.dma_start(kst[g * DH:(g + 1) * DH, s % 2], kscr[s % 2, j].rearrange("(h d) k -> d h k", d=DH))\
                        .then_inc(k_stk[s % 2], 16)

            stack_keys(0)
            stack_keys(1)
            sp.wait_ge(k_mm, 2 * len(CH))
            sp.wait_ge(v_mm, (KT + 1) // 2)
            load(ld_ctx, (ctxT, ctx_in[1]))
            for t in range(TILES):
                sp.wait_ge(qpart_rdy, t + 1)
                for j in range(3):
                    sp.dma_start(qscr[j].rearrange("(c p) t -> p c t", p=P)[:, :, t * P:(t + 1) * P],
                                 qpart[t % 2][:, j, :].rearrange("p (c t) -> p c t", c=FC)).then_inc(q_wr[t % 2], 16)
                if t % 2 == 1:
                    b = t // 2
                    for w in q_wr:
                        sp.wait_ge(w, 48 * (b + 1))
                    if b == 0:
                        sp.wait_ge(m_mm, 6)
                    for g, j in enumerate(STACK_Q):
                        sp.dma_start(qst[g * DH:(g + 1) * DH, :, b * LQ:(b + 1) * LQ],
                                     qscr[j].rearrange("(h d) t -> d h t", d=DH)[:, :, b * LQ:(b + 1) * LQ])\
                            .then_inc(q_stk[b], 16)
            sp.wait_ge(dn_mm, TILES)
            load(ld_ffn1, (wup, wup_in), (wdn, wdn_in), (wex, wex_in), (wg, wg_in))

            def store(b):
                for t in (2 * b, 2 * b + 1):
                    sp.wait_ge(y_rdy, t + 1)
                    sp.dma_start(out[t * P:(t + 1) * P, :], y[t % 2][:, :]).then_inc(stored[t % 2], 16)

            for s in range(2, STAGES):
                stack_keys(s)
                if s % 2 == 1 and s // 2 + 1 < B:
                    sp.wait_ge(k_mm, len(CH) * (s + 1))
                    sp.wait_ge(v_mm, (KT + 1) // 2 * (s // 2 + 1))
                    load(ld_ctx, (ctxT, ctx_in[s // 2 + 1]))
                if s % 2 == 1:
                    store(s // 2 - 1)
            store(B - 1)
            for w in stored:
                sp.wait_ge(w, 16 * TILES // 2)

        @block.gpsimd
        def _(pool):
            def rsqrt(n):
                pool.wait_ge(eps_rdy, n + 1)
                nc.gpsimd.tensor_tensor(rstd[n % 2], mv[n % 2][:, 1:2], neghalf, ALU.pow).then_inc(rstd_rdy, 1)

            for t in range(TILES):
                rsqrt(t)
            for hf in range(2):
                for pair in range(H // 2):
                    n = hf * (H // 2) + pair
                    pool.wait_ge(qb_ev, n + 1)
                    pool.wait_ge(qa_ev, 2 * n + 2)
                    for par in range(2):
                        at = slice(par * R, par * R + R)
                        q = qf(2 * pair + par)[at, hf * 512:(hf + 1) * 512]
                        nc.gpsimd.tensor_tensor(q, q, ropet[n % 2][at, :], ALU.add).then_inc(q_rdy, 1)
                        pool.wait_ge(q_rdy, 2 * n + par + 1)
            for t in range(TILES):
                pool.wait_ge(s_rec, t + 1)
                nc.gpsimd.tensor_tensor(sm[t % 2], sm[t % 2], rec0[t % 2].unsqueeze(2).to_broadcast([P, H, K0]),
                                        ALU.mult).then_inc(s_norm, 1)

            def split_keys(s):
                pool.wait_ge(ks_a, s + 1)
                nc.gpsimd.tensor_tensor(kf, kf, kpart[0], ALU.subtract).then_inc(ks_b, 1)
                pool.wait_ge(ks_c, s + 1)
                pool.wait_ge(ks_b, s + 1)
                nc.gpsimd.tensor_tensor(kpart[2], kf, kpart[1], ALU.subtract).then_inc(kpart_rdy, 1)

            split_keys(0)
            split_keys(1)
            n = TILES

            def split_queries(t):
                pool.wait_ge(qs_a, t + 1)
                nc.gpsimd.tensor_tensor(qTf[:, :], qTf[:, :], qpart[t % 2][:, 0, :], ALU.subtract).then_inc(qs_b, 1)
                pool.wait_ge(qs_c, t + 1)
                pool.wait_ge(qs_b, t + 1)
                nc.gpsimd.tensor_tensor(qpart[t % 2][:, 2, :], qTf[:, :], qpart[t % 2][:, 1, :], ALU.subtract)\
                    .then_inc(qpart_rdy, 1)

            rsqrt(n)
            n += 1
            for t in range(TILES + 2):
                if t < TILES:
                    pool.wait_ge(ntop_rdy, t + 1)
                    nc.gpsimd.tensor_tensor(sig[t % 2], eul.to_broadcast([P, 2]), ntop, ALU.pow).then_inc(pow_rdy, 1)
                if t + 1 < TILES:
                    rsqrt(n)
                    n += 1
                if 1 <= t <= TILES:
                    rsqrt(n)
                    n += 1
                if t >= 2:
                    split_queries(t - 2)
            for s in range(2, STAGES):
                split_keys(s)
                if s % 2 == 1:
                    for _ in range(2):
                        rsqrt(n)
                        n += 1
            for _ in range(2):
                rsqrt(n)
                n += 1

        @block.tensor
        def _(pe):
            mm = nc.tensor.matmul

            pe.wait_ge(ld_key, 64)
            for c in range(FC):
                last = mm(bank(6), wkvc[:, c, :], ctx0[:, c, :], start=c == 0, stop=c == FC - 1)
            last.then_inc(kv_mm, 1)
            for b in range(B):
                for c in range(FC):
                    last = mm(bank(5)[:, b * KVC:(b + 1) * KVC], ctx0[:, c, b * K0:(b + 1) * K0], wkvc[:, c, 0:KVC],
                              start=c == 0, stop=c == FC - 1)
            last.then_inc(kvt_mm, 1)
            pe.wait_ge(kv_ev, 1)
            mm(bank(7), wkr, kf0[1][0:KVC, :], start=True, stop=True).then_inc(rope_mm, 1)
            pe.wait_ge(kv_ev, 2)
            mm(bank(6), wkrs, kf0[1][0:KVC, :], start=True, stop=True).then_inc(rope_mm, 1)
            pe.wait_ge(ld_q, 96)
            for h in range(H):
                last = mm(bank(h // 8)[0:QC, (h % 8) * KVC:(h % 8 + 1) * KVC], wuq[:, h, :], wuk[:, h, :],
                          start=True, stop=True)
                if h % 8 == 7:
                    last.then_inc(m_mm, 1)
            pe.wait_ge(ld_const, 48)
            for t in range(TILES):
                pe.wait_ge(xn_rdy, t + 1)
                if t >= 2:
                    pe.wait_ge(xnT_ev, t - 1)
                for c in range(FC):
                    last = nc.tensor.transpose(bank(2 + t % 2)[:, c * P:(c + 1) * P], xn[t % 2][:, c * P:(c + 1) * P],
                                               ident[:, :])
                last.then_inc(xnT_mm, 1)
            for hf in range(2):
                pe.wait_ge(xnT_ev, 4 * hf + 4)
                for c in range(FC):
                    last = mm(bank(4 - hf)[0:QC, :], wdq[:, c, :], xnT[:, c, hf * 512:(hf + 1) * 512], start=c == 0,
                              stop=c == FC - 1)
                last.then_inc(qc_mm, 1)
            for m in range(2):
                pe.wait_ge(wint_rdy, m + 1)
                if m == 0:
                    pe.wait_ge(rope_done, 1)
                tb = bank(6 + m).bitcast(BF16)
                for c in range(FC):
                    for o in range(FC):
                        last = nc.tensor.transpose(tb[:, (c * FC + o) * P:(c * FC + o + 1) * P],
                                                   (wint, wint2)[m][:, o, c * P:(c + 1) * P], identb[:, :])
                last.then_inc(wt_mm, 1)
            pe.wait_ge(kvt_ev, 1)
            for m in range(2):
                for o in range(FC):
                    last = mm(bank(5)[:, m * D + o * P:m * D + (o + 1) * P],
                              wsc[:, 2 * m + o:2 * m + o + 1].to_broadcast([P, P]), ident[:, :], start=True, stop=True)
            last.then_inc(sw_mm, 1)
            pe.wait_ge(ld_vo, 32)
            pe.wait_ge(m_ev, 2)
            pe.wait_ge(xnT_ev, TILES)
            pe.wait_ge(qc_ev, 2)
            for h in range(H):
                p2 = h // 2
                last = mm(bank(p2 // 2)[(h % 2) * KVC:(h % 2 + 1) * KVC, (p2 % 2) * D:(p2 % 2 + 1) * D],
                          wuv[:, h, :], wo[:, h, :], start=True, stop=True)
                if h % 4 == 3:
                    last.then_inc(m_mm, 1)

            for hf in range(2):
                at = slice(hf * 512, (hf + 1) * 512)
                for h in range(H):
                    n = hf * H + h
                    if n >= 4:
                        pe.wait_ge(qa_ev, n - 3)
                    else:
                        pe.wait_ge(m_ev, 3 + n)
                    mm(bank(n % 4), weff[:, h, :], qcT[:, at], start=True, stop=True).then_inc(qa_mm, 1)
                    if h % 2 == 1:
                        k = hf * (H // 2) + h // 2
                        if k >= 2:
                            pe.wait_ge(qb_ev, k - 1)
                        elif k == 0:
                            pe.wait_ge(sw_ev, 1)
                        mm(bank(4 + k % 2), wqrs[:, h // 2, :], qcT[:, at], start=True,
                           stop=True).then_inc(qb_mm, 1)

            def attend0(t):
                b = t // 2
                at = slice(t * P, (t + 1) * P)
                pe.wait_ge(mask_rdy, t + 1)
                if t % 4 == 0:
                    pe.wait_ge(q_rdy, H * (t // 4 + 1))
                    pe.wait_ge(qa_ev, H * (t // 4 + 1))
                if t == 0:
                    pe.wait_ge(qa_ev, 2 * H)
                if t > 0:
                    pe.wait_ge(s_sub, t)
                for g in range(4):
                    mm(bank(g), identb[:, :], maskb[t % 2].unsqueeze(1).to_broadcast([P, 4, K0]), start=True,
                       stop=False, skip_group_check=True)
                    for k in range(4):
                        h = 4 * g + k
                        last = mm(bank(g)[:, k * K0:(k + 1) * K0], qf(h)[:, at], kf0[h % 2][:, b * K0:(b + 1) * K0],
                                  start=False, stop=True, skip_group_check=True)
                last.then_inc(s_mm, 1)

            def values0(t):
                b = t // 2
                pe.wait_ge(s_norm, t + 1)
                if t == 0:
                    pe.wait_ge(qb_ev, H)
                    pe.wait_ge(kvt_ev, 1)
                for g in range(4):
                    n = 4 * t + g
                    if n >= 2:
                        pe.wait_ge(pt_ev, n - 1)
                    for k in range(4):
                        last = nc.tensor.transpose(bank(4 + n % 2)[:, k * P:(k + 1) * P], sm[t % 2][:, 4 * g + k, :],
                                                   ident[:, :])
                    last.then_inc(pt_mm, 1)
                for j in range(2):
                    n = 2 * t + j
                    pe.wait_ge(pt_ev, 4 * t + 2 * j + 2)
                    if n >= 1:
                        pe.wait_ge(pv_ev, n)
                    elif n == 0:
                        pe.wait_ge(wt_ev, 2)
                    for par in range(2):
                        last = mm(bank(6)[par * KVC:(par + 1) * KVC, :], kvtok[:, b, :],
                                  pT[:, 8 * j + par:8 * j + 8:2, :], start=True, stop=True)
                    last.then_inc(pv_mm, 1)
                if t >= 1:
                    pe.wait_ge(x1_rdy, t)
                for p2 in range(H // 2):
                    if p2 % 4 == 0:
                        pe.wait_ge(pv_ev, 2 * t + p2 // 4 + 1)
                    last = mm(bank(7)[:, 0:D], olat[:, p2, :], wuvo[:, p2, :], start=p2 == 0, stop=p2 == H // 2 - 1)
                last.then_inc(ao_mm, 1)

            for t in range(TILES + 1):
                if t < TILES:
                    attend0(t)
                if t >= 1:
                    values0(t - 1)

            def keys(s, c, bnk):
                a, n = CH[c]
                for k in range(FC):
                    last = mm(bank(bnk)[:, 0:n], wkvT[:, k, (s % 2) * P:(s % 2 + 1) * P], ctxT[:, k, a:a + n],
                              start=k == 0, stop=k == FC - 1)
                last.then_inc(k_mm, 1)

            def values(b, j, bnk):
                for i in range(2 * j, min(2 * j + 2, KT)):
                    n = P if i < KT - 1 else KLAST
                    for k in range(FC):
                        last = mm(bank(bnk)[0:n, (i % 2) * D:(i % 2 + 1) * D], ctxT[:, k, i * P:i * P + n],
                                  wkvT[:, k, D:2 * D], start=k == 0, stop=k == FC - 1)
                last.then_inc(v_mm, 1)

            NV = (KT + 1) // 2
            pe.wait_ge(ld_ctx, 16)
            pe.wait_ge(x1_rdy, TILES)
            done = []
            for s in range(2):
                for c in range(len(CH)):
                    if len(done) >= 2:
                        pe.wait_ge(*done[-2])
                    keys(s, c, 6 + len(done) % 2)
                    done.append((k_ev, len(CH) * s + c + 1))
            for j in range(NV):
                pe.wait_ge(*done[-2])
                values(0, j, 6 + len(done) % 2)
                done.append((v_ev, j + 1))

            def turn_h(t):
                pe.wait_ge(xn_rdy, TILES + 1 + t + max(0, t - 2))
                if t == 0:
                    pe.wait_ge(v_ev, NV)
                for c in range(FC):
                    last = nc.tensor.transpose(bank(7)[:, c * P:(c + 1) * P], xn[0][:, c * P:(c + 1) * P], ident[:, :])
                last.then_inc(hT_mm, 1)

            def gate_up(t, c):
                n = 5 * t + c
                if c == 0:
                    pe.wait_ge(hT_ev, t + 1)
                if n >= 4:
                    pe.wait_ge(hid_rdy, n - 3)
                w = gu[:, :, c * 512:(c + 1) * 512] if c < 4 else sgu
                for k in range(FC):
                    last = mm(bank(n % 4)[:, 0:w.shape[2]], hT[t % 2][:, k, :], w[:, k, :], start=k == 0,
                              stop=k == FC - 1)
                last.then_inc(gu_mm, 1)

            def route(t):
                for k in range(FC):
                    last = mm(bank(7)[:, 0:E], hT[t % 2][:, k, :], router[:, k, :], start=k == 0, stop=k == FC - 1)
                last.then_inc(rt_mm, 1)

            def combine(t):
                pe.wait_ge(hid_rdy, 5 * t + 5)
                for g in range(3):
                    n = 3 * t + g
                    if n >= 2:
                        pe.wait_ge(ht_ev, n - 1)
                    for e in range(4 * g, min(4 * g + 4, HB)):
                        last = nc.tensor.transpose(bank(4 + n % 2)[:, (e % 4) * P:(e % 4 + 1) * P], hid[t % 2][:, e, :],
                                                   ident[:, :])
                    last.then_inc(ht_mm, 1)
                if t >= 1:
                    pe.wait_ge(x2_rdy, t)
                for e in range(HB):
                    if e % 4 == 0:
                        pe.wait_ge(ht_ev, 3 * t + e // 4 + 1)
                    last = mm(bank(6)[:, 0:D], hidT[:, e, :], down[:, e, :], start=e == 0, stop=e == HB - 1)
                last.then_inc(dn_mm, 1)

            def turn_xq(t):
                pe.wait_ge(xq_rdy, t + 1)
                pe.wait_ge(lg_rdy, min(t + 3, TILES))
                if t >= 1:
                    pe.wait_ge(q1T_ev, t)
                for c in range(FC):
                    last = nc.tensor.transpose(bank(7).bitcast(BF16)[:, c * P:(c + 1) * P],
                                               xq[t % 2][:, c * P:(c + 1) * P], identb[:, :])
                last.then_inc(xqT_mm, 1)

            def project_q(t):
                pe.wait_ge(xqT_ev, t + 1)
                for k in range(FC):
                    last = mm(bank(7)[:, 0:D], xqT[:, k, :], wintT[:, 0, k, :], start=k == 0, stop=k == FC - 1)
                last.then_inc(q1_mm, 1)

            def turn_q(t):
                pe.wait_ge(q1_rdy, t + 1)
                for c in range(FC):
                    last = nc.tensor.transpose(bank(7)[:, c * P:(c + 1) * P], qtok[:, c * P:(c + 1) * P], ident[:, :])
                last.then_inc(q1T_mm, 1)

            pe.wait_ge(ld_ffn, 64)
            for t in range(TILES + 2):
                if t < TILES:
                    if t >= 3:
                        pe.wait_ge(q1T_ev, t - 2)
                    turn_h(t)
                    gate_up(t, 0)
                    route(t)
                    gate_up(t, 1)
                if 1 <= t <= TILES:
                    combine(t - 1)
                if t >= 2:
                    turn_xq(t - 2)
                if t < TILES:
                    gate_up(t, 2)
                if t >= 2:
                    project_q(t - 2)
                if t < TILES:
                    gate_up(t, 3)
                if t >= 2:
                    turn_q(t - 2)
                if t < TILES:
                    gate_up(t, 4)

            taken = [(q1T_ev, TILES)]

            def bank7(reader, value):
                pe.wait_ge(*taken[0])
                taken[0] = (reader, value)

            def max_scores(quad, n):
                b, s, u, c = quad // 4, quad // 2, n // len(CH), n % len(CH)
                h = 4 * (quad % 4) + u // 2
                ca = 8 * len(CH) * quad + n
                if n == 0:
                    pe.wait_ge(k_stk[s % 2], 96 * (s // 2 + 1))
                    pe.wait_ge(q_stk[b], 96)
                if ca >= 2:
                    pe.wait_ge(mx_rdy, ca - 1)
                a, m = CH[c]
                q0 = b * LQ + (u % 2) * P
                mm(bank(ca % 2)[:, 0:m], qst[0:SROWS, h, q0:q0 + P], kst[0:SROWS, s % 2, h % HALF, a:a + m],
                   start=True, stop=True).then_inc(mx_mm, 1)

            def shift(quad):
                bank7(sh_rdy, quad + 1)
                pe.wait_ge(nst_rdy, quad + 1)
                tb = bank(7).bitcast(BF16)
                for u in range(8):
                    last = nc.tensor.transpose(tb[SROWS:SROWS + 3, u * P:(u + 1) * P], nst[quad % 2][:, u, :],
                                               identb[:, :])
                last.then_inc(sh_mm, 1)

            def scores(quad, kt, first):
                i, b, s = KT * quad + kt, quad // 4, quad // 2
                n = P if kt < KT - 1 else KLAST
                if first == 0:
                    if kt == 0:
                        pe.wait_ge(sh_rdy, quad + 1)
                    if i == 0:
                        pe.wait_ge(ld_ones, 16)
                    if i >= 2:
                        pe.wait_ge(ex_rdy, i - 1)
                for k in (first, first + 1):
                    h = 4 * (quad % 4) + k
                    last = mm(bank(2 + 2 * (i % 2), 2)[0:n, k * LQ:(k + 1) * LQ],
                              kst[0:SROWS + 3, s % 2, h % HALF, kt * P:kt * P + n],
                              qst[0:SROWS + 3, h, b * LQ:(b + 1) * LQ], start=True, stop=True)
                if first == 2:
                    last.then_inc(sc_mm, 1)

            def weigh(i):
                quad, kt = i // KT, i % KT
                b = quad // 4
                n = P if kt < KT - 1 else KLAST
                pe.wait_ge(ex_rdy, i + 1)
                if kt == 0:
                    pe.wait_ge(v_ev, NV * (b + 1))
                    if quad >= 1:
                        pe.wait_ge(po_rdy, quad)
                if i == 0:
                    pe.wait_ge(vone_rdy, 1)
                    pe.wait_ge(po_zero, 1)
                for k in range(4):
                    h = 4 * (quad % 4) + k
                    last = mm(bank(6)[32 * k:32 * k + VW, 0:LQ], vx[0:n, b % 2, kt, h, :],
                              pr[i % 3][0:n, k * LQ:(k + 1) * LQ], start=kt == 0, stop=kt == KT - 1,
                              skip_group_check=True)
                last.then_inc(av_mm, 1)

            def turn_out(quad):
                bank7(o_rdy, quad + 1)
                pe.wait_ge(po_rdy, quad + 1)
                for q in range(2):
                    last = nc.tensor.transpose(bank(7)[:, q * P:(q + 1) * P], poS[quad % 2][:, q * P:(q + 1) * P],
                                               ident[:, :])
                last.then_inc(ot_mm, 1)

            def tail(t, part):
                if part == 0:
                    bank7(oiT_ev, t + 1)
                    pe.wait_ge(oi_rdy, t + 1)
                    for c in range(FC):
                        last = nc.tensor.transpose(bank(7).bitcast(BF16)[:, c * P:(c + 1) * P],
                                                   xq[t % 2][:, c * P:(c + 1) * P], identb[:, :])
                    last.then_inc(oiT_mm, 1)
                if part == 1:
                    bank7(x3_rdy, t + 1)
                    pe.wait_ge(oiT_ev, t + 1)
                    for k in range(FC):
                        last = mm(bank(7)[:, 0:D], xqT[:, k, :], wintT[:, 1, k, :], start=k == 0, stop=k == FC - 1)
                    last.then_inc(wp_mm, 1)
                if part == 2:
                    bank7(x3T_ev, t + 1)
                    pe.wait_ge(x3_rdy, t + 1)
                    pe.wait_ge(xn_rdy, 3 * TILES + t + 1)
                    for c in range(FC):
                        last = nc.tensor.transpose(bank(7)[:, c * P:(c + 1) * P],
                                                   xn[t % 2][:, c * P:(c + 1) * P], ident[:, :])
                    last.then_inc(x3T_mm, 1)
                if part == 3:
                    bank7(up_rdy, t + 1)
                    pe.wait_ge(x3T_ev, t + 1)
                    if t == 0:
                        pe.wait_ge(ld_ffn1, 64)
                    for f in range(FC):
                        for k in range(FC):
                            mm(bank(7)[:, f * P:(f + 1) * P], wup[:, k, f * P:(f + 1) * P], hT[0][:, k, :],
                               start=k == 0, stop=k == FC - 1)
                    for k in range(FC):
                        last = mm(bank(7)[:, D:D + E], hT[0][:, k, :], wg[:, k, :], start=k == 0, stop=k == FC - 1)
                    last.then_inc(up_mm, 1)
                if part == 4:
                    bank7(y_ev, t + 1)
                    pe.wait_ge(up_rdy, t + 1)
                    for k in range(FC):
                        mm(bank(7)[:, 0:D], upT[:, k, :], wdn[:, k, :], start=k == 0, stop=k == FC - 1)
                    for k in range(FC):
                        last = mm(bank(7)[:, D:2 * D], hT[0][:, k, :], wex[:, k, :], start=k == 0, stop=k == FC - 1)
                    last.then_inc(y_mm, 1)

            def beside(jobs):
                for what, *a in jobs:
                    if what == "max":
                        max_scores(*a)
                    elif what == "shift":
                        shift(*a)
                    elif what == "k":
                        s, c = a
                        bank7(k_ev, len(CH) * s + c + 1)
                        if c == 0:
                            pe.wait_ge(ld_ctx, 16 * (s // 2 + 1))
                        keys(s, c, 7)
                    elif what == "v":
                        b, j = a
                        bank7(v_ev, NV * b + j + 1)
                        values(b, j, 7)
                    elif what == "out":
                        turn_out(*a)
                    elif what == "tail":
                        tail(*a)

            for n in range(8 * len(CH)):
                max_scores(0, n)
            shift(0)
            for quad in range(QUADS):
                for kt in range(KT):
                    jobs = BESIDE.get((quad, kt), [])
                    maxima = [j for j in jobs if j[0] == "max"]
                    beside(maxima[0:1])
                    scores(quad, kt, 0)
                    beside(maxima[1:2])
                    scores(quad, kt, 2)
                    beside(maxima[2:3])
                    if quad or kt:
                        weigh(KT * quad + kt - 1)
                    beside(maxima[3:] + [j for j in jobs if j[0] != "max"])
            weigh(STEPS - 1)
            for kt in range(KT):
                beside(BESIDE.get((QUADS, kt), []))

        @block.scalar
        def _(act):
            fn = nc.scalar.activation

            act.wait_ge(kv_mm, 1)
            fn(kf0[1][0:KVC, :], bank(6)[0:KVC, :], ACT.Copy).then_inc(kv_ev, 1)
            fn(kf0[0][KVC:P, :], bank(6)[KVC:P, :], ACT.Copy).then_inc(kv_ev, 1)
            act.wait_ge(kvt_mm, 1)
            fn(kvtok, bank(5)[:, 0:B * KVC].rearrange("p (b n) -> p b n", b=B), ACT.Copy).then_inc(kvt_ev, 1)
            act.wait_ge(ld_q, 96)
            for g in range(2):
                act.wait_ge(m_mm, g + 1)
                src = bank(g)[0:QC, :].rearrange("p (h n) -> p h n", h=8)
                fn(weff[:, 8 * g:8 * g + 8:2, R:P], src[:, 0::2, :], ACT.Copy)
                fn(weff[:, 8 * g + 1:8 * g + 8:2, 0:KVC], src[:, 1::2, :], ACT.Copy).then_inc(m_ev, 1)
            for t in range(TILES):
                act.wait_ge(xnT_mm, t + 1)
                fn(xnT[:, :, t * P:(t + 1) * P], bank(2 + t % 2)[:, 0:D].rearrange("p (c t) -> p c t", c=FC),
                   ACT.Copy).then_inc(xnT_ev, 1)
            for hf in range(2):
                act.wait_ge(qc_mm, hf + 1)
                fn(qcT[:, hf * 512:(hf + 1) * 512], bank(4 - hf)[0:QC, :], ACT.Copy).then_inc(qc_ev, 1)
            for m in range(2):
                act.wait_ge(wt_mm, m + 1)
                fn(wintT[:, m], bank(6 + m).bitcast(BF16)[:, 0:2 * D].rearrange("p (c n) -> p c n", c=FC),
                   ACT.Copy).then_inc(wt_ev, 1)
            act.wait_ge(sw_mm, 1)
            act.wait_ge(ld_w1, 96)
            fn(rows[:, 3:5, :], bank(5).rearrange("p (r d) -> p r d", r=2), ACT.Copy).then_inc(sw_ev, 1)
            for g in range(4):
                act.wait_ge(m_mm, 3 + g)
                fn(wuvo[:, 2 * g:2 * g + 2, :], bank(g).rearrange("p (h n) -> p h n", h=2), ACT.Copy)\
                    .then_inc(m_ev, 1)
            act.wait_ge(m_ev, 6)

            for t in range(TILES + 1):
                if t < TILES:
                    act.wait_ge(s_sub, t + 1)
                    fn(sm[t % 2], sm[t % 2], ACT.Exp, scale=SCALE0).then_inc(s_exp, 1)
                if t >= 1:
                    for g in range(4):
                        act.wait_ge(pt_mm, 4 * (t - 1) + g + 1)
                        if t >= 2 and g == 0:
                            act.wait_ge(pv_mm, 2 * (t - 1))
                        elif t == 1 and g == 0:
                            act.wait_ge(kv_mm, 1)
                        fn(pT[:, 4 * g:4 * g + 4, :], bank(4 + g % 2).rearrange("p (h n) -> p h n", h=4), ACT.Copy)\
                            .then_inc(pt_ev, 1)

            def keys_bias(s, c, bnk):
                a, n = CH[c]
                act.wait_ge(k_mm, len(CH) * s + c + 1)
                if c == 0 and s == 0:
                    act.wait_ge(pt_mm, 4 * TILES)
                elif c == 0:
                    act.wait_ge(kpart_rdy, s)
                fn(kf[:, a:a + n], bank(bnk)[:, 0:n], ACT.Identity, bias=bk[:, s % 2:s % 2 + 1]).then_inc(k_ev, 1)

            NV = (KT + 1) // 2

            def values_copy(b, j, bnk):
                act.wait_ge(v_mm, NV * b + j + 1)
                if b >= 2 and j == 0:
                    act.wait_ge(av_mm, 4 * KT * (b - 1))
                n = P if j < NV - 1 else KLAST
                tiles = 2 if 2 * j + 2 <= KT else 1
                fn(vx[0:n, b % 2, 2 * j:2 * j + tiles, :, 0:DH],
                   bank(bnk)[0:n, 0:tiles * D].rearrange("p (k h n) -> p k h n", k=tiles, h=H), ACT.Copy)\
                    .then_inc(v_ev, 1)

            n = 0
            for s in range(2):
                for c in range(len(CH)):
                    keys_bias(s, c, 6 + n % 2)
                    n += 1
            act.wait_ge(x1_rdy, TILES)
            for j in range(NV):
                values_copy(0, j, 6 + n % 2)
                n += 1

            def silu(t, c):
                n = 5 * t + c
                act.wait_ge(gu_mm, n + 1)
                if c == 0:
                    act.wait_ge(p_rdy, t + 1)
                if n >= 2:
                    act.wait_ge(hid_rdy, n - 1)
                src = bank(n % 4)
                if c < 4:
                    for e in range(2):
                        fn(sg[n % 2][:, e, :], src[:, e * 2 * I:e * 2 * I + I], ACT.Silu,
                           scale=probs[t % 2][:, 2 * c + e:2 * c + e + 1]).then_inc(silu_rdy, 1)
                else:
                    fn(sg[n % 2][:, 0, :], src[:, 0:I], ACT.Silu).then_inc(silu_rdy, 1)

            act.wait_ge(k_wr, 96)
            for t in range(TILES + 2):
                if t < TILES:
                    act.wait_ge(hT_mm, t + 1)
                    if t >= 2:
                        act.wait_ge(gu_mm, 5 * (t - 1))
                    fn(hT[t % 2], bank(7)[:, 0:D].rearrange("p (c t) -> p c t", c=FC), ACT.Copy).then_inc(hT_ev, 1)
                    silu(t, 0)
                    silu(t, 1)
                if 1 <= t <= TILES:
                    for g in range(3):
                        n = 3 * (t - 1) + g
                        act.wait_ge(ht_mm, n + 1)
                        if g == 0 and t >= 2:
                            act.wait_ge(dn_mm, t - 1)
                        e = min(4, HB - 4 * g)
                        fn(hidT[:, 4 * g:4 * g + e, :], bank(4 + n % 2)[:, 0:e * P].rearrange("p (e n) -> p e n", e=e),
                           ACT.Copy).then_inc(ht_ev, 1)
                if t >= 2:
                    act.wait_ge(xqT_mm, t - 1)
                    if t >= 3:
                        act.wait_ge(q1_mm, t - 2)
                    fn(xqT, bank(7).bitcast(BF16)[:, 0:D].rearrange("p (c t) -> p c t", c=FC), ACT.Copy)\
                        .then_inc(xqT_ev, 1)
                if t < TILES:
                    silu(t, 2)
                    silu(t, 3)
                if t >= 2:
                    act.wait_ge(q1T_mm, t - 1)
                    if t >= 3:
                        act.wait_ge(qpart_rdy, t - 2)
                    fn(qTf[:, :], bank(7)[:, 0:D], ACT.Copy).then_inc(q1T_ev, 1)
                if t < TILES:
                    silu(t, 4)

            def beside(quad, kt):
                for what, *a in BESIDE.get((quad, kt), []):
                    if what == "shift":
                        shift_rows(*a)
                    elif what == "k":
                        keys_bias(*a, 7)
                    elif what == "v":
                        values_copy(*a, 7)
                    elif what == "tail":
                        t, part = a
                        if part == 0:
                            act.wait_ge(oiT_mm, t + 1)
                            if t >= 1:
                                act.wait_ge(wp_mm, t)
                            else:
                                act.wait_ge(q1_mm, TILES)
                            fn(xqT, bank(7).bitcast(BF16)[:, 0:D].rearrange("p (c t) -> p c t", c=FC), ACT.Copy)\
                                .then_inc(oiT_ev, 1)
                        if part == 2:
                            act.wait_ge(x3T_mm, t + 1)
                            if t >= 1:
                                act.wait_ge(y_mm, t)
                            fn(hT[0], bank(7)[:, 0:D].rearrange("p (c t) -> p c t", c=FC), ACT.Copy)\
                                .then_inc(x3T_ev, 1)
                        if part == 3:
                            act.wait_ge(dtop_rdy, t + 1)
                            fn(etop, dtop, ACT.Exp).then_inc(etop_rdy, 1)

            def shift_rows(quad):
                act.wait_ge(sh_mm, quad + 1)
                h, b = 4 * (quad % 4), quad // 4
                if quad == 0:
                    act.wait_ge(m_mm, 6)
                fn(qst[SROWS:SROWS + 3, h:h + 4, b * LQ:(b + 1) * LQ],
                   bank(7).bitcast(BF16)[SROWS:SROWS + 3, :].rearrange("p (h t) -> p h t", h=4), ACT.Copy)\
                    .then_inc(sh_rdy, 1)

            def out_copy(quad):
                act.wait_ge(av_mm, KT * (quad + 1))
                if quad >= 2:
                    act.wait_ge(ot_mm, quad - 1)
                fn(poS[quad % 2], bank(6)[:, 0:LQ], ACT.Copy).then_inc(po_rdy, 1)

            shift_rows(0)
            act.wait_ge(dn_mm, TILES)
            for quad in range(QUADS + 1):
                for kt in range(KT):
                    if quad < QUADS:
                        i = KT * quad + kt
                        n = P if kt < KT - 1 else KLAST
                        act.wait_ge(sc_mm, i + 1)
                        if i >= 3:
                            act.wait_ge(av_mm, i - 2)
                        fn(pr[i % 3][0:n, :], bank(2 + 2 * (i % 2), 2)[0:n, :], ACT.Exp, scale=SCALE1)\
                            .then_inc(ex_rdy, 1)
                    if kt == 0 and quad >= 1:
                        out_copy(quad - 1)
                    beside(quad, kt)

        @block.vector
        def _(dve):
            v = nc.vector
            chain = [0]

            def link(ins):
                chain[0] += 1
                ins.then_inc(dve_chain, 1)
                dve.wait_ge(dve_chain, chain[0])

            norms = [0]

            def layer_norm(t, into):
                n = norms[0]
                norms[0] += 1
                link(v.bn_stats(stats, x[:, t, :]))
                link(v.bn_aggr(mv[n % 2], stats))
                v.tensor_scalar(mv[n % 2][:, 1:2], mv[n % 2][:, 1:2], LN_EPS, None, ALU.add).then_inc(eps_rdy, 1)
                dve.wait_ge(rstd_rdy, n + 1)
                v.tensor_scalar(into, x[:, t, :], mv[n % 2][:, 0:1], rstd[n % 2], ALU.subtract, ALU.mult)\
                    .then_inc(xn_rdy, 1)
                dve.wait_ge(xn_rdy, n + 1)

            def quantise(src, amax, rscale, scale, mag, into, done):
                link(v.tensor_reduce(amax, src, AX_X, ALU.max, apply_absolute_value=True))
                link(v.tensor_scalar(scale, amax, float(np.float32(1) / np.float32(127)), 1e-8, ALU.mult, ALU.max))
                link(v.reciprocal(rscale, scale))
                link(v.tensor_scalar(mag, src, rscale, 127.0, ALU.mult, ALU.min))
                link(v.tensor_scalar(mag, mag, -127.0, MAGIC, ALU.max, ALU.add))
                v.tensor_scalar(into, mag, -MAGIC, None, ALU.add).then_inc(done, 1)

            link(v.memset(neghalf, -0.5))
            link(v.memset(eul, float(np.exp(np.float64(1.0)))))
            dve.wait_ge(ld_const, 48)
            link(v.tensor_copy(identb[:, :], ident[:, :]))
            cosr, sinr = (tabs[:, i, 0:K0].unsqueeze(1).to_broadcast([P, B, K0]) for i in (2, 3))
            as_b = "p (b k) -> p b k"
            dve.wait_ge(rope_mm, 1)
            link(v.tensor_tensor(ropet[0].rearrange(as_b, b=B), bank(7).rearrange(as_b, b=B), cosr, ALU.mult))
            dve.wait_ge(rope_mm, 2)
            link(v.tensor_tensor(ropet[1].rearrange(as_b, b=B), bank(6).rearrange(as_b, b=B), sinr, ALU.mult))
            link(v.tensor_tensor(kf0[1][KVC:P, :], ropet[0][KVC:P, :], ropet[1][KVC:P, :], ALU.add))
            v.tensor_tensor(kf0[0][0:R, :], ropet[0][0:R, :], ropet[1][0:R, :], ALU.add).then_inc(rope_done, 1)
            dve.wait_ge(rope_done, 1)
            dve.wait_ge(ld_x, 32)
            link(v.tensor_copy(segf, segi[:, :]))
            link(v.tensor_scalar(seglo, segf, float(-LOOKBACK), None, ALU.add))
            for t in range(TILES):
                if t >= 2:
                    dve.wait_ge(xnT_mm, t - 1)
                layer_norm(t, xn[t % 2][:, :])
            dve.wait_ge(ld_w1, 96)
            for m in range(2):
                for o in range(FC):
                    n = 2 * m + o
                    quantise(wnat[:, m, o, :], wam[:, n:n + 1], wrs[:, n:n + 1], wsc[:, n:n + 1], wmag[:, m, o, :],
                             (wint, wint2)[m][:, o, :], wint_rdy if o == FC - 1 else dve_chain)
                    if o < FC - 1:
                        chain[0] += 1
            for hf in range(2):
                for h in range(H):
                    n = hf * H + h
                    q = qf(h)[:, hf * 512:(hf + 1) * 512].rearrange(as_b, b=2)
                    cosq = tabs[:, h % 2, :].unsqueeze(1).to_broadcast([P, 2, LQ])
                    dve.wait_ge(qa_mm, n + 1)
                    v.tensor_tensor(q, bank(n % 4).rearrange(as_b, b=2), cosq, ALU.mult).then_inc(qa_ev, 1)
                    if h % 2 == 1:
                        k = hf * (H // 2) + h // 2
                        dve.wait_ge(qb_mm, k + 1)
                        if k >= 2:
                            dve.wait_ge(q_rdy, 2 * k - 2)
                        sinq = tabs[:, 3, :].unsqueeze(1).to_broadcast([P, 2, LQ])
                        v.tensor_tensor(ropet[k % 2].rearrange(as_b, b=2),
                                        bank(4 + k % 2).rearrange(as_b, b=2), sinq, ALU.mult).then_inc(qb_ev, 1)

            def mask(t):
                if t >= 2:
                    dve.wait_ge(s_mm, t - 1)
                link(v.tensor_scalar(xmag[:, 0:K0], kk[:, :], segf[:, t:t + 1], MASK, ALU.is_le, ALU.mult))
                link(v.tensor_scalar(xmag[:, K0:2 * K0], kk[:, :], seglo[:, t:t + 1], MASK, ALU.is_ge, ALU.mult))
                v.scalar_tensor_tensor(out=maskb[t % 2], in0=xmag[:, 0:K0], scalar=-2 * MASK, in1=xmag[:, K0:2 * K0],
                                       op0=ALU.add, op1=ALU.add).then_inc(mask_rdy, 1)
                dve.wait_ge(mask_rdy, t + 1)

            mask(0)
            for t in range(TILES + 1):
                if t < TILES:
                    if t + 1 < TILES:
                        mask(t + 1)
                    dve.wait_ge(s_mm, t + 1)
                    s4 = bank(0, 4).rearrange("p (h n) -> p h n", h=H)
                    link(v.tensor_reduce(mx0, s4, AX_X, ALU.max))
                    if t >= 2:
                        dve.wait_ge(pt_mm, 4 * (t - 1))
                    elif t == 0:
                        dve.wait_ge(qb_mm, H)
                        dve.wait_ge(qb_ev, H)
                    v.tensor_tensor(sm[t % 2], s4, mx0.unsqueeze(2).to_broadcast([P, H, K0]), ALU.subtract)\
                        .then_inc(s_sub, 1)
                if t >= 1:
                    for j in range(2):
                        dve.wait_ge(pv_mm, 2 * (t - 1) + j + 1)
                        if t >= 2 and j == 0:
                            dve.wait_ge(ao_mm, t - 1)
                        v.tensor_copy(olat[:, 4 * j:4 * j + 4, :], bank(6).rearrange("p (h n) -> p h n", h=4))\
                            .then_inc(pv_ev, 1)
                if t < TILES:
                    dve.wait_ge(s_exp, t + 1)
                    link(v.tensor_reduce(den0, sm[t % 2], AX_X, ALU.add))
                    v.reciprocal(rec0[t % 2], den0).then_inc(s_rec, 1)
                if t >= 1:
                    dve.wait_ge(ao_mm, t)
                    v.tensor_tensor(x[:, t - 1, :], x[:, t - 1, :], bank(7)[:, 0:D], ALU.add).then_inc(x1_rdy, 1)
            dve.wait_ge(x1_rdy, TILES)
            v.memset(vx[:, :, :, :, DH:VW].rearrange("p r k h n -> p (r k) (h n)"), 1.0).then_inc(vone_rdy, 1)

            def split_keys(s):
                dve.wait_ge(k_ev, len(CH) * (s + 1))
                if s >= 1:
                    dve.wait_ge(k_wr, 48 * s)
                v.tensor_copy(kpart[0], kf).then_inc(ks_a, 1)
                dve.wait_ge(ks_b, s + 1)
                v.tensor_copy(kpart[1], kf).then_inc(ks_c, 1)

            split_keys(0)
            split_keys(1)

            def route(t):
                dve.wait_ge(rt_mm, t + 1)
                v.tensor_copy(lg, bank(7)[:, 0:E]).then_inc(lg_rdy, 1)
                dve.wait_ge(lg_rdy, t + 1)
                link(v.max(top8, lg))
                link(v.max_index(top8i[:, :], top8, lg))
                link(v.tensor_copy(idf, top8i[:, :]))
                v.tensor_scalar(ntop, top8[:, 0:2], -1.0, 80.0, ALU.mult, ALU.min).then_inc(ntop_rdy, 1)
                dve.wait_ge(pow_rdy, t + 1)
                link(v.tensor_scalar(sigd, sig[t % 2], 1.0, None, ALU.add))
                link(v.reciprocal(sigr, sigd))
                link(v.tensor_scalar(pe0, kk[:, 0:E], idf[:, 0:1], sigr[:, 0:1], ALU.is_equal, ALU.mult))
                link(v.tensor_scalar(pe1, kk[:, 0:E], idf[:, 1:2], sigr[:, 1:2], ALU.is_equal, ALU.mult))
                v.tensor_tensor(probs[t % 2], pe0, pe1, ALU.add).then_inc(p_rdy, 1)
                dve.wait_ge(p_rdy, t + 1)

            def hidden(t, c):
                n = 5 * t + c
                dve.wait_ge(silu_rdy, 9 * t + min(2 * c + 2, HB))
                if c == 0 and t >= 2:
                    dve.wait_ge(ht_mm, 3 * (t - 1))
                src = bank(n % 4)
                if c < 4:
                    for e in range(2):
                        k = 2 * c + e
                        last = v.scalar_tensor_tensor(out=hid[t % 2][:, k, :], in0=src[:, (2 * e + 1) * I:(2 * e + 2) * I],
                                                      scalar=probs[t % 2][:, k:k + 1], in1=sg[n % 2][:, e, :],
                                                      op0=ALU.mult, op1=ALU.mult)
                else:
                    last = v.tensor_tensor(hid[t % 2][:, E, :], src[:, I:2 * I], sg[n % 2][:, 0, :], ALU.mult)
                last.then_inc(hid_rdy, 1)

            dve.wait_ge(k_wr, 96)
            layer_norm(0, xn[0][:, :])
            for t in range(TILES + 2):
                if t < TILES:
                    route(t)
                    if t + 1 < TILES:
                        dve.wait_ge(hT_mm, t + 1)
                        layer_norm(t + 1, xn[0][:, :])
                    hidden(t, 0)
                    hidden(t, 1)
                if 1 <= t <= TILES:
                    dve.wait_ge(dn_mm, t)
                    v.tensor_tensor(x[:, t - 1, :], x[:, t - 1, :], bank(6)[:, 0:D], ALU.add).then_inc(x2_rdy, 1)
                    dve.wait_ge(x2_rdy, t)
                if t >= 2:
                    dve.wait_ge(q1_mm, t - 1)
                    if t >= 3:
                        dve.wait_ge(q1T_mm, t - 2)
                    link(v.scalar_tensor_tensor(out=qtok[:, :], in0=bank(7)[:, 0:D], scalar=xsc[(t - 2) % 3],
                                                in1=SWQ, op0=ALU.mult, op1=ALU.mult))
                    v.tensor_tensor(qtok[:, :], qtok[:, :], BQ, ALU.add).then_inc(q1_rdy, 1)
                if 1 <= t <= TILES:
                    layer_norm(t - 1, xn[1][:, :])
                    if t >= 3:
                        dve.wait_ge(xqT_mm, t - 2)
                    quantise(xn[1][:, :], xam, xrs, xsc[(t - 1) % 3], xmag[:, :], xq[(t - 1) % 2][:, :], xq_rdy)
                if t < TILES:
                    hidden(t, 2)
                    hidden(t, 3)
                if t >= 2:
                    dve.wait_ge(q1T_ev, t - 1)
                    if t >= 4:
                        dve.wait_ge(q_wr[t % 2], 48 * (t // 2 - 1))
                    v.tensor_copy(qpart[t % 2][:, 0, :], qTf[:, :]).then_inc(qs_a, 1)
                    dve.wait_ge(qs_b, t - 1)
                    v.tensor_copy(qpart[t % 2][:, 1, :], qTf[:, :]).then_inc(qs_c, 1)
                if t < TILES:
                    hidden(t, 4)

            def max_chunk(quad, n):
                m = CH[n % len(CH)][1]
                ca = 8 * len(CH) * quad + n
                dve.wait_ge(mx_mm, ca + 1)
                v.tensor_reduce(mxc[quad % 2][:, n:n + 1], bank(ca % 2)[:, 0:m], AX_X, ALU.max).then_inc(mx_rdy, 1)
                if n == 8 * len(CH) - 1:
                    dve.wait_ge(mx_rdy, ca + 1)
                    link(v.tensor_reduce(mx1, mxc[quad % 2].rearrange("p (u c) -> p u c", u=8), AX_X, ALU.max))
                    if quad >= 2:
                        dve.wait_ge(sh_mm, quad - 1)
                    s3 = nst[quad % 2]
                    link(v.tensor_scalar(s3[:, :, 0], mx1, -1.0, None, ALU.mult))
                    link(v.scalar_tensor_tensor(out=nrem, in0=mx1, scalar=-1.0, in1=s3[:, :, 0], op0=ALU.mult,
                                                op1=ALU.subtract))
                    link(v.tensor_copy(s3[:, :, 1], nrem))
                    v.tensor_tensor(s3[:, :, 2], nrem, s3[:, :, 1], ALU.subtract).then_inc(nst_rdy, 1)

            def out_norm(quad):
                dve.wait_ge(ot_mm, quad + 1)
                o4 = bank(7)[:, 0:2 * P].rearrange("p (t h n) -> p t h n", t=2, h=4)
                r8 = recd.rearrange("p (t h) -> p t h", t=2)
                link(v.reciprocal(r8, o4[:, :, :, DH]))
                g = quad % 4
                dst = otok[quad // 4 % 2][:, :, g * 64:(g + 1) * 64]
                v.tensor_tensor(dst.rearrange("p t (h n) -> p t h n", h=4), o4[:, :, :, 0:DH],
                                r8.unsqueeze(3).to_broadcast([P, 2, 4, DH]), ALU.mult).then_inc(o_rdy, 1)

            def out_quant(t):
                dve.wait_ge(o_rdy, 4 * (t // 2 + 1))
                link(v.tensor_tensor(ob, otok[t // 2 % 2][:, t % 2, :], BV, ALU.add))
                if t >= 2:
                    dve.wait_ge(oiT_mm, t - 1)
                quantise(ob, oam, ors, osc[t % 2], xmag[:, :], xq[t % 2][:, :], oi_rdy)

            def tail(t, part):
                if part == 0 and t % 2 == 0:
                    out_quant(t)
                    out_quant(t + 1)
                if part == 1:
                    dve.wait_ge(wp_mm, t + 1)
                    dve.wait_ge(oi_rdy, 2 * (t // 2) + 2)
                    link(v.scalar_tensor_tensor(out=xmag[:, :], in0=bank(7)[:, 0:D], scalar=osc[t % 2], in1=SWP,
                                                op0=ALU.mult, op1=ALU.mult))
                    link(v.tensor_tensor(xmag[:, :], xmag[:, :], BP, ALU.add))
                    v.tensor_tensor(x[:, t, :], x[:, t, :], xmag[:, :], ALU.add).then_inc(x3_rdy, 1)
                    dve.wait_ge(x3_rdy, t + 1)
                    if t >= 2:
                        dve.wait_ge(x3T_mm, t - 1)
                    layer_norm(t, xn[t % 2][:, :])
                if part == 3:
                    dve.wait_ge(up_mm, t + 1)
                    if t >= 1:
                        dve.wait_ge(y_mm, t)
                    link(v.tensor_scalar(upT, bank(7)[:, 0:D].rearrange("p (c t) -> p c t", c=FC), 0.0, None, ALU.max))
                    v.tensor_copy(lg1, bank(7)[:, D:D + E]).then_inc(up_rdy, 1)
                    dve.wait_ge(up_rdy, t + 1)
                    link(v.max(top1, lg1))
                    v.tensor_tensor(dtop, top1[:, 1:2], top1[:, 0:1], ALU.subtract).then_inc(dtop_rdy, 1)
                    dve.wait_ge(etop_rdy, t + 1)
                    link(v.tensor_scalar(rden, etop, 1.0, None, ALU.add))
                    link(v.reciprocal(rden, rden))
                    link(v.scalar_tensor_tensor(out=rsum, in0=etop, scalar=rden, in1=rden, op0=ALU.mult, op1=ALU.add))
                if part == 4:
                    dve.wait_ge(y_mm, t + 1)
                    if t >= 2:
                        dve.wait_ge(stored[t % 2], 16 * (t // 2))
                    link(v.tensor_tensor(xmag[:, :], x[:, t, :], bank(7)[:, 0:D], ALU.add))
                    v.scalar_tensor_tensor(out=y[t % 2][:, :], in0=bank(7)[:, D:2 * D], scalar=rsum, in1=xmag[:, :],
                                           op0=ALU.mult, op1=ALU.add).then_inc(y_ev, 1)
                    dve.wait_ge(y_ev, t + 1)
                    v.tensor_copy(recd[:, 0:1], rsum).then_inc(y_rdy, 1)

            dve.wait_ge(x2_rdy, TILES)
            v.memset(bank(6), 0.0).then_inc(po_zero, 1)
            for n in range(8 * len(CH)):
                max_chunk(0, n)
            for quad in range(QUADS + 1):
                for kt in range(KT):
                    for what, *a in BESIDE.get((quad, kt), []):
                        if what == "max":
                            max_chunk(*a)
                        elif what == "k" and a[1] == len(CH) - 1:
                            split_keys(a[0])
                        elif what == "out":
                            out_norm(*a)
                        elif what == "tail":
                            tail(*a)


def kernel(**inputs):
    import concourse.bacc as _bacc
    from concourse.bass_utils import run_bass_kernel_spmd as _run

    def chunks(w):
        return w.reshape(w.shape[0] // P, P, -1).transpose(1, 0, 2)

    a = {k: np.asarray(v) for k, v in inputs.items()}
    ctx = a["ctx_2048"]
    ctxT = ctx.transpose(0, 2, 1).reshape(B, FC, P, KEYS).transpose(0, 2, 1, 3)
    ctx0 = ctx[:, :K0].transpose(2, 0, 1).reshape(FC, P, B * K0).transpose(1, 0, 2)
    half = R // 2
    swap = np.r_[half:R, 0:half]
    wkr = a["L0_xattn_W_kr"]
    wqr = a["L0_xattn_W_qr"].reshape(QC, H, R)
    inv = (1.0 / 10000.0 ** (np.arange(half, dtype=np.float32) / np.float32(half))).astype(np.float32)
    ang = (np.arange(LQ, dtype=np.float32)[:, None] * inv).T
    cos, sin = np.cos(ang).astype(np.float32), np.sin(ang).astype(np.float32)
    cos2, sin2, one = np.concatenate([cos, cos]), np.concatenate([-sin, sin]), np.ones((KVC, LQ), np.float32)
    tabs = np.stack([np.concatenate(z) for z in ((cos2, one), (one, cos2), (cos2, cos2), (sin2, sin2))], 1)
    gu = a["L0_ffn_gate_up_w"].transpose(1, 0, 2).reshape(D, E * 2 * I)
    rows = np.stack([a["L1_xattn_bq"], a["L1_xattn_bkv"][D:], a["L1_xattn_bp"]])
    vals = {
        "x": a["x"].reshape(TOK, D), "ctx": ctxT, "ctx0": ctx0,
        "seg": a["itok_BxS_0_1023"].reshape(TILES, P).T,
        "ident": np.eye(P, dtype=np.float32), "tabs": tabs,
        "kk": np.broadcast_to(np.arange(P, dtype=np.float32), (P, P)),
        "ones": np.ones((3, 2, HALF, KEYS), mybir.dt.np(BF16)),
        "wkvc": chunks(np.concatenate([a["L0_xattn_W_kvc"]] * 2, 1)),
        "wkr": np.concatenate([wkr, wkr], 1), "wkrs": np.concatenate([wkr[:, swap]] * 2, 1),
        "wdq": chunks(a["L0_xattn_W_dq"]),
        "wuq": a["L0_xattn_W_uq"].reshape(QC, H, HD).transpose(2, 1, 0),
        "wuk": a["L0_xattn_W_uk"].reshape(KVC, H, HD).transpose(2, 1, 0),
        "wqr": wqr, "wqrs": wqr[:, :, swap].reshape(QC, H // 2, 2 * R),
        "wuv": a["L0_xattn_W_uv"].reshape(KVC, H, HD).transpose(2, 1, 0),
        "wo": a["L0_xattn_W_o"].reshape(H, HD, D).transpose(1, 0, 2),
        "router": chunks(a["L0_ffn_router_w"]), "gu": chunks(gu),
        "sgu": chunks(np.concatenate([a["L0_ffn_shared_gate_w"], a["L0_ffn_shared_up_w"]], 1)),
        "down": a["L0_ffn_down_w"].transpose(1, 0, 2), "sdown": a["L0_ffn_shared_down_w"],
        "wq": chunks(a["L1_xattn_wq"]), "wp": chunks(a["L1_xattn_wp"]), "wkv": chunks(a["L1_xattn_wkv"].T),
        "bk": a["L1_xattn_bkv"][:D].reshape(FC, P).T,
        "rows": np.broadcast_to(rows, (P, 3, D)),
        "wup": chunks(a["L1_ffn_W_up"].T), "wdn": chunks(a["L1_ffn_W_down"].T), "wex": chunks(a["L1_ffn_W_expert"]),
        "wg": chunks(a["L1_ffn_W_gate"].T),
    }
    nc = _bacc.Bacc("TRN2", target_bir_lowering=False, num_devices=1)
    arrays, args = {}, []
    for name, val in vals.items():
        val = np.ascontiguousarray(val)
        arrays[f"in_{name}_dram"] = val
        args.append(nc.dram_tensor(f"in_{name}_dram", val.shape, mybir.dt.from_np(val.dtype),
                                   kind="ExternalInput").ap())
    args.append(nc.dram_tensor("out_0_dram", (TOK, D), F32, kind="ExternalOutput").ap())
    program(nc, *args)
    r = _run(nc, [arrays], core_ids=[0])
    return r.results[0]["out_0_dram"].reshape(B, LQ, D)
```

```python
from contextlib import ExitStack

import numpy as np

import concourse.bass as bass
from concourse import mybir

F32 = mybir.dt.float32
BF16 = mybir.dt.bfloat16
I32 = mybir.dt.int32
U32 = mybir.dt.uint32
ACT = mybir.ActivationFunctionType
ALU = mybir.AluOpType
AX_X = mybir.AxisListType.X

P = 128
B, LQ, D = 4, 256, 256
KEYS = 1601
TOK = B * LQ
TILES = TOK // P
FC = D // P
H = 16
HD, KVC, QC, R = 128, 64, 96, 64
LOOKBACK = 8
K0 = 128
NEG = -1e30
MASK = float(2.0 ** 99)
SCALE0 = float(1.0 / np.sqrt(HD + R).astype(np.float32))
E, I = 8, 128
HB = E + 1
DH = D // H
SCALE1 = float(1.0 / np.sqrt(DH))
KT = (KEYS + P - 1) // P
KLAST = KEYS - (KT - 1) * P
HALF = H // 2
STAGES = B * 2
QUADS = STAGES * 2
STEPS = QUADS * KT
STACK_Q = (0, 0, 1, 0, 2, 1)
STACK_K = (0, 1, 0, 2, 0, 1)
SROWS = len(STACK_Q) * DH
VW = DH + 1
CH = [(0, 401), (401, 400), (801, 400), (1201, 400)]
MAGIC = float(1.5 * 2 ** 23)
LN_EPS = 1e-5


TAIL = ((3, "bias"), (4, "scale"), (5, "round"), (6, "turn_o"), (7, "project"), (8, "residual"), (9, "moments"),
        (10, "variance"), (11, "norm"), (12, "turn_x"), (13, "up"), (14, "gate"), (15, "route"), (16, "down"),
        (17, "expert"))


ALONE = ("bias", "scale", "round", "residual", "moments", "variance", "norm")


def schedule():
    beside = {}

    def put(step, *job):
        beside.setdefault((step // KT, step % KT), []).append(job)

    for quad in range(1, QUADS):
        put((quad - 1) * KT + 11, "shift", quad)
    for quad in range(QUADS):
        put((quad + 1) * KT + 2, "out", quad)
    for b in range(B):
        start = b * 4 * KT
        if b + 1 < B:
            for s, at in ((2 * b + 2, KSTEPS[0]), (2 * b + 3, KSTEPS[1])):
                for c in range(len(CH)):
                    put(start + at[c], "k", s, c)
            for j, at in enumerate(VSTEPS):
                put(start + at, "v", b + 1, j)
        for at, part in TAIL:
            put(start + 4 * KT + at, "tail", b, part)
    for quad in range(1, QUADS):
        first = (quad - 1) * KT - 2
        window = range(max(0, first), first + KT)
        work = [step_work(beside.get((i // KT, i % KT), [])) for i in window]
        done = 0.0
        put_to = 0
        for i, w in zip(window, work):
            done += w
            until = round(NMAX * done / sum(work))
            for n in range(put_to, until):
                put(i, "max", quad, n)
            put_to = until
    return beside


def step_work(jobs):
    cost = {"k": 8 * 401, "v": 16 * D, "out": 2 * 4 * P, "shift": 8 * P, "up": 16 * D, "down": 16 * D,
            "expert": 16 * D, "turn_x": 4 * 4 * P, "turn_o": 4 * P, "project": 4 * D, "gate": 4 * 4 * E}
    return 4 * LQ + 4 * LQ + sum(cost.get(j[-1] if j[0] == "tail" else j[0], 0) for j in jobs)


NMAX = 8 * len(CH)
KSTEPS = ((18, 19, 20, 21), (42, 43, 44, 45))
VSTEPS = (23, 25, 27, 29, 31, 33, 35)
def first_chunks(t, third):
    slot = 3 * (t - TILES) + third
    return range(slot * NMAX // 6, (slot + 1) * NMAX // 6)


BESIDE = schedule()


def program(nc, x_in, ctx_in, ctx0_in, seg_in, ident_in, tabs_in, kk_in, ones_in, wkvc_in, wkr_in, wkrs_in,
            wdq_in, wuq_in, wuk_in, wqr_in, wqrs_in, wuv_in, wo_in, router_in, gu_in, sgu_in, down_in, sdown_in,
            wq_in, wp_in, wkv_in, bk_in, rows_in, wup_in, wdn_in, wex_in, wg_in, segrow_in, keyrope_in, keyid_in,
            out):
    with ExitStack() as ctx:
        def sb(name, cols, dt=F32):
            return ctx.enter_context(nc.sbuf_tensor(name, [P, cols], dt))

        def sem(name):
            return ctx.enter_context(nc.semaphore(name))

        ps = ctx.enter_context(nc.psum_tensor("ps", [P, 8 * 512], F32))

        def bank(i, n=1):
            return ps[:, i * 512:(i + n) * 512]

        r1 = sb("r1", 13 * TOK)
        r2 = sb("r2", H * TOK // 2)
        r3 = sb("r3", 7168)
        r4 = sb("r4", FC * KEYS)
        r5 = sb("r5", 4096)
        r6 = sb("r6", 6912)
        x = sb("x", TILES * D)[:, :].rearrange("p (t d) -> p t d", t=TILES)
        ident = sb("ident", P)
        identb = sb("identb", P, BF16)
        wkvT = sb("wkvT", FC * 2 * D)[:, :].rearrange("p (c n) -> p c n", c=FC)
        bk = sb("bk", FC)
        rows = sb("rows", 5 * D)[:, :].rearrange("p (r d) -> p r d", r=5)
        BQ, BV, BP, SWQ, SWP = (rows[:, i, :] for i in range(5))
        wintT = sb("wintT", 2 * FC * D, BF16)[:, :].rearrange("p (m c n) -> p m c n", m=2, c=FC)
        router = sb("router", FC * E)[:, :].rearrange("p (c n) -> p c n", c=FC)
        kk = sb("kk", P)
        segi = sb("segi", TILES, I32)
        small = sb("small", 512)
        def qf(h):
            return r1[:, h * TOK:(h + 1) * TOK] if h < 13 else r6[:, 3584 + (h - 13) * TOK:3584 + (h - 12) * TOK]
        wuq = r2[:, 0:1536].rearrange("p (h n) -> p h n", h=H)
        wuk = r2[:, 1536:2560].rearrange("p (h n) -> p h n", h=H)
        wuv = r2[:, 2560:3584].rearrange("p (h n) -> p h n", h=H)
        wo = r2[:, 3584:7680].rearrange("p (h n) -> p h n", h=H)
        weff = r3[0:QC, 0:2048].rearrange("p (h n) -> p h n", h=H)
        wqrs = r3[0:QC, 2048:3072].rearrange("p (h n) -> p h n", h=H // 2)
        wuvo = r3[:, 3072:5120].rearrange("p (h n) -> p h n", h=H // 2)
        pT = r3[:, 5120:7168].rearrange("p (h n) -> p h n", h=H)
        ctx0 = r3[:, 5120:6144].rearrange("p (c n) -> p c n", c=FC)
        xnT = r5[:, 0:2048].rearrange("p (c t) -> p c t", c=FC)
        qcT = r5[0:QC, 2048:3072]
        tabs = r5[:, 3072:4096].rearrange("p (k t) -> p k t", k=4)
        sm = [r5[:, i * 2048:(i + 1) * 2048].rearrange("p (h n) -> p h n", h=H) for i in range(2)]
        kf0 = [r6[:, i * 512:(i + 1) * 512] for i in range(2)]
        kvtok = r6[:, 1024:1280].rearrange("p (b n) -> p b n", b=B)
        ropet = [r6[:, 1280 + i * 512:1792 + i * 512] for i in range(2)]
        olat = r6[:, 2304:3328].rearrange("p (h n) -> p h n", h=H // 2)
        maskb = [r6[:, 3328 + 64 * i:3392 + 64 * i].bitcast(BF16) for i in range(2)]
        wkvc = r4[:, 0:256].rearrange("p (c n) -> p c n", c=FC)
        wkr = r4[0:KVC, 256:384]
        wkrs = r4[0:KVC, 384:512]
        wdq = r4[:, 512:704].rearrange("p (c n) -> p c n", c=FC)
        wnat = r4[:, 1024:2048].rearrange("p (m c n) -> p m c n", m=2, c=FC)
        wmag = r4[:, 2048:3072].rearrange("p (m c n) -> p m c n", m=2, c=FC)
        wint = r4[:, 704:960].bitcast(BF16).rearrange("p (c n) -> p c n", c=FC)
        wint2 = sb("wint2", FC * D, BF16)[:, :].rearrange("p (c n) -> p c n", c=FC)
        xn2 = sb("xn", 2 * D)[:, :].rearrange("p (t d) -> p t d", t=2)
        xn = [xn2[:, i, :] for i in range(2)]
        hT2 = sb("hT", 2 * D)[:, :].rearrange("p (t c n) -> p t c n", t=2, c=FC)
        hT = [hT2[:, i] for i in range(2)]
        gu = r6[:, 0:4096].rearrange("p (c n) -> p c n", c=FC)
        sgu = r6[:, 4096:4608].rearrange("p (c n) -> p c n", c=FC)
        down = r6[:, 4608:6912].rearrange("p (e n) -> p e n", e=HB)
        hid = [r5[:, i * 1152:(i + 1) * 1152].rearrange("p (e n) -> p e n", e=HB) for i in range(2)]
        hidT = r5[:, 2304:3456].rearrange("p (e n) -> p e n", e=HB)
        sg = [r5[:, 3456 + 256 * i:3712 + 256 * i].rearrange("p (e n) -> p e n", e=2) for i in range(2)]
        xq2 = sb("xq", 2 * D, BF16)[:, :].rearrange("p (t d) -> p t d", t=2)
        xq = [xq2[:, i, :] for i in range(2)]
        xqT2 = sb("xqT", 2 * D, BF16)[:, :].rearrange("p (t c n) -> p t c n", t=2, c=FC)
        xqT = xqT2[:, 0]
        mag2 = sb("mag", 2 * D)[:, :].rearrange("p (t d) -> p t d", t=2)
        xmag, qtok = mag2[:, 0, :], mag2[:, 1, :]
        qTf = sb("qTf", D)
        qpart = [sb(f"qpart{i}", 3 * D, BF16)[:, :].rearrange("p (j n) -> p j n", j=3) for i in range(2)]
        kst = r1[:, 0:HALF * KEYS].bitcast(BF16).rearrange("p (r h k) -> p r h k", r=2, h=HALF)
        qst = r2[:, :].bitcast(BF16).rearrange("p (h t) -> p h t", h=H)
        vx = r3[:, 0:2 * KT * H * VW].rearrange("p (r k h n) -> p r k h n", r=2, k=KT, h=H)
        ctxT = r4[:, :].rearrange("p (c k) -> p c k", c=FC)
        kf = r5[:, 0:KEYS]
        kpart = [r5[:, 1602 + 802 * j:2404 + 802 * j].bitcast(BF16)[:, 0:KEYS] for j in range(3)]
        pr = [r6[:, i * 1024:(i + 1) * 1024] for i in range(3)]
        wup = r6[:, 3072:3584].rearrange("p (c n) -> p c n", c=FC)
        wdn = r6[:, 3584:4096].rearrange("p (c n) -> p c n", c=FC)
        wex = r6[:, 4096:4608].rearrange("p (c n) -> p c n", c=FC)
        wg = r6[:, 4608:4624].rearrange("p (c n) -> p c n", c=FC)
        poS = [r6[:, 4624 + 256 * i:4880 + 256 * i] for i in range(2)]
        otok = [r6[:, 5136 + 512 * i:5648 + 512 * i].rearrange("p (t d) -> p t d", t=2) for i in range(2)]
        upT = r6[:, 6160:6672].rearrange("p (c t) -> p c t", c=FC)
        y = [sb(f"y{i}", D) for i in range(2)]
        nst = [sb(f"nst{i}", 24, BF16)[:, :].rearrange("p (u j) -> p u j", u=8) for i in range(2)]

        cols = iter(range(0, 512))

        def col(n=1):
            a = next(cols)
            for _ in range(n - 1):
                next(cols)
            return small[:, a:a + n]

        segf, seglo = col(TILES), col(TILES)
        stats, mv, rstd = col(6), [col(2), col(2)], [col(1), col(1)]
        neghalf, eul = col(1), col(1)
        mx0, den0, rec0 = col(H), col(H), [col(H), col(H)]
        wam, wsc, wrs = col(4), col(4), col(4)
        lg, top8, idf, sig = col(E), col(E), col(E), [col(2), col(2)]
        sigd, sigr, ntop = col(2), col(2), col(2)
        pe0, pe1 = col(E), col(E)
        probs = [col(E), col(E)]
        top8i = sb("top8i", 8, U32)
        xam, xrs, xsc = col(1), col(1), [col(1), col(1), col(1)]
        mxc, mx1, nrem = [col(32), col(32)], col(8), col(8)
        recd = col(8)
        oam, ors, osc = col(2), col(2), [col(2), col(2)]
        lg1, top1 = (col(2 * E).rearrange("p (t e) -> p t e", t=2) for _ in range(2))
        dtop, etop, rden, rsum = col(2), col(2), col(2), col(2)
        stats3 = col(12).rearrange("p (t n) -> p t n", t=2)
        mv3 = col(4).rearrange("p (t n) -> p t n", t=2)
        rstd3 = col(2)

        kscr = nc.dram_tensor("kscr", (2, 3, P, KEYS), BF16, kind="Internal").ap()
        qscr = nc.dram_tensor("qscr", (3, D, TOK), BF16, kind="Internal").ap()

        ld_const, ld_x, ld_key, ld_q, ld_vo, ld_w1, ld_ctx, ld_ffn, ld_ffn1, ld_ones = (
            sem(n) for n in ("ld_const", "ld_x", "ld_key", "ld_q", "ld_vo", "ld_w1", "ld_ctx", "ld_ffn", "ld_ffn1",
                             "ld_ones"))
        dve_chain, act_chain, pool_chain = sem("dve_chain"), sem("act_chain"), sem("pool_chain")
        (m_mm, m_ev, kv_mm, kv_ev, rope_mm, rope_done, kvt_mm, kvt_ev, eps_rdy, rstd_rdy, xn_rdy, xnT_mm, xnT_ev,
         qc_mm, qc_ev, qa_mm, qa_ev, qb_mm, qb_ev, q_rdy, mask_rdy, s_mm, s_sub, s_exp, s_rec, s_norm, pt_mm, pt_ev,
         pv_mm, pv_ev, ao_mm, x1_rdy) = (sem(n) for n in (
             "m_mm", "m_ev", "kv_mm", "kv_ev", "rope_mm", "rope_done", "kvt_mm", "kvt_ev", "eps_rdy", "rstd_rdy",
             "xn_rdy", "xnT_mm", "xnT_ev", "qc_mm", "qc_ev", "qa_mm", "qa_ev", "qb_mm", "qb_ev", "q_rdy", "mask_rdy",
             "s_mm", "s_sub", "s_exp", "s_rec", "s_norm", "pt_mm", "pt_ev", "pv_mm", "pv_ev", "ao_mm", "x1_rdy"))
        (hT_mm, hT_ev, rt_mm, lg_rdy, ntop_rdy, pow_rdy, p_rdy, gu_mm, silu_rdy, hid_rdy, ht_mm, ht_ev, dn_mm,
         x2_rdy) = (sem(n) for n in ("hT_mm", "hT_ev", "rt_mm", "lg_rdy", "ntop_rdy", "pow_rdy", "p_rdy", "gu_mm",
                                     "silu_rdy", "hid_rdy", "ht_mm", "ht_ev", "dn_mm", "x2_rdy"))
        (wint_rdy, wt_mm, wt_ev, sw_mm, sw_ev, xq_rdy, xqT_mm, xqT_ev, q1_mm, q1_rdy, q1T_mm, q1T_ev, qs_a, qs_b,
         qs_c, qpart_rdy) = (sem(n) for n in (
             "wint_rdy", "wt_mm", "wt_ev", "sw_mm", "sw_ev", "xq_rdy", "xqT_mm", "xqT_ev", "q1_mm", "q1_rdy",
             "q1T_mm", "q1T_ev", "qs_a", "qs_b", "qs_c", "qpart_rdy"))
        (k_mm, k_ev, ks_a, ks_b, ks_c, kpart_rdy, k_wr, v_mm, v_ev, vone_rdy, mx_mm, mx_rdy, nst_rdy, sh_mm,
         sh_rdy, sc_mm, ex_rdy, av_mm, po_rdy, po_zero, ot_mm, o_rdy, oi_rdy, oiT_mm, oiT_ev, wp_mm, x3_rdy, x3T_mm,
         x3T_ev, up_mm, up_rdy, dtop_rdy, etop_rdy, y_mm, y_ev, y_rdy) = (sem(n) for n in (
             "k_mm", "k_ev", "ks_a", "ks_b", "ks_c", "kpart_rdy", "k_wr", "v_mm", "v_ev", "vone_rdy",
             "mx_mm", "mx_rdy", "nst_rdy", "sh_mm", "sh_rdy", "sc_mm", "ex_rdy", "av_mm", "po_rdy", "po_zero",
             "ot_mm", "o_rdy", "oi_rdy", "oiT_mm", "oiT_ev", "wp_mm", "x3_rdy", "x3T_mm", "x3T_ev", "up_mm",
             "up_rdy", "dtop_rdy", "etop_rdy", "y_mm", "y_ev", "y_rdy"))
        n3_eps, n3_rstd, n3_rdy, lg1_rdy, wp_ev, d_mm, d_rdy = (sem(n) for n in (
            "n3_eps", "n3_rstd", "n3_rdy", "lg1_rdy", "wp_ev", "d_mm", "d_rdy"))
        q_wr = [sem(f"q_wr{i}") for i in range(2)]
        k_stk = [sem(f"k_stk{i}") for i in range(2)]
        stored = [sem(f"stored{i}") for i in range(2)]
        q_stk = [sem(f"q_stk{b}") for b in range(B)]

        (ld_seg, far_rdy, g_load, g_ctx, g_kv_mm, g_kv_ev, g_rope_mm, g_rope_ev, g_tok_mm, g_tok_ev, g_s_mm, g_max,
         g_exp, g_norm, g_t_mm, g_t_ev, g_pv_mm, g_pv_ev, g_o_mm, g_x, g_q_ev, g_chain) = (sem(n) for n in (
             "ld_seg", "far_rdy", "g_load", "g_ctx", "g_kv_mm", "g_kv_ev", "g_rope_mm", "g_rope_ev", "g_tok_mm",
             "g_tok_ev", "g_s_mm", "g_max", "g_exp", "g_norm", "g_t_mm", "g_t_ev", "g_pv_mm", "g_pv_ev", "g_o_mm",
             "g_x", "g_q_ev", "g_chain"))
        g_kf = [r2[:, i * KEYS:(i + 1) * KEYS] for i in range(2)]
        g_cos, g_sin = (r2[:, i * KEYS:(i + 1) * KEYS] for i in (2, 3))
        g_tok = r2[:, 4 * KEYS:4 * KEYS + KT * KVC].rearrange("p (k n) -> p k n", k=KT)
        g_wkvc = r2[:, 7236:7492].rearrange("p (c n) -> p c n", c=FC)
        g_wkr, g_wkrs = r2[0:KVC, 7492:7620], r2[0:KVC, 7620:7748]
        g_bias = r3[:, 0:KEYS]
        g_q = [r3[:, 1664 + i * P:1664 + (i + 1) * P] for i in range(2)]
        g_tmp = r5[:, 0:1024].rearrange("p (i n) -> p i n", i=2)
        g_w = r5[:, 0:KEYS]
        g_wT = r5[:, 1664:1664 + KT * P].rearrange("p (k n) -> p k n", k=KT)
        g_id = r6[:, 0:KEYS]
        g_mx, g_sum, g_rec, far = col(1), col(1), col(1), col(1)
        segend = [col(1), col(1)]
        segrow = r6[0:1, 3584:3584 + TOK].bitcast(I32)
        segrowf = r6[0:1, 4608:4608 + TOK]
        fari = sb("fari", 1, I32)

        block = ctx.enter_context(nc.Block())

        def far_ids(eng, body):
            eng.wait_ge(far_rdy, 1)
            found = eng.value_load(fari[0:1, 0:1], min_val=0, max_val=1)
            with eng.If(found != 0):
                body()

        def key_tile(i):
            return P if i < KT - 1 else KLAST

        def general_sync():
            sp = nc.sync
            sp.wait_ge(x1_rdy, TILES)
            sp.wait_ge(s_norm, 2 * TILES)
            for dst, src in ((x, x_in.rearrange("(t p) d -> p t d", p=P)), (r2[:, 2 * KEYS:4 * KEYS], keyrope_in),
                             (g_id, keyid_in), (g_wkvc, wkvc_in), (g_wkr, wkr_in), (g_wkrs, wkrs_in)):
                sp.dma_start(dst, src).then_inc(g_load, 16)
            sp.wait_ge(ld_ctx, 16)
            for b in range(B):
                sp.dma_start(ctxT, ctx_in[b]).then_inc(g_ctx, 16)
                sp.wait_ge(g_tok_mm, b + 1)
            sp.dma_start(ctxT, ctx_in[0]).then_inc(g_ctx, 16)
            sp.wait_ge(g_x, TILES)
            sp.wait_ge(g_ctx, 16 * (B + 1))

        def general_tensor():
            pe, mm = nc.tensor, nc.tensor.matmul
            pe.wait_ge(g_load, 96)
            with pe.Fori(0, B) as b:
                pe.wait_ge(g_ctx, b * 16 + 16)
                for c, (a, n) in enumerate(CH):
                    for k in range(FC):
                        last = mm(bank(0)[:, 0:n], g_wkvc[:, k, :], ctxT[:, k, a:a + n], start=k == 0,
                                  stop=k == FC - 1)
                    last.then_inc(g_kv_mm, 1)
                    pe.wait_ge(g_kv_ev, b * 4 + c + 1)
                    if c >= 1:
                        pe.wait_ge(g_rope_ev, b * 4 + c)
                    mm(bank(1)[:, 0:n], g_wkr, g_kf[1][0:KVC, a:a + n], start=True, stop=True)
                    mm(bank(2)[:, 0:n], g_wkrs, g_kf[1][0:KVC, a:a + n], start=True, stop=True)\
                        .then_inc(g_rope_mm, 1)
                for i in range(KT):
                    n = key_tile(i)
                    for k in range(FC):
                        last = mm(bank(4 + i // 8)[0:n, (i % 8) * KVC:(i % 8 + 1) * KVC], ctxT[:, k, i * P:i * P + n],
                                  g_wkvc[:, k, 0:KVC], start=k == 0, stop=k == FC - 1)
                last.then_inc(g_tok_mm, 1)
                pe.wait_ge(g_rope_ev, b * 4 + 4)
                pe.wait_ge(g_tok_ev, b + 1)
                for t in range(2):
                    for h in range(H):
                        n0 = t * H + h
                        if h >= 1:
                            pe.wait_ge(g_pv_ev, b * 32 + n0)
                        pe.wait_ge(g_q_ev, b * 32 + n0 + 1)
                        for c, (a, n) in enumerate(CH):
                            last = mm(bank(c)[:, 0:n], g_q[n0 % 2], g_kf[h % 2][:, a:a + n],
                                      start=True, stop=True)
                        last.then_inc(g_s_mm, 1)
                        pe.wait_ge(g_norm, b * 32 + n0 + 1)
                        for i in range(KT):
                            n = key_tile(i)
                            last = nc.tensor.transpose(bank(4 + i // 4)[0:n, (i % 4) * P:(i % 4 + 1) * P],
                                                       g_w[:, i * P:i * P + n], ident[:, :])
                        last.then_inc(g_t_mm, 1)
                        pe.wait_ge(g_t_ev, b * 32 + n0 + 1)
                        lo = (h % 2) * KVC
                        for i in range(KT):
                            n = key_tile(i)
                            last = mm(bank(0)[lo:lo + KVC, 0:P], g_tok[0:n, i, :], g_wT[0:n, i, :], start=i == 0,
                                      stop=i == KT - 1)
                        last.then_inc(g_pv_mm, 1)
                    pe.wait_ge(g_pv_ev, b * 32 + t * H + H)
                    for p2 in range(H // 2):
                        last = mm(bank(1)[:, 0:D], olat[:, p2, :], wuvo[:, p2, :], start=p2 == 0, stop=p2 == H // 2 - 1)
                    last.then_inc(g_o_mm, 1)
                    pe.wait_ge(g_x, b * 2 + t + 1)
            pe.wait_ge(g_x, TILES)
            pe.wait_ge(g_ctx, 16 * (B + 1))

        def general_scalar():
            act, fn = nc.scalar, nc.scalar.activation
            act.wait_ge(x1_rdy, TILES)
            with act.Fori(0, B) as b:
                for c, (a, n) in enumerate(CH):
                    act.wait_ge(g_kv_mm, b * 4 + c + 1)
                    fn(g_kf[1][0:KVC, a:a + n], bank(0)[0:KVC, 0:n], ACT.Copy)
                    fn(g_kf[0][KVC:P, a:a + n], bank(0)[KVC:P, 0:n], ACT.Copy).then_inc(g_kv_ev, 1)
                act.wait_ge(g_tok_mm, b + 1)
                fn(g_tok[:, 0:8, :], bank(4).rearrange("p (k n) -> p k n", k=8), ACT.Copy)
                fn(g_tok[:, 8:KT - 1, :], bank(5)[:, 0:4 * KVC].rearrange("p (k n) -> p k n", k=4), ACT.Copy)
                fn(g_tok[0:KLAST, KT - 1, :], bank(5)[0:KLAST, 4 * KVC:5 * KVC], ACT.Copy).then_inc(g_tok_ev, 1)
                def query(n0):
                    fn(g_q[n0 % 2], qf(n0 % H)[:, bass.ds(b * LQ + n0 // H * P, P)], ACT.Copy).then_inc(g_q_ev, 1)

                query(0)
                for n0 in range(2 * H):
                    if n0 + 1 < 2 * H:
                        query(n0 + 1)
                    act.wait_ge(g_max, b * 32 + n0 + 1)
                    fn(g_w, g_w, ACT.Exp, scale=SCALE0).then_inc(g_exp, 1)
                    act.wait_ge(g_t_mm, b * 32 + n0 + 1)
                    fn(g_wT[:, 0:12, :], bank(4, 3).rearrange("p (k n) -> p k n", k=12), ACT.Copy)
                    fn(g_wT[0:KLAST, 12, :], bank(7)[0:KLAST, 0:P], ACT.Copy).then_inc(g_t_ev, 1)

        def general_vector():
            dve, v = nc.vector, nc.vector
            dve.wait_ge(g_load, 96)
            links = [0]
            per_batch = 2 * len(CH) + 2 * (5 + 4 * H)

            with dve.Fori(0, B) as b:
                def link(ins):
                    links[0] += 1
                    ins.then_inc(g_chain, 1)
                    dve.wait_ge(g_chain, b * per_batch + links[0])

                for c, (a, n) in enumerate(CH):
                    dve.wait_ge(g_rope_mm, b * 4 + c + 1)
                    link(v.tensor_tensor(g_tmp[:, 0, 0:n], bank(1)[:, 0:n], g_cos[:, a:a + n], ALU.mult))
                    link(v.tensor_tensor(g_tmp[:, 1, 0:n], bank(2)[:, 0:n], g_sin[:, a:a + n], ALU.mult))
                    v.tensor_tensor(g_kf[0][0:R, a:a + n], g_tmp[0:R, 0, 0:n], g_tmp[0:R, 1, 0:n], ALU.add)
                    v.tensor_tensor(g_kf[1][R:P, a:a + n], g_tmp[R:P, 0, 0:n], g_tmp[R:P, 1, 0:n], ALU.add)\
                        .then_inc(g_rope_ev, 1)
                    dve.wait_ge(g_rope_ev, b * 4 + c + 1)
                for t in range(2):
                    for i, seg in enumerate((segf, seglo)):
                        link(v.tensor_copy(segend[i], seg[:, bass.ds(b * 2 + t, 1)]))
                    link(v.tensor_scalar(g_bias, g_id, segend[0], None, ALU.is_le))
                    link(v.scalar_tensor_tensor(out=g_bias, in0=g_id, scalar=segend[1], in1=g_bias, op0=ALU.is_ge,
                                                op1=ALU.mult))
                    link(v.tensor_scalar(g_bias, g_bias, -1.0, -NEG, ALU.add, ALU.mult))
                    for h in range(H):
                        n0 = t * H + h
                        dve.wait_ge(g_s_mm, b * 32 + n0 + 1)
                        for c, (a, n) in enumerate(CH):
                            last = v.tensor_tensor(g_w[:, a:a + n], bank(c)[:, 0:n], g_bias[:, a:a + n], ALU.add)
                        link(last)
                        link(v.tensor_reduce(g_mx, g_w, AX_X, ALU.max))
                        v.tensor_scalar(g_w, g_w, g_mx, None, ALU.subtract).then_inc(g_max, 1)
                        dve.wait_ge(g_exp, b * 32 + n0 + 1)
                        link(v.tensor_reduce(g_sum, g_w, AX_X, ALU.add))
                        link(v.reciprocal(g_rec, g_sum))
                        v.tensor_scalar(g_w, g_w, g_rec, None, ALU.mult).then_inc(g_norm, 1)
                        dve.wait_ge(g_pv_mm, b * 32 + n0 + 1)
                        lo = (h % 2) * KVC
                        v.tensor_copy(olat[lo:lo + KVC, h // 2, :], bank(0)[lo:lo + KVC, 0:P]).then_inc(g_pv_ev, 1)
                    dve.wait_ge(g_o_mm, b * 2 + t + 1)
                    xt = x[:, bass.ds(b * 2 + t, 1), :]
                    v.tensor_tensor(xt, xt, bank(1)[:, 0:D].unsqueeze(1), ALU.add).then_inc(g_x, 1)
            assert links[0] == per_batch, links[0]
            dve.wait_ge(g_x, TILES)

        def general_gpsimd():
            nc.gpsimd.wait_ge(g_x, TILES)

        @block.sync
        def _(sp):
            def load(s, *pairs):
                for dst, src in pairs:
                    sp.dma_start(dst, src).then_inc(s, 16)

            load(ld_key, (ctx0, ctx0_in), (wkvc, wkvc_in), (wkr, wkr_in), (wkrs, wkrs_in))
            load(ld_x, (x, x_in.rearrange("(t p) d -> p t d", p=P)), (segi[:, :], seg_in))
            load(ld_seg, (segrow, segrow_in))
            load(ld_const, (ident[:, :], ident_in), (tabs, tabs_in), (kk[:, :], kk_in))
            load(ld_q, (wuq, wuq_in), (wuk, wuk_in), (weff[:, 0::2, 0:R], wqr_in[:, 0::2, :]),
                 (weff[:, 1::2, KVC:P], wqr_in[:, 1::2, :]), (wqrs, wqrs_in), (wdq, wdq_in))
            load(ld_w1, (wnat[:, 0], wq_in), (wnat[:, 1], wp_in), (rows[:, 0:3, :], rows_in), (wkvT, wkv_in),
                 (bk[:, :], bk_in), (router, router_in))
            load(ld_vo, (wuv, wuv_in), (wo, wo_in))
            sp.wait_ge(wt_mm, 2)
            sp.wait_ge(qc_mm, 2)
            sp.wait_ge(rope_mm, 2)
            sp.wait_ge(kvt_mm, 1)
            load(ld_ctx, (ctxT, ctx_in[0]))
            far_ids(sp, general_sync)
            sp.wait_ge(x1_rdy, TILES)
            load(ld_ones, (kst[SROWS:SROWS + 3], ones_in))
            load(ld_ffn, (gu, gu_in), (sgu, sgu_in), (down[:, 0:E, :], down_in), (down[:, E, :], sdown_in))

            def stack_keys(s):
                sp.wait_ge(kpart_rdy, s + 1)
                sp.wait_ge(k_ev, len(CH) * (s + 1))
                if s >= 2:
                    sp.wait_ge(k_stk[s % 2], 96 * (s // 2))
                for j in range(3):
                    sp.dma_start(kscr[s % 2, j], kpart[j]).then_inc(k_wr, 16)
                sp.wait_ge(k_wr, 48 * (s + 1))
                if s >= 2:
                    sp.wait_ge(sc_mm, 2 * KT * (s - 1))
                for g, j in enumerate(STACK_K):
                    sp.dma_start(kst[g * DH:(g + 1) * DH, s % 2], kscr[s % 2, j].rearrange("(h d) k -> d h k", d=DH))\
                        .then_inc(k_stk[s % 2], 16)

            stack_keys(0)
            stack_keys(1)
            sp.wait_ge(k_mm, 2 * len(CH))
            sp.wait_ge(v_mm, (KT + 1) // 2)
            load(ld_ctx, (ctxT, ctx_in[1]))
            for t in range(TILES):
                sp.wait_ge(qpart_rdy, t + 1)
                for j in range(3):
                    sp.dma_start(qscr[j].rearrange("(c p) t -> p c t", p=P)[:, :, t * P:(t + 1) * P],
                                 qpart[t % 2][:, j, :].rearrange("p (c t) -> p c t", c=FC)).then_inc(q_wr[t % 2], 16)
                if t % 2 == 1:
                    b = t // 2
                    for w in q_wr:
                        sp.wait_ge(w, 48 * (b + 1))
                    if b == 0:
                        sp.wait_ge(m_mm, 6)
                    for g, j in enumerate(STACK_Q):
                        sp.dma_start(qst[g * DH:(g + 1) * DH, :, b * LQ:(b + 1) * LQ],
                                     qscr[j].rearrange("(h d) t -> d h t", d=DH)[:, :, b * LQ:(b + 1) * LQ])\
                            .then_inc(q_stk[b], 16)
            sp.wait_ge(dn_mm, TILES)
            load(ld_ffn1, (wup, wup_in), (wdn, wdn_in), (wex, wex_in), (wg, wg_in))

            def store(b):
                for i in range(2):
                    t = 2 * b + i
                    sp.wait_ge(y_rdy, t + 1)
                    sp.dma_start(out[t * P:(t + 1) * P, :], y[i][:, :]).then_inc(stored[i], 16)

            for b in range(B - 1):
                if b >= 1:
                    store(b - 1)
                stack_keys(2 * b + 2)
                stack_keys(2 * b + 3)
                if b + 2 < B:
                    sp.wait_ge(v_mm, (KT + 1) // 2 * (b + 2))
                    load(ld_ctx, (ctxT, ctx_in[b + 2]))
            store(B - 2)
            store(B - 1)
            for w in stored:
                sp.wait_ge(w, 16 * TILES // 2)

        @block.gpsimd
        def _(pool):
            def rsqrt(n):
                pool.wait_ge(eps_rdy, n + 1)
                nc.gpsimd.tensor_tensor(rstd[n % 2], mv[n % 2][:, 1:2], neghalf, ALU.pow).then_inc(rstd_rdy, 1)

            for t in range(TILES):
                rsqrt(t)
            for hf in range(2):
                for pair in range(H // 2):
                    n = hf * (H // 2) + pair
                    pool.wait_ge(qb_ev, n + 1)
                    pool.wait_ge(qa_ev, 2 * n + 2)
                    for par in range(2):
                        at = slice(par * R, par * R + R)
                        q = qf(2 * pair + par)[at, hf * 512:(hf + 1) * 512]
                        nc.gpsimd.tensor_tensor(q, q, ropet[n % 2][at, :], ALU.add).then_inc(q_rdy, 1)
                        pool.wait_ge(q_rdy, 2 * n + par + 1)
            for t in range(TILES):
                for j in range(2):
                    pool.wait_ge(s_rec, 2 * t + j + 1)
                    heads = slice(j * H // 2, (j + 1) * H // 2)
                    nc.gpsimd.tensor_tensor(sm[t % 2][:, heads, :], sm[t % 2][:, heads, :],
                                            rec0[t % 2][:, heads].unsqueeze(2).to_broadcast([P, H // 2, K0]),
                                            ALU.mult).then_inc(s_norm, 1)

            far_ids(pool, general_gpsimd)

            def split_keys(s):
                pool.wait_ge(k_ev, len(CH) * (s + 1))
                if s >= 1:
                    pool.wait_ge(k_wr, 48 * s)
                nc.gpsimd.tensor_tensor(kpart[1], kf, kpart[0], ALU.subtract).then_inc(ks_a, 1)
                pool.wait_ge(ks_a, s + 1)
                nc.gpsimd.tensor_tensor(kf, kf, kpart[0], ALU.subtract).then_inc(ks_b, 1)
                pool.wait_ge(ks_b, s + 1)
                nc.gpsimd.tensor_tensor(kpart[2], kf, kpart[1], ALU.subtract).then_inc(kpart_rdy, 1)

            split_keys(0)
            split_keys(1)
            n = TILES

            def split_queries(t):
                pool.wait_ge(qs_a, t + 1)
                nc.gpsimd.tensor_tensor(qTf[:, :], qTf[:, :], qpart[t % 2][:, 0, :], ALU.subtract).then_inc(qs_b, 1)
                pool.wait_ge(qs_c, t + 1)
                pool.wait_ge(qs_b, t + 1)
                nc.gpsimd.tensor_tensor(qpart[t % 2][:, 2, :], qTf[:, :], qpart[t % 2][:, 1, :], ALU.subtract)\
                    .then_inc(qpart_rdy, 1)

            rsqrt(n)
            n += 1
            for t in range(TILES + 2):
                if t < TILES:
                    pool.wait_ge(ntop_rdy, t + 1)
                    nc.gpsimd.tensor_tensor(sig[t % 2], eul.to_broadcast([P, 2]), ntop, ALU.pow).then_inc(pow_rdy, 1)
                if t + 1 < TILES:
                    rsqrt(n)
                    n += 1
                if 1 <= t <= TILES:
                    rsqrt(n)
                    n += 1
                if t >= 2:
                    split_queries(t - 2)
            def rsqrt3(b):
                pool.wait_ge(n3_eps, b + 1)
                nc.gpsimd.tensor_tensor(rstd3, mv3[:, :, 1], neghalf.to_broadcast([P, 2]), ALU.pow)\
                    .then_inc(n3_rstd, 1)

            for b in range(B):
                if b >= 1:
                    rsqrt3(b - 1)
                if b + 1 < B:
                    split_keys(2 * b + 2)
                    split_keys(2 * b + 3)
            rsqrt3(B - 1)

        @block.tensor
        def _(pe):
            mm = nc.tensor.matmul

            pe.wait_ge(ld_key, 64)
            for c in range(FC):
                last = mm(bank(6), wkvc[:, c, :], ctx0[:, c, :], start=c == 0, stop=c == FC - 1)
            last.then_inc(kv_mm, 1)
            for b in range(B):
                for c in range(FC):
                    last = mm(bank(5)[:, b * KVC:(b + 1) * KVC], ctx0[:, c, b * K0:(b + 1) * K0], wkvc[:, c, 0:KVC],
                              start=c == 0, stop=c == FC - 1)
            last.then_inc(kvt_mm, 1)
            pe.wait_ge(kv_ev, 1)
            mm(bank(7), wkr, kf0[1][0:KVC, :], start=True, stop=True).then_inc(rope_mm, 1)
            pe.wait_ge(kv_ev, 2)
            mm(bank(6), wkrs, kf0[1][0:KVC, :], start=True, stop=True).then_inc(rope_mm, 1)
            pe.wait_ge(ld_q, 96)
            for h in range(H):
                last = mm(bank(h // 8)[0:QC, (h % 8) * KVC:(h % 8 + 1) * KVC], wuq[:, h, :], wuk[:, h, :],
                          start=True, stop=True)
                if h % 8 == 7:
                    last.then_inc(m_mm, 1)
            pe.wait_ge(ld_const, 48)
            for t in range(TILES):
                pe.wait_ge(xn_rdy, t + 1)
                if t >= 2:
                    pe.wait_ge(xnT_ev, t - 1)
                for c in range(FC):
                    last = nc.tensor.transpose(bank(2 + t % 2)[:, c * P:(c + 1) * P], xn[t % 2][:, c * P:(c + 1) * P],
                                               ident[:, :])
                last.then_inc(xnT_mm, 1)
            for hf in range(2):
                pe.wait_ge(xnT_ev, 4 * hf + 4)
                for c in range(FC):
                    last = mm(bank(4 - hf)[0:QC, :], wdq[:, c, :], xnT[:, c, hf * 512:(hf + 1) * 512], start=c == 0,
                              stop=c == FC - 1)
                last.then_inc(qc_mm, 1)
            for m in range(2):
                pe.wait_ge(wint_rdy, m + 1)
                if m == 0:
                    pe.wait_ge(rope_done, 1)
                tb = bank(6 + m).bitcast(BF16)
                for c in range(FC):
                    for o in range(FC):
                        last = nc.tensor.transpose(tb[:, (c * FC + o) * P:(c * FC + o + 1) * P],
                                                   (wint, wint2)[m][:, o, c * P:(c + 1) * P], identb[:, :])
                last.then_inc(wt_mm, 1)
            pe.wait_ge(kvt_ev, 1)
            for m in range(2):
                for o in range(FC):
                    last = mm(bank(5)[:, m * D + o * P:m * D + (o + 1) * P],
                              wsc[:, 2 * m + o:2 * m + o + 1].to_broadcast([P, P]), ident[:, :], start=True, stop=True)
            last.then_inc(sw_mm, 1)
            pe.wait_ge(ld_vo, 32)
            pe.wait_ge(m_ev, 2)
            pe.wait_ge(xnT_ev, TILES)
            pe.wait_ge(qc_ev, 2)
            for h in range(H):
                p2 = h // 2
                last = mm(bank(p2 // 2)[(h % 2) * KVC:(h % 2 + 1) * KVC, (p2 % 2) * D:(p2 % 2 + 1) * D],
                          wuv[:, h, :], wo[:, h, :], start=True, stop=True)
                if h % 4 == 3:
                    last.then_inc(m_mm, 1)

            for hf in range(2):
                at = slice(hf * 512, (hf + 1) * 512)
                for h in range(H):
                    n = hf * H + h
                    if n >= 4:
                        pe.wait_ge(qa_ev, n - 3)
                    else:
                        pe.wait_ge(m_ev, 3 + n)
                    mm(bank(n % 4), weff[:, h, :], qcT[:, at], start=True, stop=True).then_inc(qa_mm, 1)
                    if h % 2 == 1:
                        k = hf * (H // 2) + h // 2
                        if k >= 2:
                            pe.wait_ge(qb_ev, k - 1)
                        elif k == 0:
                            pe.wait_ge(sw_ev, 1)
                        mm(bank(4 + k % 2), wqrs[:, h // 2, :], qcT[:, at], start=True,
                           stop=True).then_inc(qb_mm, 1)

            def attend0(t):
                b = t // 2
                at = slice(t * P, (t + 1) * P)
                pe.wait_ge(mask_rdy, t + 1)
                if t % 4 == 0:
                    pe.wait_ge(q_rdy, H * (t // 4 + 1))
                    pe.wait_ge(qa_ev, H * (t // 4 + 1))
                if t == 0:
                    pe.wait_ge(qa_ev, 2 * H)
                for g in range(4):
                    if t > 0 and g % 2 == 0:
                        pe.wait_ge(s_sub, 2 * t - 1 + g // 2)
                    mm(bank(g), identb[:, :], maskb[t % 2].unsqueeze(1).to_broadcast([P, 4, K0]), start=True,
                       stop=False, skip_group_check=True)
                    for k in range(4):
                        h = 4 * g + k
                        last = mm(bank(g)[:, k * K0:(k + 1) * K0], qf(h)[:, at], kf0[h % 2][:, b * K0:(b + 1) * K0],
                                  start=False, stop=True, skip_group_check=True)
                    if g % 2 == 1:
                        last.then_inc(s_mm, 1)

            def values0(t):
                b = t // 2
                if t == 0:
                    pe.wait_ge(qb_ev, H)
                    pe.wait_ge(kvt_ev, 1)
                for g in range(4):
                    n = 4 * t + g
                    if g % 2 == 0:
                        pe.wait_ge(s_norm, 2 * t + g // 2 + 1)
                    if n >= 2:
                        pe.wait_ge(pt_ev, n - 1)
                    for k in range(4):
                        last = nc.tensor.transpose(bank(4 + n % 2)[:, k * P:(k + 1) * P], sm[t % 2][:, 4 * g + k, :],
                                                   ident[:, :])
                    last.then_inc(pt_mm, 1)
                for j in range(2):
                    n = 2 * t + j
                    pe.wait_ge(pt_ev, 4 * t + 2 * j + 2)
                    if n >= 1:
                        pe.wait_ge(pv_ev, n)
                    elif n == 0:
                        pe.wait_ge(wt_ev, 2)
                    for par in range(2):
                        last = mm(bank(6)[par * KVC:(par + 1) * KVC, :], kvtok[:, b, :],
                                  pT[:, 8 * j + par:8 * j + 8:2, :], start=True, stop=True)
                    last.then_inc(pv_mm, 1)
                if t >= 1:
                    pe.wait_ge(x1_rdy, t)
                for p2 in range(H // 2):
                    if p2 % 4 == 0:
                        pe.wait_ge(pv_ev, 2 * t + p2 // 4 + 1)
                    last = mm(bank(7)[:, 0:D], olat[:, p2, :], wuvo[:, p2, :], start=p2 == 0, stop=p2 == H // 2 - 1)
                last.then_inc(ao_mm, 1)

            for t in range(TILES + 1):
                if t < TILES:
                    attend0(t)
                if t >= 1:
                    values0(t - 1)

            far_ids(pe, general_tensor)

            def keys(s, c, bnk, between=None):
                a, n = CH[c]
                for k in range(FC):
                    if k >= 1 and between:
                        between(4 * n)
                    last = mm(bank(bnk)[:, 0:n], wkvT[:, k, (s % 2) * P:(s % 2 + 1) * P], ctxT[:, k, a:a + n],
                              start=k == 0, stop=k == FC - 1)
                last.then_inc(k_mm, 1)

            def values(b, j, bnk, between=None):
                for i in range(2 * j, min(2 * j + 2, KT)):
                    n = P if i < KT - 1 else KLAST
                    for k in range(FC):
                        if i % 2 + k >= 1 and between:
                            between(4 * D)
                        last = mm(bank(bnk)[0:n, (i % 2) * D:(i % 2 + 1) * D], ctxT[:, k, i * P:i * P + n],
                                  wkvT[:, k, D:2 * D], start=k == 0, stop=k == FC - 1)
                last.then_inc(v_mm, 1)

            NV = (KT + 1) // 2
            pe.wait_ge(ld_ctx, 16)
            pe.wait_ge(x1_rdy, TILES)
            done = []
            for s in range(2):
                for c in range(len(CH)):
                    if len(done) >= 2:
                        pe.wait_ge(*done[-2])
                    keys(s, c, 6 + len(done) % 2)
                    done.append((k_ev, len(CH) * s + c + 1))
            for j in range(NV):
                pe.wait_ge(*done[-2])
                values(0, j, 6 + len(done) % 2)
                done.append((v_ev, j + 1))

            def turn_h(t):
                pe.wait_ge(xn_rdy, TILES + 1 + t + max(0, t - 2))
                if t == 0:
                    pe.wait_ge(v_ev, NV)
                for c in range(FC):
                    last = nc.tensor.transpose(bank(7)[:, c * P:(c + 1) * P], xn[0][:, c * P:(c + 1) * P], ident[:, :])
                last.then_inc(hT_mm, 1)

            def gate_up(t, c):
                n = 5 * t + c
                if c == 0:
                    pe.wait_ge(hT_ev, t + 1)
                if n >= 4:
                    pe.wait_ge(hid_rdy, n - 3)
                w = gu[:, :, c * 512:(c + 1) * 512] if c < 4 else sgu
                for k in range(FC):
                    last = mm(bank(n % 4)[:, 0:w.shape[2]], hT[t % 2][:, k, :], w[:, k, :], start=k == 0,
                              stop=k == FC - 1)
                last.then_inc(gu_mm, 1)

            def route(t):
                for k in range(FC):
                    last = mm(bank(7)[:, 0:E], hT[t % 2][:, k, :], router[:, k, :], start=k == 0, stop=k == FC - 1)
                last.then_inc(rt_mm, 1)

            def combine(t):
                pe.wait_ge(hid_rdy, 5 * t + 5)
                for g in range(3):
                    n = 3 * t + g
                    if n >= 2:
                        pe.wait_ge(ht_ev, n - 1)
                    for e in range(4 * g, min(4 * g + 4, HB)):
                        last = nc.tensor.transpose(bank(4 + n % 2)[:, (e % 4) * P:(e % 4 + 1) * P], hid[t % 2][:, e, :],
                                                   ident[:, :])
                    last.then_inc(ht_mm, 1)
                if t >= 1:
                    pe.wait_ge(x2_rdy, t)
                for e in range(HB):
                    if e % 4 == 0:
                        pe.wait_ge(ht_ev, 3 * t + e // 4 + 1)
                    last = mm(bank(6)[:, 0:D], hidT[:, e, :], down[:, e, :], start=e == 0, stop=e == HB - 1)
                last.then_inc(dn_mm, 1)

            def turn_xq(t):
                pe.wait_ge(xq_rdy, t + 1)
                pe.wait_ge(lg_rdy, min(t + 3, TILES))
                if t >= 1:
                    pe.wait_ge(q1T_ev, t)
                for c in range(FC):
                    last = nc.tensor.transpose(bank(7).bitcast(BF16)[:, c * P:(c + 1) * P],
                                               xq[t % 2][:, c * P:(c + 1) * P], identb[:, :])
                last.then_inc(xqT_mm, 1)

            def project_q(t):
                pe.wait_ge(xqT_ev, t + 1)
                for k in range(FC):
                    last = mm(bank(7)[:, 0:D], xqT[:, k, :], wintT[:, 0, k, :], start=k == 0, stop=k == FC - 1)
                last.then_inc(q1_mm, 1)

            def turn_q(t):
                pe.wait_ge(q1_rdy, t + 1)
                for c in range(FC):
                    last = nc.tensor.transpose(bank(7)[:, c * P:(c + 1) * P], qtok[:, c * P:(c + 1) * P], ident[:, :])
                last.then_inc(q1T_mm, 1)

            def max_scores(quad, n):
                b, s, u, c = quad // 4, quad // 2, n // len(CH), n % len(CH)
                h = 4 * (quad % 4) + u // 2
                ca = 8 * len(CH) * quad + n
                if n == 0:
                    pe.wait_ge(k_stk[s % 2], 96 * (s // 2 + 1))
                    pe.wait_ge(q_stk[b], 96)
                if ca >= 2:
                    pe.wait_ge(mx_rdy, ca - 1)
                a, m = CH[c]
                q0 = b * LQ + (u % 2) * P
                mm(bank(ca % 2)[:, 0:m], qst[0:SROWS, h, q0:q0 + P], kst[0:SROWS, s % 2, h % HALF, a:a + m],
                   start=True, stop=True).then_inc(mx_mm, 1)

            def first_maxima(t, third):
                for n in first_chunks(t, third):
                    max_scores(0, n)

            pe.wait_ge(ld_ffn, 64)
            for t in range(TILES + 2):
                if t < TILES:
                    if t >= 3:
                        pe.wait_ge(q1T_ev, t - 2)
                    turn_h(t)
                    gate_up(t, 0)
                    route(t)
                    gate_up(t, 1)
                if 1 <= t <= TILES:
                    combine(t - 1)
                if t >= 2:
                    turn_xq(t - 2)
                if t < TILES:
                    gate_up(t, 2)
                else:
                    first_maxima(t, 0)
                if t >= 2:
                    project_q(t - 2)
                if t < TILES:
                    gate_up(t, 3)
                else:
                    first_maxima(t, 1)
                if t >= 2:
                    turn_q(t - 2)
                if t < TILES:
                    gate_up(t, 4)
                else:
                    first_maxima(t, 2)

            taken = [(q1T_ev, TILES)]

            def bank7(reader, value):
                pe.wait_ge(*taken[0])
                taken[0] = (reader, value)

            def shift(quad):
                bank7(sh_rdy, quad + 1)
                pe.wait_ge(nst_rdy, quad + 1)
                tb = bank(7).bitcast(BF16)
                for u in range(8):
                    last = nc.tensor.transpose(tb[SROWS:SROWS + 3, u * P:(u + 1) * P], nst[quad % 2][:, u, :],
                                               identb[:, :])
                last.then_inc(sh_mm, 1)

            def scores(quad, kt, first):
                i, b, s = KT * quad + kt, quad // 4, quad // 2
                n = P if kt < KT - 1 else KLAST
                if first == 0:
                    if kt == 0:
                        pe.wait_ge(sh_rdy, quad + 1)
                    if i == 0:
                        pe.wait_ge(ld_ones, 16)
                    if i >= 2:
                        pe.wait_ge(ex_rdy, i - 1)
                for k in (first, first + 1):
                    h = 4 * (quad % 4) + k
                    last = mm(bank(2 + 2 * (i % 2), 2)[0:n, k * LQ:(k + 1) * LQ],
                              kst[0:SROWS + 3, s % 2, h % HALF, kt * P:kt * P + n],
                              qst[0:SROWS + 3, h, b * LQ:(b + 1) * LQ], start=True, stop=True)
                if first == 2:
                    last.then_inc(sc_mm, 1)

            def weigh(i):
                quad, kt = i // KT, i % KT
                b = quad // 4
                n = P if kt < KT - 1 else KLAST
                pe.wait_ge(ex_rdy, i + 1)
                if kt == 0:
                    pe.wait_ge(v_ev, NV * (b + 1))
                    if quad >= 1:
                        pe.wait_ge(po_rdy, quad)
                if i == 0:
                    pe.wait_ge(vone_rdy, 1)
                    pe.wait_ge(po_zero, 1)
                for k in range(4):
                    h = 4 * (quad % 4) + k
                    last = mm(bank(6)[32 * k:32 * k + VW, 0:LQ], vx[0:n, b % 2, kt, h, :],
                              pr[i % 3][0:n, k * LQ:(k + 1) * LQ], start=kt == 0, stop=kt == KT - 1,
                              skip_group_check=True)
                last.then_inc(av_mm, 1)

            def turn_out(quad):
                bank7(o_rdy, quad + 1)
                pe.wait_ge(po_rdy, quad + 1)
                for q in range(2):
                    last = nc.tensor.transpose(bank(7)[:, q * P:(q + 1) * P], poS[quad % 2][:, q * P:(q + 1) * P],
                                               ident[:, :])
                last.then_inc(ot_mm, 1)

            def tail(b, part, between):
                tiles = range(2)
                if part == "turn_o":
                    bank7(oiT_ev, b + 1)
                    pe.wait_ge(oi_rdy, b + 1)
                    for i in tiles:
                        for c in range(FC):
                            at = (i * FC + c) * P
                            last = nc.tensor.transpose(bank(7).bitcast(BF16)[:, at:at + P],
                                                       xq[i][:, c * P:(c + 1) * P], identb[:, :])
                    last.then_inc(oiT_mm, 1)
                elif part == "project":
                    bank7(wp_ev, b + 1)
                    pe.wait_ge(oiT_ev, b + 1)
                    for i in tiles:
                        for k in range(FC):
                            last = mm(bank(7)[:, i * D:(i + 1) * D], xqT2[:, i, k, :], wintT[:, 1, k, :],
                                      start=k == 0, stop=k == FC - 1)
                    last.then_inc(wp_mm, 1)
                elif part == "turn_x":
                    bank7(x3T_ev, b + 1)
                    pe.wait_ge(n3_rdy, b + 1)
                    for i in tiles:
                        for c in range(FC):
                            at = (i * FC + c) * P
                            last = nc.tensor.transpose(bank(7)[:, at:at + P], xn[i][:, c * P:(c + 1) * P],
                                                       ident[:, :])
                    last.then_inc(x3T_mm, 1)
                elif part == "up":
                    bank7(up_rdy, b + 1)
                    pe.wait_ge(x3T_ev, b + 1)
                    if b == 0:
                        pe.wait_ge(ld_ffn1, 64)
                    for f in range(FC):
                        for k in range(FC):
                            if f + k >= 1:
                                between(4 * D)
                            last = mm(bank(7)[:, f * 2 * P:(f + 1) * 2 * P], wup[:, k, f * P:(f + 1) * P],
                                      hT2[:, :, k, :], start=k == 0, stop=k == FC - 1)
                    last.then_inc(up_mm, 1)
                elif part == "gate":
                    bank7(lg1_rdy, b + 1)
                    for i in tiles:
                        for k in range(FC):
                            last = mm(bank(7)[:, i * E:(i + 1) * E], hT[i][:, k, :], wg[:, k, :], start=k == 0,
                                      stop=k == FC - 1)
                    last.then_inc(rt_mm, 1)
                elif part == "down":
                    bank7(d_rdy, b + 1)
                    pe.wait_ge(up_rdy, b + 1)
                    for i in tiles:
                        for k in range(FC):
                            if i + k >= 1:
                                between(4 * D)
                            last = mm(bank(7)[:, i * D:(i + 1) * D], upT[:, k, i * P:(i + 1) * P], wdn[:, k, :],
                                      start=k == 0, stop=k == FC - 1)
                    last.then_inc(d_mm, 1)
                elif part == "expert":
                    bank7(y_rdy, 2 * b + 2)
                    for i in tiles:
                        for k in range(FC):
                            if i + k >= 1:
                                between(4 * D)
                            last = mm(bank(7)[:, i * D:(i + 1) * D], hT[i][:, k, :], wex[:, k, :], start=k == 0,
                                      stop=k == FC - 1)
                    last.then_inc(y_mm, 1)

            def beside(jobs, between):
                for what, *a in jobs:
                    if what == "shift":
                        shift(*a)
                    elif what == "k":
                        s, c = a
                        bank7(k_ev, len(CH) * s + c + 1)
                        if c == 0:
                            pe.wait_ge(ld_ctx, 16 * (s // 2 + 1))
                        keys(s, c, 7, between)
                    elif what == "v":
                        b, j = a
                        bank7(v_ev, NV * b + j + 1)
                        values(b, j, 7, between)
                    elif what == "out":
                        turn_out(*a)
                    elif what == "tail":
                        tail(*a, between)

            shift(0)
            for quad in range(QUADS + 2):
                for kt in range(KT):
                    jobs = BESIDE.get((quad, kt), [])
                    maxima = [j for j in jobs if j[0] == "max"]
                    others = [j for j in jobs if j[0] != "max"]

                    total, count = step_work(others), len(maxima)
                    passed = [0]

                    def pace(columns):
                        passed[0] += columns
                        while maxima and (count - len(maxima)) * total < count * passed[0]:
                            max_scores(*maxima.pop(0)[1:])

                    if quad < QUADS:
                        pace(1)
                        scores(quad, kt, 0)
                        pace(2 * LQ)
                        scores(quad, kt, 2)
                        pace(2 * LQ)
                        if quad or kt:
                            weigh(KT * quad + kt - 1)
                        pace(4 * LQ)
                    elif quad == QUADS and kt == 0:
                        weigh(STEPS - 1)
                    beside(others, pace)
                    while maxima:
                        max_scores(*maxima.pop(0)[1:])

        @block.scalar
        def _(act):
            fn = nc.scalar.activation

            act.wait_ge(kv_mm, 1)
            fn(kf0[1][0:KVC, :], bank(6)[0:KVC, :], ACT.Copy).then_inc(kv_ev, 1)
            fn(kf0[0][KVC:P, :], bank(6)[KVC:P, :], ACT.Copy).then_inc(kv_ev, 1)
            act.wait_ge(kvt_mm, 1)
            fn(kvtok, bank(5)[:, 0:B * KVC].rearrange("p (b n) -> p b n", b=B), ACT.Copy).then_inc(kvt_ev, 1)
            act.wait_ge(ld_q, 96)
            for g in range(2):
                act.wait_ge(m_mm, g + 1)
                src = bank(g)[0:QC, :].rearrange("p (h n) -> p h n", h=8)
                fn(weff[:, 8 * g:8 * g + 8:2, R:P], src[:, 0::2, :], ACT.Copy)
                fn(weff[:, 8 * g + 1:8 * g + 8:2, 0:KVC], src[:, 1::2, :], ACT.Copy).then_inc(m_ev, 1)
            for t in range(TILES):
                act.wait_ge(xnT_mm, t + 1)
                fn(xnT[:, :, t * P:(t + 1) * P], bank(2 + t % 2)[:, 0:D].rearrange("p (c t) -> p c t", c=FC),
                   ACT.Copy).then_inc(xnT_ev, 1)
            for hf in range(2):
                act.wait_ge(qc_mm, hf + 1)
                fn(qcT[:, hf * 512:(hf + 1) * 512], bank(4 - hf)[0:QC, :], ACT.Copy).then_inc(qc_ev, 1)
            for m in range(2):
                act.wait_ge(wt_mm, m + 1)
                fn(wintT[:, m], bank(6 + m).bitcast(BF16)[:, 0:2 * D].rearrange("p (c n) -> p c n", c=FC),
                   ACT.Copy).then_inc(wt_ev, 1)
            act.wait_ge(sw_mm, 1)
            act.wait_ge(ld_w1, 96)
            fn(rows[:, 3:5, :], bank(5).rearrange("p (r d) -> p r d", r=2), ACT.Copy).then_inc(sw_ev, 1)
            for g in range(4):
                act.wait_ge(m_mm, 3 + g)
                fn(wuvo[:, 2 * g:2 * g + 2, :], bank(g).rearrange("p (h n) -> p h n", h=2), ACT.Copy)\
                    .then_inc(m_ev, 1)
            act.wait_ge(m_ev, 6)

            for t in range(TILES + 1):
                if t >= 1:
                    for g in range(4):
                        act.wait_ge(pt_mm, 4 * (t - 1) + g + 1)
                        if t >= 2 and g == 0:
                            act.wait_ge(pv_mm, 2 * (t - 1))
                        elif t == 1 and g == 0:
                            act.wait_ge(kv_mm, 1)
                        fn(pT[:, 4 * g:4 * g + 4, :], bank(4 + g % 2).rearrange("p (h n) -> p h n", h=4), ACT.Copy)\
                            .then_inc(pt_ev, 1)
                    for j in range(2):
                        act.wait_ge(pv_mm, 2 * (t - 1) + j + 1)
                        if t >= 2 and j == 0:
                            act.wait_ge(ao_mm, t - 1)
                        fn(olat[:, 4 * j:4 * j + 4, :], bank(6).rearrange("p (h n) -> p h n", h=4), ACT.Copy)\
                            .then_inc(pv_ev, 1)
                if t < TILES:
                    for j in range(2):
                        act.wait_ge(s_sub, 2 * t + j + 1)
                        half = sm[t % 2][:, j * H // 2:(j + 1) * H // 2, :]
                        fn(half, half, ACT.Exp, scale=SCALE0).then_inc(s_exp, 1)

            far_ids(act, general_scalar)

            def keys_bias(s, c, bnk):
                a, n = CH[c]
                act.wait_ge(k_mm, len(CH) * s + c + 1)
                if c == 0 and s == 0:
                    act.wait_ge(pt_mm, 4 * TILES)
                elif c == 0:
                    act.wait_ge(kpart_rdy, s)
                    act.wait_ge(k_wr, 48 * s)
                fn(kf[:, a:a + n], bank(bnk)[:, 0:n], ACT.Identity, bias=bk[:, s % 2:s % 2 + 1])
                fn(kpart[0][:, a:a + n], bank(bnk)[:, 0:n], ACT.Identity, bias=bk[:, s % 2:s % 2 + 1])\
                    .then_inc(k_ev, 1)

            NV = (KT + 1) // 2

            def values_copy(b, j, bnk):
                act.wait_ge(v_mm, NV * b + j + 1)
                if b >= 2 and j == 0:
                    act.wait_ge(av_mm, 4 * KT * (b - 1))
                n = P if j < NV - 1 else KLAST
                tiles = 2 if 2 * j + 2 <= KT else 1
                fn(vx[0:n, b % 2, 2 * j:2 * j + tiles, :, 0:DH],
                   bank(bnk)[0:n, 0:tiles * D].rearrange("p (k h n) -> p k h n", k=tiles, h=H), ACT.Copy)\
                    .then_inc(v_ev, 1)

            n = 0
            for s in range(2):
                for c in range(len(CH)):
                    keys_bias(s, c, 6 + n % 2)
                    n += 1
            act.wait_ge(x1_rdy, TILES)
            for j in range(NV):
                values_copy(0, j, 6 + n % 2)
                n += 1

            def silu(t, c):
                n = 5 * t + c
                act.wait_ge(gu_mm, n + 1)
                if c == 0:
                    act.wait_ge(p_rdy, t + 1)
                if n >= 2:
                    act.wait_ge(hid_rdy, n - 1)
                src = bank(n % 4)
                if c < 4:
                    for e in range(2):
                        fn(sg[n % 2][:, e, :], src[:, e * 2 * I:e * 2 * I + I], ACT.Silu,
                           scale=probs[t % 2][:, 2 * c + e:2 * c + e + 1]).then_inc(silu_rdy, 1)
                else:
                    fn(sg[n % 2][:, 0, :], src[:, 0:I], ACT.Silu).then_inc(silu_rdy, 1)

            act.wait_ge(k_wr, 96)
            for t in range(TILES + 2):
                if t < TILES:
                    act.wait_ge(hT_mm, t + 1)
                    if t >= 2:
                        act.wait_ge(gu_mm, 5 * (t - 1))
                    fn(hT[t % 2], bank(7)[:, 0:D].rearrange("p (c t) -> p c t", c=FC), ACT.Copy).then_inc(hT_ev, 1)
                    silu(t, 0)
                    silu(t, 1)
                if 1 <= t <= TILES:
                    for g in range(3):
                        n = 3 * (t - 1) + g
                        act.wait_ge(ht_mm, n + 1)
                        if g == 0 and t >= 2:
                            act.wait_ge(dn_mm, t - 1)
                        e = min(4, HB - 4 * g)
                        fn(hidT[:, 4 * g:4 * g + e, :], bank(4 + n % 2)[:, 0:e * P].rearrange("p (e n) -> p e n", e=e),
                           ACT.Copy).then_inc(ht_ev, 1)
                if t >= 2:
                    act.wait_ge(xqT_mm, t - 1)
                    if t >= 3:
                        act.wait_ge(q1_mm, t - 2)
                    fn(xqT, bank(7).bitcast(BF16)[:, 0:D].rearrange("p (c t) -> p c t", c=FC), ACT.Copy)\
                        .then_inc(xqT_ev, 1)
                if t < TILES:
                    silu(t, 2)
                    silu(t, 3)
                if t >= 2:
                    act.wait_ge(q1T_mm, t - 1)
                    if t >= 3:
                        act.wait_ge(qpart_rdy, t - 2)
                    fn(qTf[:, :], bank(7)[:, 0:D], ACT.Copy).then_inc(q1T_ev, 1)
                if t < TILES:
                    silu(t, 4)

            def beside(quad, kt):
                for what, *a in BESIDE.get((quad, kt), []):
                    if what == "shift":
                        shift_rows(*a)
                    elif what == "k":
                        keys_bias(*a, 7)
                    elif what == "v":
                        values_copy(*a, 7)
                    elif what == "tail":
                        b, part = a
                        if part == "turn_o":
                            act.wait_ge(oiT_mm, b + 1)
                            if b == 0:
                                act.wait_ge(q1_mm, TILES)
                            fn(xqT2, bank(7).bitcast(BF16)[:, 0:2 * D].rearrange("p (t c n) -> p t c n", t=2, c=FC),
                               ACT.Copy).then_inc(oiT_ev, 1)
                        elif part == "turn_x":
                            act.wait_ge(x3T_mm, b + 1)
                            fn(hT2, bank(7).rearrange("p (t c n) -> p t c n", t=2, c=FC), ACT.Copy)\
                                .then_inc(x3T_ev, 1)
                        elif part == "route":
                            act.wait_ge(dtop_rdy, b + 1)
                            fn(etop, dtop, ACT.Exp).then_inc(etop_rdy, 1)

            def shift_rows(quad):
                act.wait_ge(sh_mm, quad + 1)
                h, b = 4 * (quad % 4), quad // 4
                if quad == 0:
                    act.wait_ge(m_mm, 6)
                fn(qst[SROWS:SROWS + 3, h:h + 4, b * LQ:(b + 1) * LQ],
                   bank(7).bitcast(BF16)[SROWS:SROWS + 3, :].rearrange("p (h t) -> p h t", h=4), ACT.Copy)\
                    .then_inc(sh_rdy, 1)

            def out_copy(quad):
                act.wait_ge(av_mm, KT * (quad + 1))
                if quad >= 2:
                    act.wait_ge(ot_mm, quad - 1)
                fn(poS[quad % 2], bank(6)[:, 0:LQ], ACT.Copy).then_inc(po_rdy, 1)

            shift_rows(0)
            act.wait_ge(dn_mm, TILES)
            for quad in range(QUADS + 2):
                for kt in range(KT):
                    if quad < QUADS:
                        i = KT * quad + kt
                        n = P if kt < KT - 1 else KLAST
                        act.wait_ge(sc_mm, i + 1)
                        if i >= 3:
                            act.wait_ge(av_mm, i - 2)
                        fn(pr[i % 3][0:n, :], bank(2 + 2 * (i % 2), 2)[0:n, :], ACT.Exp, scale=SCALE1)\
                            .then_inc(ex_rdy, 1)
                    if kt == 0 and 1 <= quad <= QUADS:
                        out_copy(quad - 1)
                    beside(quad, kt)

        @block.vector
        def _(dve):
            v = nc.vector
            chain = [0]

            def link(ins):
                chain[0] += 1
                ins.then_inc(dve_chain, 1)
                dve.wait_ge(dve_chain, chain[0])

            norms = [0]

            def layer_norm(t, into):
                n = norms[0]
                norms[0] += 1
                link(v.bn_stats(stats, x[:, t, :]))
                link(v.bn_aggr(mv[n % 2], stats))
                v.tensor_scalar(mv[n % 2][:, 1:2], mv[n % 2][:, 1:2], LN_EPS, None, ALU.add).then_inc(eps_rdy, 1)
                dve.wait_ge(rstd_rdy, n + 1)
                v.tensor_scalar(into, x[:, t, :], mv[n % 2][:, 0:1], rstd[n % 2], ALU.subtract, ALU.mult)\
                    .then_inc(xn_rdy, 1)
                dve.wait_ge(xn_rdy, n + 1)

            def quantise(src, amax, rscale, scale, mag, into, done):
                link(v.tensor_reduce(amax, src, AX_X, ALU.max, apply_absolute_value=True))
                link(v.tensor_scalar(scale, amax, float(np.float32(1) / np.float32(127)), 1e-8, ALU.mult, ALU.max))
                link(v.reciprocal(rscale, scale))
                link(v.tensor_scalar(mag, src, rscale, 127.0, ALU.mult, ALU.min))
                link(v.tensor_scalar(mag, mag, -127.0, MAGIC, ALU.max, ALU.add))
                v.tensor_scalar(into, mag, -MAGIC, None, ALU.add).then_inc(done, 1)

            link(v.memset(neghalf, -0.5))
            link(v.memset(eul, float(np.exp(np.float64(1.0)))))
            dve.wait_ge(ld_const, 48)
            link(v.tensor_copy(identb[:, :], ident[:, :]))
            cosr, sinr = (tabs[:, i, 0:K0].unsqueeze(1).to_broadcast([P, B, K0]) for i in (2, 3))
            as_b = "p (b k) -> p b k"
            dve.wait_ge(rope_mm, 1)
            link(v.tensor_tensor(ropet[0].rearrange(as_b, b=B), bank(7).rearrange(as_b, b=B), cosr, ALU.mult))
            dve.wait_ge(rope_mm, 2)
            link(v.tensor_tensor(ropet[1].rearrange(as_b, b=B), bank(6).rearrange(as_b, b=B), sinr, ALU.mult))
            link(v.tensor_tensor(kf0[1][KVC:P, :], ropet[0][KVC:P, :], ropet[1][KVC:P, :], ALU.add))
            v.tensor_tensor(kf0[0][0:R, :], ropet[0][0:R, :], ropet[1][0:R, :], ALU.add).then_inc(rope_done, 1)
            dve.wait_ge(rope_done, 1)
            dve.wait_ge(ld_x, 32)
            link(v.tensor_copy(segf, segi[:, :]))
            link(v.tensor_scalar(seglo, segf, float(-LOOKBACK), None, ALU.add))
            dve.wait_ge(ld_seg, 16)
            link(v.tensor_copy(segrowf, segrow))
            link(v.tensor_reduce(far[0:1], segrowf, AX_X, ALU.max))
            link(v.tensor_reduce(g_mx[0:1], segrowf, AX_X, ALU.min))
            link(v.tensor_scalar(far[0:1], far[0:1], float(K0 - 1), None, ALU.is_gt))
            link(v.tensor_scalar(g_mx[0:1], g_mx[0:1], 0.0, far[0:1], ALU.is_lt, ALU.max))
            v.tensor_copy(fari[0:1, :], g_mx[0:1]).then_inc(far_rdy, 1)
            for t in range(TILES):
                if t >= 2:
                    dve.wait_ge(xnT_mm, t - 1)
                layer_norm(t, xn[t % 2])
            dve.wait_ge(ld_w1, 96)
            for m in range(2):
                for o in range(FC):
                    n = 2 * m + o
                    quantise(wnat[:, m, o, :], wam[:, n:n + 1], wrs[:, n:n + 1], wsc[:, n:n + 1], wmag[:, m, o, :],
                             (wint, wint2)[m][:, o, :], wint_rdy if o == FC - 1 else dve_chain)
                    if o < FC - 1:
                        chain[0] += 1
            for hf in range(2):
                for h in range(H):
                    n = hf * H + h
                    q = qf(h)[:, hf * 512:(hf + 1) * 512].rearrange(as_b, b=2)
                    cosq = tabs[:, h % 2, :].unsqueeze(1).to_broadcast([P, 2, LQ])
                    dve.wait_ge(qa_mm, n + 1)
                    v.tensor_tensor(q, bank(n % 4).rearrange(as_b, b=2), cosq, ALU.mult).then_inc(qa_ev, 1)
                    if h % 2 == 1:
                        k = hf * (H // 2) + h // 2
                        dve.wait_ge(qb_mm, k + 1)
                        if k >= 2:
                            dve.wait_ge(q_rdy, 2 * k - 2)
                        sinq = tabs[:, 3, :].unsqueeze(1).to_broadcast([P, 2, LQ])
                        v.tensor_tensor(ropet[k % 2].rearrange(as_b, b=2),
                                        bank(4 + k % 2).rearrange(as_b, b=2), sinq, ALU.mult).then_inc(qb_ev, 1)

            def mask(t):
                if t >= 2:
                    dve.wait_ge(s_mm, 2 * (t - 1))
                link(v.tensor_scalar(xmag[:, 0:K0], kk[:, :], segf[:, t:t + 1], MASK, ALU.is_le, ALU.mult))
                link(v.tensor_scalar(xmag[:, K0:2 * K0], kk[:, :], seglo[:, t:t + 1], MASK, ALU.is_ge, ALU.mult))
                v.scalar_tensor_tensor(out=maskb[t % 2], in0=xmag[:, 0:K0], scalar=-2 * MASK, in1=xmag[:, K0:2 * K0],
                                       op0=ALU.add, op1=ALU.add).then_inc(mask_rdy, 1)
                dve.wait_ge(mask_rdy, t + 1)

            mask(0)
            for t in range(TILES + 1):
                if t < TILES:
                    if t + 1 < TILES:
                        mask(t + 1)
                    if t >= 2:
                        dve.wait_ge(pt_mm, 4 * (t - 1))
                    elif t == 0:
                        dve.wait_ge(qb_mm, H)
                        dve.wait_ge(qb_ev, H)
                    for j in range(2):
                        dve.wait_ge(s_mm, 2 * t + j + 1)
                        heads = slice(j * H // 2, (j + 1) * H // 2)
                        s4 = bank(2 * j, 2).rearrange("p (h n) -> p h n", h=H // 2)
                        link(v.tensor_reduce(mx0[:, heads], s4, AX_X, ALU.max))
                        v.tensor_tensor(sm[t % 2][:, heads, :], s4,
                                        mx0[:, heads].unsqueeze(2).to_broadcast([P, H // 2, K0]), ALU.subtract)\
                            .then_inc(s_sub, 1)
                if t < TILES:
                    for j in range(2):
                        heads = slice(j * H // 2, (j + 1) * H // 2)
                        dve.wait_ge(s_exp, 2 * t + j + 1)
                        link(v.tensor_reduce(den0[:, heads], sm[t % 2][:, heads, :], AX_X, ALU.add))
                        v.reciprocal(rec0[t % 2][:, heads], den0[:, heads]).then_inc(s_rec, 1)
                if t >= 1:
                    dve.wait_ge(ao_mm, t)
                    v.tensor_tensor(x[:, t - 1, :], x[:, t - 1, :], bank(7)[:, 0:D], ALU.add).then_inc(x1_rdy, 1)
            dve.wait_ge(x1_rdy, TILES)
            far_ids(dve, general_vector)
            v.memset(vx[:, :, :, :, DH:VW].rearrange("p r k h n -> p (r k) (h n)"), 1.0).then_inc(vone_rdy, 1)

            def route(t):
                dve.wait_ge(rt_mm, t + 1)
                v.tensor_copy(lg, bank(7)[:, 0:E]).then_inc(lg_rdy, 1)
                dve.wait_ge(lg_rdy, t + 1)
                link(v.max(top8, lg))
                link(v.max_index(top8i[:, :], top8, lg))
                link(v.tensor_copy(idf, top8i[:, :]))
                v.tensor_scalar(ntop, top8[:, 0:2], -1.0, 80.0, ALU.mult, ALU.min).then_inc(ntop_rdy, 1)
                dve.wait_ge(pow_rdy, t + 1)
                link(v.tensor_scalar(sigd, sig[t % 2], 1.0, None, ALU.add))
                link(v.reciprocal(sigr, sigd))
                link(v.tensor_scalar(pe0, kk[:, 0:E], idf[:, 0:1], sigr[:, 0:1], ALU.is_equal, ALU.mult))
                link(v.tensor_scalar(pe1, kk[:, 0:E], idf[:, 1:2], sigr[:, 1:2], ALU.is_equal, ALU.mult))
                v.tensor_tensor(probs[t % 2], pe0, pe1, ALU.add).then_inc(p_rdy, 1)
                dve.wait_ge(p_rdy, t + 1)

            def hidden(t, c):
                n = 5 * t + c
                dve.wait_ge(silu_rdy, 9 * t + min(2 * c + 2, HB))
                if c == 0 and t >= 2:
                    dve.wait_ge(ht_mm, 3 * (t - 1))
                src = bank(n % 4)
                if c < 4:
                    for e in range(2):
                        k = 2 * c + e
                        last = v.scalar_tensor_tensor(out=hid[t % 2][:, k, :], in0=src[:, (2 * e + 1) * I:(2 * e + 2) * I],
                                                      scalar=probs[t % 2][:, k:k + 1], in1=sg[n % 2][:, e, :],
                                                      op0=ALU.mult, op1=ALU.mult)
                else:
                    last = v.tensor_tensor(hid[t % 2][:, E, :], src[:, I:2 * I], sg[n % 2][:, 0, :], ALU.mult)
                last.then_inc(hid_rdy, 1)

            def max_chunk(quad, n):
                m = CH[n % len(CH)][1]
                ca = 8 * len(CH) * quad + n
                dve.wait_ge(mx_mm, ca + 1)
                v.tensor_reduce(mxc[quad % 2][:, n:n + 1], bank(ca % 2)[:, 0:m], AX_X, ALU.max).then_inc(mx_rdy, 1)
                if n == 8 * len(CH) - 1:
                    dve.wait_ge(mx_rdy, ca + 1)
                    link(v.tensor_reduce(mx1, mxc[quad % 2].rearrange("p (u c) -> p u c", u=8), AX_X, ALU.max))
                    if quad >= 2:
                        dve.wait_ge(sh_mm, quad - 1)
                    s3 = nst[quad % 2]
                    link(v.tensor_scalar(s3[:, :, 0], mx1, -1.0, None, ALU.mult))
                    link(v.scalar_tensor_tensor(out=nrem, in0=mx1, scalar=-1.0, in1=s3[:, :, 0], op0=ALU.mult,
                                                op1=ALU.subtract))
                    link(v.tensor_copy(s3[:, :, 1], nrem))
                    v.tensor_tensor(s3[:, :, 2], nrem, s3[:, :, 1], ALU.subtract).then_inc(nst_rdy, 1)

            def first_maxima(t, third):
                for n in first_chunks(t, third):
                    max_chunk(0, n)

            dve.wait_ge(k_wr, 96)
            layer_norm(0, xn[0])
            for t in range(TILES + 2):
                if t < TILES:
                    route(t)
                    if t + 1 < TILES:
                        dve.wait_ge(hT_mm, t + 1)
                        layer_norm(t + 1, xn[0])
                    hidden(t, 0)
                    hidden(t, 1)
                if 1 <= t <= TILES:
                    dve.wait_ge(dn_mm, t)
                    v.tensor_tensor(x[:, t - 1, :], x[:, t - 1, :], bank(6)[:, 0:D], ALU.add).then_inc(x2_rdy, 1)
                    dve.wait_ge(x2_rdy, t)
                if t >= TILES:
                    first_maxima(t, 0)
                if t >= 2:
                    dve.wait_ge(q1_mm, t - 1)
                    if t >= 3:
                        dve.wait_ge(q1T_mm, t - 2)
                    link(v.scalar_tensor_tensor(out=qtok, in0=bank(7)[:, 0:D], scalar=xsc[(t - 2) % 3],
                                                in1=SWQ, op0=ALU.mult, op1=ALU.mult))
                    v.tensor_tensor(qtok, qtok, BQ, ALU.add).then_inc(q1_rdy, 1)
                if 1 <= t <= TILES:
                    layer_norm(t - 1, xn[1])
                    if t >= 3:
                        dve.wait_ge(xqT_mm, t - 2)
                    quantise(xn[1], xam, xrs, xsc[(t - 1) % 3], xmag, xq[(t - 1) % 2], xq_rdy)
                if t < TILES:
                    hidden(t, 2)
                    hidden(t, 3)
                else:
                    first_maxima(t, 1)
                if t >= 2:
                    dve.wait_ge(q1T_ev, t - 1)
                    if t >= 4:
                        dve.wait_ge(q_wr[t % 2], 48 * (t // 2 - 1))
                    v.tensor_copy(qpart[t % 2][:, 0, :], qTf[:, :]).then_inc(qs_a, 1)
                    dve.wait_ge(qs_b, t - 1)
                    v.tensor_copy(qpart[t % 2][:, 1, :], qTf[:, :]).then_inc(qs_c, 1)
                if t < TILES:
                    hidden(t, 4)
                else:
                    first_maxima(t, 2)

            def out_norm(quad):
                dve.wait_ge(ot_mm, quad + 1)
                o4 = bank(7)[:, 0:2 * P].rearrange("p (t h n) -> p t h n", t=2, h=4)
                r8 = recd.rearrange("p (t h) -> p t h", t=2)
                link(v.reciprocal(r8, o4[:, :, :, DH]))
                g = quad % 4
                dst = otok[quad // 4 % 2][:, :, g * 64:(g + 1) * 64]
                v.tensor_tensor(dst.rearrange("p t (h n) -> p t h n", h=4), o4[:, :, :, 0:DH],
                                r8.unsqueeze(3).to_broadcast([P, 2, 4, DH]), ALU.mult).then_inc(o_rdy, 1)

            def tail(b, part, between):
                tiles = range(2)
                o2, x2 = otok[b % 2], x[:, 2 * b:2 * b + 2, :]
                both = lambda row: row.unsqueeze(1).to_broadcast([P, 2, D])
                if part == "bias":
                    dve.wait_ge(o_rdy, 4 * (b + 1))
                    link(v.tensor_tensor(o2, o2, both(BV), ALU.add))
                    between()
                    link(v.tensor_reduce(oam, o2, AX_X, ALU.max, apply_absolute_value=True))
                elif part == "scale":
                    link(v.tensor_scalar(osc[b % 2], oam, float(np.float32(1) / np.float32(127)), 1e-8, ALU.mult,
                                         ALU.max))
                    link(v.reciprocal(ors, osc[b % 2]))
                    between()
                    for i in tiles:
                        link(v.tensor_scalar(o2[:, i, :], o2[:, i, :], ors[:, i:i + 1], 127.0, ALU.mult, ALU.min))
                elif part == "round":
                    link(v.tensor_scalar(o2, o2, -127.0, MAGIC, ALU.max, ALU.add))
                    between()
                    v.tensor_scalar(xq2, o2, -MAGIC, None, ALU.add).then_inc(oi_rdy, 1)
                elif part == "project":
                    dve.wait_ge(wp_mm, b + 1)
                    for i in tiles:
                        last = v.scalar_tensor_tensor(out=mag2[:, i, :], in0=bank(7)[:, i * D:(i + 1) * D],
                                                      scalar=osc[b % 2][:, i:i + 1], in1=SWP, op0=ALU.mult,
                                                      op1=ALU.mult)
                    last.then_inc(wp_ev, 1)
                elif part == "residual":
                    dve.wait_ge(wp_ev, b + 1)
                    link(v.tensor_tensor(mag2, mag2, both(BP), ALU.add))
                    between()
                    v.tensor_tensor(x2, x2, mag2, ALU.add).then_inc(x3_rdy, 1)
                elif part == "moments":
                    dve.wait_ge(x3_rdy, b + 1)
                    for i in tiles:
                        last = v.bn_stats(stats3[:, i, :], x2[:, i, :])
                    link(last)
                elif part == "variance":
                    for i in tiles:
                        last = v.bn_aggr(mv3[:, i, :], stats3[:, i, :])
                    link(last)
                    v.tensor_scalar(mv3[:, :, 1], mv3[:, :, 1], LN_EPS, None, ALU.add).then_inc(n3_eps, 1)
                elif part == "norm":
                    dve.wait_ge(n3_rstd, b + 1)
                    for i in tiles:
                        last = v.tensor_scalar(xn[i], x2[:, i, :], mv3[:, i, 0:1], rstd3[:, i:i + 1], ALU.subtract,
                                               ALU.mult)
                    last.then_inc(n3_rdy, 1)
                elif part == "up":
                    dve.wait_ge(up_mm, b + 1)
                    v.tensor_scalar(upT, bank(7).rearrange("p (c t) -> p c t", c=FC), 0.0, None, ALU.max)\
                        .then_inc(up_rdy, 1)
                elif part == "gate":
                    dve.wait_ge(rt_mm, TILES + b + 1)
                    v.tensor_copy(lg1, bank(7)[:, 0:2 * E].rearrange("p (t e) -> p t e", t=2)).then_inc(lg1_rdy, 1)
                    dve.wait_ge(lg1_rdy, b + 1)
                    for i in tiles:
                        last = v.max(top1[:, i, :], lg1[:, i, :])
                    link(last)
                    v.tensor_tensor(dtop, top1[:, :, 1], top1[:, :, 0], ALU.subtract).then_inc(dtop_rdy, 1)
                elif part == "down":
                    dve.wait_ge(d_mm, b + 1)
                    v.tensor_tensor(mag2, x2, bank(7).rearrange("p (t d) -> p t d", t=2), ALU.add)\
                        .then_inc(d_rdy, 1)
                    between()
                    dve.wait_ge(etop_rdy, b + 1)
                    link(v.tensor_scalar(rden, etop, 1.0, None, ALU.add))
                    link(v.reciprocal(rden, rden))
                    link(v.tensor_tensor(rsum, etop, rden, ALU.mult))
                    link(v.tensor_tensor(rsum, rsum, rden, ALU.add))
                elif part == "expert":
                    dve.wait_ge(y_mm, b + 1)
                    dve.wait_ge(d_rdy, b + 1)
                    for i in tiles:
                        if b >= 1:
                            dve.wait_ge(stored[i], 16 * b)
                        v.scalar_tensor_tensor(out=y[i][:, :], in0=bank(7)[:, i * D:(i + 1) * D],
                                               scalar=rsum[:, i:i + 1], in1=mag2[:, i, :], op0=ALU.mult,
                                               op1=ALU.add).then_inc(y_rdy, 1)

            dve.wait_ge(x2_rdy, TILES)
            v.memset(bank(6), 0.0).then_inc(po_zero, 1)
            for quad in range(QUADS + 2):
                for kt in range(KT):
                    jobs = BESIDE.get((quad, kt), [])
                    maxima = [j for j in jobs if j[0] == "max"]

                    def next_max():
                        if maxima:
                            max_chunk(*maxima.pop(0)[1:])

                    next_max()
                    while maxima and not any(j[-1] in ALONE for j in jobs):
                        next_max()
                    for what, *a in jobs:
                        if what == "out":
                            out_norm(*a)
                        elif what == "tail":
                            tail(*a, next_max)
                    while maxima:
                        next_max()


def kernel(**inputs):
    import concourse.bacc as _bacc
    from concourse.bass_utils import run_bass_kernel_spmd as _run

    def chunks(w):
        return w.reshape(w.shape[0] // P, P, -1).transpose(1, 0, 2)

    a = {k: np.asarray(v) for k, v in inputs.items()}
    ctx = a["ctx_2048"]
    ctxT = ctx.transpose(0, 2, 1).reshape(B, FC, P, KEYS).transpose(0, 2, 1, 3)
    ctx0 = ctx[:, :K0].transpose(2, 0, 1).reshape(FC, P, B * K0).transpose(1, 0, 2)
    half = R // 2
    swap = np.r_[half:R, 0:half]
    wkr = a["L0_xattn_W_kr"]
    wqr = a["L0_xattn_W_qr"].reshape(QC, H, R)
    inv = (1.0 / 10000.0 ** (np.arange(half, dtype=np.float32) / np.float32(half))).astype(np.float32)
    ang = (np.arange(KEYS, dtype=np.float32)[:, None] * inv).T
    cos, sin = np.cos(ang).astype(np.float32), np.sin(ang).astype(np.float32)
    keyrope = np.concatenate([np.concatenate([cos] * 4), np.concatenate([-sin, sin] * 2)], 1)
    cos, sin = cos[:, 0:LQ], sin[:, 0:LQ]
    cos2, sin2, one = np.concatenate([cos, cos]), np.concatenate([-sin, sin]), np.ones((KVC, LQ), np.float32)
    tabs = np.stack([np.concatenate(z) for z in ((cos2, one), (one, cos2), (cos2, cos2), (sin2, sin2))], 1)
    gu = a["L0_ffn_gate_up_w"].transpose(1, 0, 2).reshape(D, E * 2 * I)
    rows = np.stack([a["L1_xattn_bq"], a["L1_xattn_bkv"][D:], a["L1_xattn_bp"]])
    vals = {
        "x": a["x"].reshape(TOK, D), "ctx": ctxT, "ctx0": ctx0,
        "seg": a["itok_BxS_0_1023"].reshape(TILES, P).T,
        "ident": np.eye(P, dtype=np.float32), "tabs": tabs,
        "kk": np.broadcast_to(np.arange(P, dtype=np.float32), (P, P)),
        "ones": np.ones((3, 2, HALF, KEYS), mybir.dt.np(BF16)),
        "wkvc": chunks(np.concatenate([a["L0_xattn_W_kvc"]] * 2, 1)),
        "wkr": np.concatenate([wkr, wkr], 1), "wkrs": np.concatenate([wkr[:, swap]] * 2, 1),
        "wdq": chunks(a["L0_xattn_W_dq"]),
        "wuq": a["L0_xattn_W_uq"].reshape(QC, H, HD).transpose(2, 1, 0),
        "wuk": a["L0_xattn_W_uk"].reshape(KVC, H, HD).transpose(2, 1, 0),
        "wqr": wqr, "wqrs": wqr[:, :, swap].reshape(QC, H // 2, 2 * R),
        "wuv": a["L0_xattn_W_uv"].reshape(KVC, H, HD).transpose(2, 1, 0),
        "wo": a["L0_xattn_W_o"].reshape(H, HD, D).transpose(1, 0, 2),
        "router": chunks(a["L0_ffn_router_w"]), "gu": chunks(gu),
        "sgu": chunks(np.concatenate([a["L0_ffn_shared_gate_w"], a["L0_ffn_shared_up_w"]], 1)),
        "down": a["L0_ffn_down_w"].transpose(1, 0, 2), "sdown": a["L0_ffn_shared_down_w"],
        "wq": chunks(a["L1_xattn_wq"]), "wp": chunks(a["L1_xattn_wp"]), "wkv": chunks(a["L1_xattn_wkv"].T),
        "bk": a["L1_xattn_bkv"][:D].reshape(FC, P).T,
        "rows": np.broadcast_to(rows, (P, 3, D)),
        "wup": chunks(a["L1_ffn_W_up"].T), "wdn": chunks(a["L1_ffn_W_down"].T), "wex": chunks(a["L1_ffn_W_expert"]),
        "wg": chunks(a["L1_ffn_W_gate"].T),
        "segrow": a["itok_BxS_0_1023"].reshape(1, TOK), "keyrope": keyrope,
        "keyid": np.broadcast_to(np.arange(KEYS, dtype=np.float32), (P, KEYS)),
    }
    nc = _bacc.Bacc("TRN2", target_bir_lowering=False, num_devices=1)
    arrays, args = {}, []
    for name, val in vals.items():
        val = np.ascontiguousarray(val)
        arrays[f"in_{name}_dram"] = val
        args.append(nc.dram_tensor(f"in_{name}_dram", val.shape, mybir.dt.from_np(val.dtype),
                                   kind="ExternalInput").ap())
    args.append(nc.dram_tensor("out_0_dram", (TOK, D), F32, kind="ExternalOutput").ap())
    program(nc, *args)
    r = _run(nc, [arrays], core_ids=[0])
    return r.results[0]["out_0_dram"].reshape(B, LQ, D)
```

```python
from contextlib import ExitStack

import numpy as np

import concourse.bass as bass
from concourse import mybir

F32 = mybir.dt.float32
BF16 = mybir.dt.bfloat16
I32 = mybir.dt.int32
U32 = mybir.dt.uint32
ACT = mybir.ActivationFunctionType
ALU = mybir.AluOpType
AX_X = mybir.AxisListType.X

P = 128
B, LQ, D = 4, 256, 256
KEYS = 1601
TOK = B * LQ
TILES = TOK // P
FC = D // P
H = 16
HD, KVC, QC, R = 128, 64, 96, 64
LOOKBACK = 8
K0 = 128
NEG = -1e30
MASK = float(2.0 ** 99)
SCALE0 = float(1.0 / np.sqrt(HD + R).astype(np.float32))
E, I = 8, 128
HB = E + 1
DH = D // H
SCALE1 = float(1.0 / np.sqrt(DH))
KT = (KEYS + P - 1) // P
KLAST = KEYS - (KT - 1) * P
HALF = H // 2
STAGES = B * 2
QUADS = STAGES * 2
STEPS = QUADS * KT
STACK_Q = (0, 0, 1, 0, 2, 1)
STACK_K = (0, 1, 0, 2, 0, 1)
SROWS = len(STACK_Q) * DH
VW = DH + 1
CH = [(0, 401), (401, 400), (801, 400), (1201, 400)]
MAGIC = float(1.5 * 2 ** 23)
LN_EPS = 1e-5


NMAX = 8 * len(CH)
KSTEPS = ((7, 10, 12, 13), (35, 42, 43, 44))
VSTEPS = (0, 3, 19, 27, 29, 33, 38)
TAIL = ((4, "scale"), (6, "round"), (8, "turn_o"), (9, "project"), (11, "residual"),
        (12, "moments"), (13, "variance"), (14, "norm"), (16, "turn_x"), (17, "up"),
        (18, "gate"), (20, "route"), (22, "down"), (23, "expert"))
ROUND_AFTER = (5, 11, 17, 23)
ALONE = ("bias", "scale", "round", "residual", "moments", "variance", "norm")


def schedule():
    beside = {}

    def put(step, *job):
        beside.setdefault((step // KT, step % KT), []).append(job)

    for quad in range(1, QUADS):
        put((quad - 1) * KT + 11, "shift", quad)
    for quad in range(QUADS):
        put((quad + 1) * KT + 2, "out", quad)
        put((quad + 1) * KT + 3, "bias", quad)
    for b in range(B):
        start = b * 4 * KT
        if b + 1 < B:
            for s, at in ((2 * b + 2, KSTEPS[0]), (2 * b + 3, KSTEPS[1])):
                for c in range(len(CH)):
                    put(start + at[c], "k", s, c)
            for j, at in enumerate(VSTEPS if b >= 1 else ()):
                put(start + at, "v", b + 1, j)
        for at, part in TAIL:
            put(start + 4 * KT + at, "tail", b, part)
    for quad in range(1, QUADS):
        first = (quad - 1) * KT - 2
        window = range(max(0, first), first + KT)
        work = [chunk_room(beside.get((i // KT, i % KT), [])) for i in window]
        done, placed = 0, 0
        for i, w in zip(window, work):
            done += w
            until = round(NMAX * done / sum(work))
            for n in range(placed, until):
                put(i, "max", quad, n)
            placed = until
    return beside


def kind(job):
    return job[-1] if job[0] == "tail" else job[0]


def tail_bank(b, part):
    return 7 if b + 1 < B else {"turn_x": 5, "up": 0, "gate": 1, "down": 2, "expert": 3}.get(part, 7)


def step_work(jobs):
    cost = {"k": 8 * 401, "v": 16 * D, "out": 2 * 4 * P, "shift": 8 * P, "up": 16 * D, "down": 16 * D,
            "expert": 16 * D, "turn_x": 4 * 4 * P, "turn_o": 4 * P, "project": 4 * D, "gate": 4 * 4 * E}
    return 4 * LQ + 4 * LQ + sum(cost.get(kind(j), 0) for j in jobs)


def chunk_room(jobs):
    busy = {"out": 2 * 2 * D, "bias": 2 * 2 * D, "scale": 3 * 2 * D, "round": 4 * 2 * D, "project": 2 * 2 * D,
            "residual": 2 * 2 * D, "moments": 2 * 2 * D, "variance": 2 * D, "norm": 2 * 2 * D, "up": 2 * 2 * D,
            "gate": 2 * 2 * D, "down": 3 * 2 * D, "expert": 2 * 2 * D}
    return max(0, step_work(jobs) + 1969 - 0.6 * sum(busy.get(kind(j), 0) for j in jobs))


def first_chunks(t, third):
    slot = 3 * (t - TILES) + third
    return range(slot * NMAX // 6, (slot + 1) * NMAX // 6)


BESIDE = schedule()


def program(nc, x_in, ctx_in, ctx0_in, seg_in, ident_in, tabs_in, kk_in, ones_in, wkvc_in, wkr_in, wkrs_in,
            wdq_in, wuq_in, wuk_in, wqr_in, wqrs_in, wuv_in, wo_in, router_in, gu_in, sgu_in, down_in, sdown_in,
            wq_in, wp_in, wkv_in, bk_in, rows_in, wup_in, wdn_in, wex_in, wg_in, segrow_in, keyrope_in, keyid_in,
            out):
    with ExitStack() as ctx:
        def sb(name, cols, dt=F32):
            return ctx.enter_context(nc.sbuf_tensor(name, [P, cols], dt))

        def sem(name):
            return ctx.enter_context(nc.semaphore(name))

        ps = ctx.enter_context(nc.psum_tensor("ps", [P, 8 * 512], F32))

        def bank(i, n=1):
            return ps[:, i * 512:(i + n) * 512]

        r1 = sb("r1", 13 * TOK)
        r2 = sb("r2", H * TOK // 2)
        r3 = sb("r3", 7168)
        r4 = sb("r4", FC * KEYS)
        r5 = sb("r5", 4096)
        r6 = sb("r6", 6912)
        x = sb("x", TILES * D)[:, :].rearrange("p (t d) -> p t d", t=TILES)
        ident = sb("ident", P)
        identb = sb("identb", P, BF16)
        wkvT = sb("wkvT", FC * 2 * D)[:, :].rearrange("p (c n) -> p c n", c=FC)
        bk = sb("bk", FC)
        rows = sb("rows", 5 * D)[:, :].rearrange("p (r d) -> p r d", r=5)
        BQ, BV, BP, SWQ, SWP = (rows[:, i, :] for i in range(5))
        wintT = sb("wintT", 2 * FC * D, BF16)[:, :].rearrange("p (m c n) -> p m c n", m=2, c=FC)
        router = sb("router", FC * E)[:, :].rearrange("p (c n) -> p c n", c=FC)
        kk = sb("kk", P)
        segi = sb("segi", TILES, I32)
        small = sb("small", 512)
        def qf(h):
            return r1[:, h * TOK:(h + 1) * TOK] if h < 13 else r6[:, 3584 + (h - 13) * TOK:3584 + (h - 12) * TOK]
        wuq = r2[:, 0:1536].rearrange("p (h n) -> p h n", h=H)
        wuk = r2[:, 1536:2560].rearrange("p (h n) -> p h n", h=H)
        wuv = r2[:, 2560:3584].rearrange("p (h n) -> p h n", h=H)
        wo = r2[:, 3584:7680].rearrange("p (h n) -> p h n", h=H)
        weff = r3[0:QC, 0:2048].rearrange("p (h n) -> p h n", h=H)
        wqrs = r3[0:QC, 2048:3072].rearrange("p (h n) -> p h n", h=H // 2)
        wuvo = r3[:, 3072:5120].rearrange("p (h n) -> p h n", h=H // 2)
        pT = r3[:, 5120:7168].rearrange("p (h n) -> p h n", h=H)
        ctx0 = r3[:, 5120:6144].rearrange("p (c n) -> p c n", c=FC)
        xnT = r5[:, 0:2048].rearrange("p (c t) -> p c t", c=FC)
        qcT = r5[0:QC, 2048:3072]
        tabs = r5[:, 3072:4096].rearrange("p (k t) -> p k t", k=4)
        sm = [r5[:, i * 2048:(i + 1) * 2048].rearrange("p (h n) -> p h n", h=H) for i in range(2)]
        kf0 = [r6[:, i * 512:(i + 1) * 512] for i in range(2)]
        kvtok = r6[:, 1024:1280].rearrange("p (b n) -> p b n", b=B)
        ropet = [r6[:, 1280 + i * 512:1792 + i * 512] for i in range(2)]
        olat = r6[:, 2304:3328].rearrange("p (h n) -> p h n", h=H // 2)
        maskb = [r6[:, 3328 + 64 * i:3392 + 64 * i].bitcast(BF16) for i in range(2)]
        wkvc = r4[:, 0:256].rearrange("p (c n) -> p c n", c=FC)
        wkr = r4[0:KVC, 256:384]
        wkrs = r4[0:KVC, 384:512]
        wdq = r4[:, 512:704].rearrange("p (c n) -> p c n", c=FC)
        wnat = r4[:, 1024:2048].rearrange("p (m c n) -> p m c n", m=2, c=FC)
        wmag = r4[:, 2048:3072].rearrange("p (m c n) -> p m c n", m=2, c=FC)
        wint = r4[:, 704:960].bitcast(BF16).rearrange("p (c n) -> p c n", c=FC)
        wint2 = sb("wint2", FC * D, BF16)[:, :].rearrange("p (c n) -> p c n", c=FC)
        zeros = r3[:, 6144:6400].bitcast(BF16)
        xn2 = sb("xn", 2 * D)[:, :].rearrange("p (t d) -> p t d", t=2)
        xn = [xn2[:, i, :] for i in range(2)]
        hT2 = sb("hT", 2 * D)[:, :].rearrange("p (t c n) -> p t c n", t=2, c=FC)
        hT = [hT2[:, i] for i in range(2)]
        gu = r6[:, 0:4096].rearrange("p (c n) -> p c n", c=FC)
        sgu = r6[:, 4096:4608].rearrange("p (c n) -> p c n", c=FC)
        down = r6[:, 4608:6912].rearrange("p (e n) -> p e n", e=HB)
        hid = [r5[:, i * 1152:(i + 1) * 1152].rearrange("p (e n) -> p e n", e=HB) for i in range(2)]
        hidT = r5[:, 2304:3456].rearrange("p (e n) -> p e n", e=HB)
        sg = [r5[:, 3456 + 256 * i:3712 + 256 * i].rearrange("p (e n) -> p e n", e=2) for i in range(2)]
        xq2 = sb("xq", 2 * D, BF16)[:, :].rearrange("p (t d) -> p t d", t=2)
        xq = [xq2[:, i, :] for i in range(2)]
        xqT2 = sb("xqT", 2 * D, BF16)[:, :].rearrange("p (t c n) -> p t c n", t=2, c=FC)
        xqT = xqT2[:, 0]
        mag2 = sb("mag", 2 * D)[:, :].rearrange("p (t d) -> p t d", t=2)
        xmag, qtok = mag2[:, 0, :], mag2[:, 1, :]
        qTf = sb("qTf", D)
        qpart = [sb(f"qpart{i}", 3 * D, BF16)[:, :].rearrange("p (j n) -> p j n", j=3) for i in range(2)]
        kst = r1[:, 0:HALF * KEYS].bitcast(BF16).rearrange("p (r h k) -> p r h k", r=2, h=HALF)
        qst = r2[:, :].bitcast(BF16).rearrange("p (h t) -> p h t", h=H)
        vx = r3[:, 0:2 * KT * H * VW].rearrange("p (r k h n) -> p r k h n", r=2, k=KT, h=H)
        ctxT = r4[:, :].rearrange("p (c k) -> p c k", c=FC)
        key_at = [r2[:, 0:4096], r2[:, 4096:8192]] + [r5[:, :]] * (STAGES - 2)
        kf = [k[:, 0:KEYS] for k in key_at]
        kpart = [[k[:, 1602 + 802 * j:2404 + 802 * j].bitcast(BF16)[:, 0:KEYS] for j in range(3)] for k in key_at]
        pr = [r6[:, i * 1024:(i + 1) * 1024] for i in range(3)]
        wup = r6[:, 3072:3584].rearrange("p (c n) -> p c n", c=FC)
        wdn = r6[:, 3584:4096].rearrange("p (c n) -> p c n", c=FC)
        wex = r6[:, 4096:4608].rearrange("p (c n) -> p c n", c=FC)
        wg = r6[:, 4608:4624].rearrange("p (c n) -> p c n", c=FC)
        poS = [r6[:, 4624 + 256 * i:4880 + 256 * i] for i in range(2)]
        otok = [r6[:, 5136 + 512 * i:5648 + 512 * i].rearrange("p (t d) -> p t d", t=2) for i in range(2)]
        upT = r6[:, 6160:6672].rearrange("p (c t) -> p c t", c=FC)
        y = [sb(f"y{i}", D) for i in range(2)]
        nst = [sb(f"nst{i}", 24, BF16)[:, :].rearrange("p (u j) -> p u j", u=8) for i in range(2)]

        cols = iter(range(0, 512))

        def col(n=1):
            a = next(cols)
            for _ in range(n - 1):
                next(cols)
            return small[:, a:a + n]

        segf, seglo = col(TILES), col(TILES)
        stats, mv, rstd = col(6), [col(2), col(2)], [col(1), col(1)]
        neghalf, eul = col(1), col(1)
        mx0, den0, rec0 = col(H), col(H), [col(H), col(H)]
        wam, wsc, wrs = col(4), col(4), col(4)
        lg, top8, idf, sig = col(E), col(E), col(E), [col(2), col(2)]
        sigd, sigr, ntop = col(2), col(2), col(2)
        pe0, pe1 = col(E), col(E)
        probs = [col(E), col(E)]
        top8i = sb("top8i", 8, U32)
        xam, xrs, xsc = col(1), col(1), [col(1), col(1), col(1)]
        mxc, mx1, nrem = [col(32), col(32)], col(8), col(8)
        recd = col(8)
        qam = col(8).rearrange("p (t g) -> p t g", t=2)
        oam, ors, osc = col(2), col(2), [col(2), col(2)]
        lg1, top1 = (col(2 * E).rearrange("p (t e) -> p t e", t=2) for _ in range(2))
        dtop, etop, rden, rsum = col(2), col(2), col(2), col(2)
        stats3 = col(12).rearrange("p (t n) -> p t n", t=2)
        mv3 = col(4).rearrange("p (t n) -> p t n", t=2)
        rstd3 = col(2)

        kscr = nc.dram_tensor("kscr", (2, 3, P, KEYS), BF16, kind="Internal").ap()
        qscr = nc.dram_tensor("qscr", (3, D, TOK), BF16, kind="Internal").ap()

        ld_const, ld_x, ld_key, ld_q, ld_vo, ld_w1, ld_ctx, ld_ffn, ld_ffn1, ld_ones = (
            sem(n) for n in ("ld_const", "ld_x", "ld_key", "ld_q", "ld_vo", "ld_w1", "ld_ctx", "ld_ffn", "ld_ffn1",
                             "ld_ones"))
        zero_rdy = sem("zero_rdy")
        dve_chain = sem("dve_chain")
        (m_mm, m_ev, kv_mm, kv_ev, rope_mm, rope_done, kvt_mm, kvt_ev, eps_rdy, rstd_rdy, xn_rdy, xnT_mm, xnT_ev,
         qc_mm, qc_ev, qa_mm, qa_ev, qb_mm, qb_ev, q_rdy, mask_rdy, s_mm, s_sub, s_exp, s_rec, s_norm, pt_mm, pt_ev,
         pv_mm, pv_ev, ao_mm, x1_rdy) = (sem(n) for n in (
             "m_mm", "m_ev", "kv_mm", "kv_ev", "rope_mm", "rope_done", "kvt_mm", "kvt_ev", "eps_rdy", "rstd_rdy",
             "xn_rdy", "xnT_mm", "xnT_ev", "qc_mm", "qc_ev", "qa_mm", "qa_ev", "qb_mm", "qb_ev", "q_rdy", "mask_rdy",
             "s_mm", "s_sub", "s_exp", "s_rec", "s_norm", "pt_mm", "pt_ev", "pv_mm", "pv_ev", "ao_mm", "x1_rdy"))
        (hT_mm, hT_ev, rt_mm, lg_rdy, ntop_rdy, pow_rdy, p_rdy, gu_mm, silu_rdy, hid_rdy, ht_mm, ht_ev, dn_mm,
         x2_rdy) = (sem(n) for n in ("hT_mm", "hT_ev", "rt_mm", "lg_rdy", "ntop_rdy", "pow_rdy", "p_rdy", "gu_mm",
                                     "silu_rdy", "hid_rdy", "ht_mm", "ht_ev", "dn_mm", "x2_rdy"))
        (wint_rdy, wt_mm, wt_ev, sw_mm, sw_ev, xq_rdy, xqT_mm, xqT_ev, q1_mm, q1_rdy, q1T_mm, q1T_ev, qs_a, qs_b,
         f_rdy, qpart_rdy) = (sem(n) for n in (
             "wint_rdy", "wt_mm", "wt_ev", "sw_mm", "sw_ev", "xq_rdy", "xqT_mm", "xqT_ev", "q1_mm", "q1_rdy",
             "q1T_mm", "q1T_ev", "qs_a", "qs_b", "f_rdy", "qpart_rdy"))
        (k_mm, k_ev, ks_a, ks_b, kpart_rdy, k_wr, v_mm, v_ev, vone_rdy, mx_mm, mx_rdy, nst_rdy, sh_mm,
         sh_rdy, sc_mm, ex_rdy, av_mm, po_rdy, po_zero, ot_mm, o_rdy, oi_rdy, oiT_mm, oiT_ev, wp_mm, x3_rdy, x3T_mm,
         x3T_ev, up_mm, up_rdy, dtop_rdy, etop_rdy, y_mm, y_rdy) = (sem(n) for n in (
             "k_mm", "k_ev", "ks_a", "ks_b", "kpart_rdy", "k_wr", "v_mm", "v_ev", "vone_rdy",
             "mx_mm", "mx_rdy", "nst_rdy", "sh_mm", "sh_rdy", "sc_mm", "ex_rdy", "av_mm", "po_rdy", "po_zero",
             "ot_mm", "o_rdy", "oi_rdy", "oiT_mm", "oiT_ev", "wp_mm", "x3_rdy", "x3T_mm", "x3T_ev", "up_mm",
             "up_rdy", "dtop_rdy", "etop_rdy", "y_mm", "y_rdy"))
        qam_rdy, n3_eps, n3_rstd, n3_rdy, lg1_rdy, wp_ev, d_mm, d_rdy = (sem(n) for n in (
            "qam_rdy", "n3_eps", "n3_rstd", "n3_rdy", "lg1_rdy", "wp_ev", "d_mm", "d_rdy"))
        q_wr = [sem(f"q_wr{i}") for i in range(2)]
        k_stk = [sem(f"k_stk{i}") for i in range(2)]
        stored = [sem(f"stored{i}") for i in range(2)]
        q_stk = [sem(f"q_stk{b}") for b in range(B)]

        (ld_seg, far_rdy, g_load, g_ctx, g_kv_mm, g_kv_ev, g_rope_mm, g_rope_ev, g_tok_mm, g_tok_ev, g_s_mm, g_max,
         g_exp, g_norm, g_t_mm, g_t_ev, g_pv_mm, g_pv_ev, g_o_mm, g_x, g_q_ev, g_chain) = (sem(n) for n in (
             "ld_seg", "far_rdy", "g_load", "g_ctx", "g_kv_mm", "g_kv_ev", "g_rope_mm", "g_rope_ev", "g_tok_mm",
             "g_tok_ev", "g_s_mm", "g_max", "g_exp", "g_norm", "g_t_mm", "g_t_ev", "g_pv_mm", "g_pv_ev", "g_o_mm",
             "g_x", "g_q_ev", "g_chain"))
        g_kf = [r2[:, i * KEYS:(i + 1) * KEYS] for i in range(2)]
        g_cos, g_sin = (r2[:, i * KEYS:(i + 1) * KEYS] for i in (2, 3))
        g_tok = r2[:, 4 * KEYS:4 * KEYS + KT * KVC].rearrange("p (k n) -> p k n", k=KT)
        g_wkvc = r2[:, 7236:7492].rearrange("p (c n) -> p c n", c=FC)
        g_wkr, g_wkrs = r2[0:KVC, 7492:7620], r2[0:KVC, 7620:7748]
        g_bias = r3[:, 0:KEYS]
        g_q = [r3[:, 1664 + i * P:1664 + (i + 1) * P] for i in range(2)]
        g_tmp = r5[:, 0:1024].rearrange("p (i n) -> p i n", i=2)
        g_w = r5[:, 0:KEYS]
        g_wT = r5[:, 1664:1664 + KT * P].rearrange("p (k n) -> p k n", k=KT)
        g_id = r6[:, 0:KEYS]
        g_mx, g_sum, g_rec, far = col(1), col(1), col(1), col(1)
        segend = [col(1), col(1)]
        segrow = r6[0:1, 3584:3584 + TOK].bitcast(I32)
        segrowf = r6[0:1, 4608:4608 + TOK]
        fari = sb("fari", 1, I32)

        block = ctx.enter_context(nc.Block())

        def far_ids(eng, body):
            eng.wait_ge(far_rdy, 1)
            found = eng.value_load(fari[0:1, 0:1], min_val=0, max_val=1)
            with eng.If(found != 0):
                body()

        def key_tile(i):
            return P if i < KT - 1 else KLAST

        def general_sync():
            sp = nc.sync
            sp.wait_ge(x1_rdy, TILES)
            sp.wait_ge(s_norm, 2 * TILES)
            for dst, src in ((x, x_in.rearrange("(t p) d -> p t d", p=P)), (r2[:, 2 * KEYS:4 * KEYS], keyrope_in),
                             (g_id, keyid_in), (g_wkvc, wkvc_in), (g_wkr, wkr_in), (g_wkrs, wkrs_in)):
                sp.dma_start(dst, src).then_inc(g_load, 16)
            sp.wait_ge(ld_ctx, 16)
            for b in range(B):
                sp.dma_start(ctxT, ctx_in[b]).then_inc(g_ctx, 16)
                sp.wait_ge(g_tok_mm, b + 1)
            sp.dma_start(ctxT, ctx_in[0]).then_inc(g_ctx, 16)
            sp.wait_ge(g_x, TILES)
            sp.wait_ge(g_ctx, 16 * (B + 1))

        def general_tensor():
            pe, mm = nc.tensor, nc.tensor.matmul
            pe.wait_ge(g_load, 96)
            with pe.Fori(0, B) as b:
                pe.wait_ge(g_ctx, b * 16 + 16)
                for c, (a, n) in enumerate(CH):
                    for k in range(FC):
                        last = mm(bank(0)[:, 0:n], g_wkvc[:, k, :], ctxT[:, k, a:a + n], start=k == 0,
                                  stop=k == FC - 1)
                    last.then_inc(g_kv_mm, 1)
                    pe.wait_ge(g_kv_ev, b * 4 + c + 1)
                    if c >= 1:
                        pe.wait_ge(g_rope_ev, b * 4 + c)
                    mm(bank(1)[:, 0:n], g_wkr, g_kf[1][0:KVC, a:a + n], start=True, stop=True)
                    mm(bank(2)[:, 0:n], g_wkrs, g_kf[1][0:KVC, a:a + n], start=True, stop=True)\
                        .then_inc(g_rope_mm, 1)
                for i in range(KT):
                    n = key_tile(i)
                    for k in range(FC):
                        last = mm(bank(4 + i // 8)[0:n, (i % 8) * KVC:(i % 8 + 1) * KVC], ctxT[:, k, i * P:i * P + n],
                                  g_wkvc[:, k, 0:KVC], start=k == 0, stop=k == FC - 1)
                last.then_inc(g_tok_mm, 1)
                pe.wait_ge(g_rope_ev, b * 4 + 4)
                pe.wait_ge(g_tok_ev, b + 1)
                for t in range(2):
                    for h in range(H):
                        n0 = t * H + h
                        if h >= 1:
                            pe.wait_ge(g_pv_ev, b * 32 + n0)
                        pe.wait_ge(g_q_ev, b * 32 + n0 + 1)
                        for c, (a, n) in enumerate(CH):
                            last = mm(bank(c)[:, 0:n], g_q[n0 % 2], g_kf[h % 2][:, a:a + n],
                                      start=True, stop=True)
                        last.then_inc(g_s_mm, 1)
                        pe.wait_ge(g_norm, b * 32 + n0 + 1)
                        for i in range(KT):
                            n = key_tile(i)
                            last = nc.tensor.transpose(bank(4 + i // 4)[0:n, (i % 4) * P:(i % 4 + 1) * P],
                                                       g_w[:, i * P:i * P + n], ident[:, :])
                        last.then_inc(g_t_mm, 1)
                        pe.wait_ge(g_t_ev, b * 32 + n0 + 1)
                        lo = (h % 2) * KVC
                        for i in range(KT):
                            n = key_tile(i)
                            last = mm(bank(0)[lo:lo + KVC, 0:P], g_tok[0:n, i, :], g_wT[0:n, i, :], start=i == 0,
                                      stop=i == KT - 1)
                        last.then_inc(g_pv_mm, 1)
                    pe.wait_ge(g_pv_ev, b * 32 + t * H + H)
                    for p2 in range(H // 2):
                        last = mm(bank(1)[:, 0:D], olat[:, p2, :], wuvo[:, p2, :], start=p2 == 0, stop=p2 == H // 2 - 1)
                    last.then_inc(g_o_mm, 1)
                    pe.wait_ge(g_x, b * 2 + t + 1)
            pe.wait_ge(g_x, TILES)
            pe.wait_ge(g_ctx, 16 * (B + 1))

        def general_scalar():
            act, fn = nc.scalar, nc.scalar.activation
            act.wait_ge(x1_rdy, TILES)
            with act.Fori(0, B) as b:
                for c, (a, n) in enumerate(CH):
                    act.wait_ge(g_kv_mm, b * 4 + c + 1)
                    fn(g_kf[1][0:KVC, a:a + n], bank(0)[0:KVC, 0:n], ACT.Copy)
                    fn(g_kf[0][KVC:P, a:a + n], bank(0)[KVC:P, 0:n], ACT.Copy).then_inc(g_kv_ev, 1)
                act.wait_ge(g_tok_mm, b + 1)
                fn(g_tok[:, 0:8, :], bank(4).rearrange("p (k n) -> p k n", k=8), ACT.Copy)
                fn(g_tok[:, 8:KT - 1, :], bank(5)[:, 0:4 * KVC].rearrange("p (k n) -> p k n", k=4), ACT.Copy)
                fn(g_tok[0:KLAST, KT - 1, :], bank(5)[0:KLAST, 4 * KVC:5 * KVC], ACT.Copy).then_inc(g_tok_ev, 1)
                def query(n0):
                    fn(g_q[n0 % 2], qf(n0 % H)[:, bass.ds(b * LQ + n0 // H * P, P)], ACT.Copy).then_inc(g_q_ev, 1)

                query(0)
                for n0 in range(2 * H):
                    if n0 + 1 < 2 * H:
                        query(n0 + 1)
                    act.wait_ge(g_max, b * 32 + n0 + 1)
                    fn(g_w, g_w, ACT.Exp, scale=SCALE0).then_inc(g_exp, 1)
                    act.wait_ge(g_t_mm, b * 32 + n0 + 1)
                    fn(g_wT[:, 0:12, :], bank(4, 3).rearrange("p (k n) -> p k n", k=12), ACT.Copy)
                    fn(g_wT[0:KLAST, 12, :], bank(7)[0:KLAST, 0:P], ACT.Copy).then_inc(g_t_ev, 1)

        def general_vector():
            dve, v = nc.vector, nc.vector
            dve.wait_ge(g_load, 96)
            links = [0]
            per_batch = 2 * len(CH) + 2 * (5 + 4 * H)

            with dve.Fori(0, B) as b:
                def link(ins):
                    links[0] += 1
                    ins.then_inc(g_chain, 1)
                    dve.wait_ge(g_chain, b * per_batch + links[0])

                for c, (a, n) in enumerate(CH):
                    dve.wait_ge(g_rope_mm, b * 4 + c + 1)
                    link(v.tensor_tensor(g_tmp[:, 0, 0:n], bank(1)[:, 0:n], g_cos[:, a:a + n], ALU.mult))
                    link(v.tensor_tensor(g_tmp[:, 1, 0:n], bank(2)[:, 0:n], g_sin[:, a:a + n], ALU.mult))
                    v.tensor_tensor(g_kf[0][0:R, a:a + n], g_tmp[0:R, 0, 0:n], g_tmp[0:R, 1, 0:n], ALU.add)
                    v.tensor_tensor(g_kf[1][R:P, a:a + n], g_tmp[R:P, 0, 0:n], g_tmp[R:P, 1, 0:n], ALU.add)\
                        .then_inc(g_rope_ev, 1)
                    dve.wait_ge(g_rope_ev, b * 4 + c + 1)
                for t in range(2):
                    for i, seg in enumerate((segf, seglo)):
                        link(v.tensor_copy(segend[i], seg[:, bass.ds(b * 2 + t, 1)]))
                    link(v.tensor_scalar(g_bias, g_id, segend[0], None, ALU.is_le))
                    link(v.scalar_tensor_tensor(out=g_bias, in0=g_id, scalar=segend[1], in1=g_bias, op0=ALU.is_ge,
                                                op1=ALU.mult))
                    link(v.tensor_scalar(g_bias, g_bias, -1.0, -NEG, ALU.add, ALU.mult))
                    for h in range(H):
                        n0 = t * H + h
                        dve.wait_ge(g_s_mm, b * 32 + n0 + 1)
                        for c, (a, n) in enumerate(CH):
                            last = v.tensor_tensor(g_w[:, a:a + n], bank(c)[:, 0:n], g_bias[:, a:a + n], ALU.add)
                        link(last)
                        link(v.tensor_reduce(g_mx, g_w, AX_X, ALU.max))
                        v.tensor_scalar(g_w, g_w, g_mx, None, ALU.subtract).then_inc(g_max, 1)
                        dve.wait_ge(g_exp, b * 32 + n0 + 1)
                        link(v.tensor_reduce(g_sum, g_w, AX_X, ALU.add))
                        link(v.reciprocal(g_rec, g_sum))
                        v.tensor_scalar(g_w, g_w, g_rec, None, ALU.mult).then_inc(g_norm, 1)
                        dve.wait_ge(g_pv_mm, b * 32 + n0 + 1)
                        lo = (h % 2) * KVC
                        v.tensor_copy(olat[lo:lo + KVC, h // 2, :], bank(0)[lo:lo + KVC, 0:P]).then_inc(g_pv_ev, 1)
                    dve.wait_ge(g_o_mm, b * 2 + t + 1)
                    xt = x[:, bass.ds(b * 2 + t, 1), :]
                    v.tensor_tensor(xt, xt, bank(1)[:, 0:D].unsqueeze(1), ALU.add).then_inc(g_x, 1)
            assert links[0] == per_batch, links[0]
            dve.wait_ge(g_x, TILES)

        def general_gpsimd():
            nc.gpsimd.wait_ge(g_x, TILES)

        @block.sync
        def _(sp):
            def load(s, *pairs):
                for dst, src in pairs:
                    sp.dma_start(dst, src).then_inc(s, 16)

            load(ld_x, (x, x_in.rearrange("(t p) d -> p t d", p=P)), (ident[:, :], ident_in), (segi[:, :], seg_in))
            load(ld_key, (ctx0, ctx0_in), (wkvc, wkvc_in), (wkr, wkr_in), (wkrs, wkrs_in))
            load(ld_q, (wuq, wuq_in), (wuk, wuk_in), (weff[:, 0::2, 0:R], wqr_in[:, 0::2, :]),
                 (weff[:, 1::2, KVC:P], wqr_in[:, 1::2, :]), (wqrs, wqrs_in), (wdq, wdq_in))
            load(ld_const, (tabs, tabs_in), (kk[:, :], kk_in))
            load(ld_seg, (segrow, segrow_in))
            load(ld_w1, (wnat[:, 0], wq_in), (wnat[:, 1], wp_in), (rows[:, 0:3, :], rows_in), (wkvT, wkv_in),
                 (bk[:, :], bk_in), (router, router_in))
            load(ld_vo, (wuv, wuv_in), (wo, wo_in))
            sp.wait_ge(wt_mm, 2)
            sp.wait_ge(qc_mm, 2)
            sp.wait_ge(rope_mm, 2)
            sp.wait_ge(kvt_mm, 1)
            load(ld_ctx, (ctxT, ctx_in[0]))
            far_ids(sp, general_sync)
            sp.wait_ge(x1_rdy, TILES)
            load(ld_ffn, (gu, gu_in), (sgu, sgu_in), (down[:, 0:E, :], down_in), (down[:, E, :], sdown_in))
            load(ld_ones, (kst[SROWS:SROWS + 3], ones_in))

            def stack_keys(s):
                sp.wait_ge(kpart_rdy, s + 1)
                sp.wait_ge(k_ev, len(CH) * (s + 1))
                if s >= 2:
                    sp.wait_ge(k_stk[s % 2], 96 * (s // 2))
                for j in range(3):
                    sp.dma_start(kscr[s % 2, j], kpart[s][j]).then_inc(k_wr, 16)
                sp.wait_ge(k_wr, 48 * (s + 1))
                if s >= 2:
                    sp.wait_ge(sc_mm, 2 * KT * (s - 1))
                for g, j in enumerate(STACK_K):
                    sp.dma_start(kst[g * DH:(g + 1) * DH, s % 2], kscr[s % 2, j].rearrange("(h d) k -> d h k", d=DH))\
                        .then_inc(k_stk[s % 2], 16)

            stack_keys(0)
            stack_keys(1)
            sp.wait_ge(k_mm, 2 * len(CH))
            sp.wait_ge(v_mm, (KT + 1) // 2)
            load(ld_ctx, (ctxT, ctx_in[1]))
            for t in range(TILES):
                sp.wait_ge(qpart_rdy, t + 1)
                for j in range(3):
                    sp.dma_start(qscr[j].rearrange("(c p) t -> p c t", p=P)[:, :, t * P:(t + 1) * P],
                                 qpart[t % 2][:, j, :].rearrange("p (c t) -> p c t", c=FC)).then_inc(q_wr[t % 2], 16)
                if t % 2 == 1:
                    b = t // 2
                    for w in q_wr:
                        sp.wait_ge(w, 48 * (b + 1))
                    if b == 0:
                        sp.wait_ge(k_wr, 96)
                    for g, j in enumerate(STACK_Q):
                        sp.dma_start(qst[g * DH:(g + 1) * DH, :, b * LQ:(b + 1) * LQ],
                                     qscr[j].rearrange("(h d) t -> d h t", d=DH)[:, :, b * LQ:(b + 1) * LQ])\
                            .then_inc(q_stk[b], 16)
            sp.wait_ge(dn_mm, TILES)
            load(ld_ffn1, (wup, wup_in), (wdn, wdn_in), (wex, wex_in), (wg, wg_in))

            def store(b):
                for i in range(2):
                    t = 2 * b + i
                    sp.wait_ge(y_rdy, t + 1)
                    sp.dma_start(out[t * P:(t + 1) * P, :], y[i][:, :]).then_inc(stored[i], 16)

            for b in range(B - 1):
                if b >= 1:
                    store(b - 1)
                stack_keys(2 * b + 2)
                if b + 2 < B:
                    sp.wait_ge(v_mm, (KT + 1) // 2 * (b + 2))
                    sp.wait_ge(k_mm, len(CH) * (2 * b + 4))
                    load(ld_ctx, (ctxT, ctx_in[b + 2]))
                stack_keys(2 * b + 3)
            store(B - 2)
            store(B - 1)
            for w in stored:
                sp.wait_ge(w, 16 * TILES // 2)

        @block.gpsimd
        def _(pool):
            def rsqrt(n):
                pool.wait_ge(eps_rdy, n + 1)
                nc.gpsimd.tensor_tensor(rstd[n % 2], mv[n % 2][:, 1:2], neghalf, ALU.pow).then_inc(rstd_rdy, 1)

            for t in range(TILES):
                rsqrt(t)
            for hf in range(2):
                for pair in range(H // 2):
                    n = hf * (H // 2) + pair
                    pool.wait_ge(qb_ev, n + 1)
                    pool.wait_ge(qa_ev, 2 * n + 2)
                    for par in range(2):
                        at = slice(par * R, par * R + R)
                        q = qf(2 * pair + par)[at, hf * 512:(hf + 1) * 512]
                        nc.gpsimd.tensor_tensor(q, q, ropet[n % 2][at, :], ALU.add).then_inc(q_rdy, 1)
                        pool.wait_ge(q_rdy, 2 * n + par + 1)
            for t in range(TILES):
                for j in range(2):
                    pool.wait_ge(s_rec, 2 * t + j + 1)
                    heads = slice(j * H // 2, (j + 1) * H // 2)
                    nc.gpsimd.tensor_tensor(sm[t % 2][:, heads, :], sm[t % 2][:, heads, :],
                                            rec0[t % 2][:, heads].unsqueeze(2).to_broadcast([P, H // 2, K0]),
                                            ALU.mult).then_inc(s_norm, 1)

            far_ids(pool, general_gpsimd)

            def split_keys(s):
                pool.wait_ge(k_ev, len(CH) * (s + 1))
                if s >= 3:
                    pool.wait_ge(k_wr, 48 * s)
                nc.gpsimd.tensor_tensor(kpart[s][1], kf[s], kpart[s][0], ALU.subtract).then_inc(ks_a, 1)
                pool.wait_ge(ks_a, s + 1)
                nc.gpsimd.tensor_tensor(kf[s], kf[s], kpart[s][0], ALU.subtract).then_inc(ks_b, 1)
                pool.wait_ge(ks_b, s + 1)
                nc.gpsimd.tensor_tensor(kpart[s][2], kf[s], kpart[s][1], ALU.subtract).then_inc(kpart_rdy, 1)

            def split_queries(t):
                part = qpart[t % 2]
                pool.wait_ge(q1T_ev, t + 1)
                if t >= 2:
                    pool.wait_ge(q_wr[t % 2], 48 * (t // 2))
                nc.gpsimd.tensor_tensor(part[:, 1, :], qTf[:, :], part[:, 0, :], ALU.subtract).then_inc(qs_a, 1)
                pool.wait_ge(qs_a, t + 1)
                nc.gpsimd.tensor_tensor(qTf[:, :], qTf[:, :], part[:, 0, :], ALU.subtract).then_inc(qs_b, 1)
                pool.wait_ge(qs_b, t + 1)
                nc.gpsimd.tensor_tensor(part[:, 2, :], qTf[:, :], part[:, 1, :], ALU.subtract).then_inc(qpart_rdy, 1)

            def sigmoid_power(t):
                pool.wait_ge(ntop_rdy, t + 1)
                nc.gpsimd.tensor_tensor(sig[t % 2], eul.to_broadcast([P, 2]), ntop, ALU.pow).then_inc(pow_rdy, 1)

            n = TILES
            for _ in range(2):
                rsqrt(n)
                n += 1
            sigmoid_power(0)
            split_keys(0)
            split_keys(1)
            for t in range(TILES + 2):
                if 1 <= t <= TILES:
                    rsqrt(n)
                    n += 1
                if t + 2 < TILES:
                    rsqrt(n)
                    n += 1
                if t + 1 < TILES:
                    sigmoid_power(t + 1)
                if t >= 3:
                    split_queries(t - 3)
            split_queries(TILES - 1)

            def rsqrt3(b):
                pool.wait_ge(n3_eps, b + 1)
                nc.gpsimd.tensor_tensor(rstd3, mv3[:, :, 1], neghalf.to_broadcast([P, 2]), ALU.pow)\
                    .then_inc(n3_rstd, 1)

            for b in range(B):
                if b >= 1:
                    rsqrt3(b - 1)
                if b + 1 < B:
                    split_keys(2 * b + 2)
                    split_keys(2 * b + 3)
            rsqrt3(B - 1)

        @block.tensor
        def _(pe):
            mm = nc.tensor.matmul

            pe.wait_ge(zero_rdy, 1)
            for _ in range(16):
                mm(bank(0), zeros[:, 0:P], zeros[:, :], start=True, stop=True)
            pe.wait_ge(ld_key, 64)
            for c in range(FC):
                last = mm(bank(6), wkvc[:, c, :], ctx0[:, c, :], start=c == 0, stop=c == FC - 1)
            last.then_inc(kv_mm, 1)
            for b in range(B):
                for c in range(FC):
                    last = mm(bank(5)[:, b * KVC:(b + 1) * KVC], ctx0[:, c, b * K0:(b + 1) * K0], wkvc[:, c, 0:KVC],
                              start=c == 0, stop=c == FC - 1)
            last.then_inc(kvt_mm, 1)
            pe.wait_ge(kv_ev, 1)
            mm(bank(7), wkr, kf0[1][0:KVC, :], start=True, stop=True).then_inc(rope_mm, 1)
            pe.wait_ge(kv_ev, 2)
            mm(bank(6), wkrs, kf0[1][0:KVC, :], start=True, stop=True).then_inc(rope_mm, 1)
            for t in range(TILES):
                pe.wait_ge(xn_rdy, t + 1)
                if t >= 2:
                    pe.wait_ge(xnT_ev, t - 1)
                for c in range(FC):
                    last = nc.tensor.transpose(bank(2 + t % 2)[:, c * P:(c + 1) * P], xn[t % 2][:, c * P:(c + 1) * P],
                                               ident[:, :])
                last.then_inc(xnT_mm, 1)
            pe.wait_ge(ld_q, 96)
            for h in range(H):
                last = mm(bank(h // 8)[0:QC, (h % 8) * KVC:(h % 8 + 1) * KVC], wuq[:, h, :], wuk[:, h, :],
                          start=True, stop=True)
                if h % 8 == 7:
                    last.then_inc(m_mm, 1)
            for hf in range(2):
                pe.wait_ge(xnT_ev, 4 * hf + 4)
                for c in range(FC):
                    last = mm(bank(4 - hf)[0:QC, :], wdq[:, c, :], xnT[:, c, hf * 512:(hf + 1) * 512], start=c == 0,
                              stop=c == FC - 1)
                last.then_inc(qc_mm, 1)
            for hf in range(2):
                at = slice(hf * 512, (hf + 1) * 512)
                for h in range(H):
                    n = hf * H + h
                    if n >= 4:
                        pe.wait_ge(qa_ev, n - 3)
                    elif n == 0:
                        pe.wait_ge(m_ev, 2)
                        pe.wait_ge(xnT_ev, TILES)
                        pe.wait_ge(qc_ev, 2)
                    mm(bank(n % 4), weff[:, h, :], qcT[:, at], start=True, stop=True).then_inc(qa_mm, 1)
                    if h % 2 == 1:
                        k = hf * (H // 2) + h // 2
                        if k >= 2:
                            pe.wait_ge(qb_ev, k - 1)
                        elif k == 1:
                            pe.wait_ge(kvt_ev, 1)
                        mm(bank(4 + k % 2), wqrs[:, h // 2, :], qcT[:, at], start=True,
                           stop=True).then_inc(qb_mm, 1)

            for m in range(2):
                pe.wait_ge(wint_rdy, m + 1)
                if m == 0:
                    pe.wait_ge(rope_done, 1)
                tb = bank(6 + m).bitcast(BF16)
                for c in range(FC):
                    for o in range(FC):
                        last = nc.tensor.transpose(tb[:, (c * FC + o) * P:(c * FC + o + 1) * P],
                                                   (wint, wint2)[m][:, o, c * P:(c + 1) * P], identb[:, :])
                last.then_inc(wt_mm, 1)
            pe.wait_ge(qb_ev, H)
            for m in range(2):
                for o in range(FC):
                    last = mm(bank(5)[:, m * D + o * P:m * D + (o + 1) * P],
                              wsc[:, 2 * m + o:2 * m + o + 1].to_broadcast([P, P]), ident[:, :], start=True, stop=True)
            last.then_inc(sw_mm, 1)
            def attend0(t, groups):
                b = t // 2
                at = slice(t * P, (t + 1) * P)
                pe.wait_ge(mask_rdy, t + 1)
                if t % 4 == 0 and 0 in groups:
                    pe.wait_ge(q_rdy, H * (t // 4 + 1))
                    pe.wait_ge(qa_ev, H * (t // 4 + 1))
                if t == 0:
                    pe.wait_ge(qa_ev, 2 * H)
                for g in groups:
                    if t > 0 and g % 2 == 0:
                        pe.wait_ge(s_sub, 2 * t - 1 + g // 2)
                    mm(bank(g), identb[:, :], maskb[t % 2].unsqueeze(1).to_broadcast([P, 4, K0]), start=True,
                       stop=False, skip_group_check=True)
                    for k in range(4):
                        h = 4 * g + k
                        last = mm(bank(g)[:, k * K0:(k + 1) * K0], qf(h)[:, at], kf0[h % 2][:, b * K0:(b + 1) * K0],
                                  start=False, stop=True, skip_group_check=True)
                    if g % 2 == 1:
                        last.then_inc(s_mm, 1)

            def values0(t):
                b = t // 2
                if t == 0:
                    pe.wait_ge(m_ev, 6)
                for g in range(4):
                    n = 4 * t + g
                    if g % 2 == 0:
                        pe.wait_ge(s_norm, 2 * t + g // 2 + 1)
                    if n >= 2:
                        pe.wait_ge(pt_ev, n - 1)
                    for k in range(4):
                        last = nc.tensor.transpose(bank(4 + n % 2)[:, k * P:(k + 1) * P], sm[t % 2][:, 4 * g + k, :],
                                                   ident[:, :])
                    last.then_inc(pt_mm, 1)
                for j in range(2):
                    n = 2 * t + j
                    pe.wait_ge(pt_ev, 4 * t + 2 * j + 2)
                    if n >= 1:
                        pe.wait_ge(pv_ev, n)
                    elif n == 0:
                        pe.wait_ge(wt_ev, 2)
                    for par in range(2):
                        last = mm(bank(6)[par * KVC:(par + 1) * KVC, :], kvtok[:, b, :],
                                  pT[:, 8 * j + par:8 * j + 8:2, :], start=True, stop=True)
                    last.then_inc(pv_mm, 1)
                    if j == 0 and 2 <= t + 2 < TILES:
                        attend0(t + 2, (0,))
                if t >= 1:
                    pe.wait_ge(x1_rdy, t)
                for p2 in range(H // 2):
                    if p2 % 4 == 0:
                        pe.wait_ge(pv_ev, 2 * t + p2 // 4 + 1)
                    last = mm(bank(7)[:, 0:D], olat[:, p2, :], wuvo[:, p2, :], start=p2 == 0, stop=p2 == H // 2 - 1)
                last.then_inc(ao_mm, 1)

            def output_weights0():
                pe.wait_ge(ld_vo, 32)
                pe.wait_ge(wt_ev, 2)
                pe.wait_ge(sw_ev, 1)
                for h in range(H):
                    p2 = h // 2
                    last = mm(bank(4 + p2 // 2)[(h % 2) * KVC:(h % 2 + 1) * KVC, (p2 % 2) * D:(p2 % 2 + 1) * D],
                              wuv[:, h, :], wo[:, h, :], start=True, stop=True)
                    if h % 4 == 3:
                        last.then_inc(m_mm, 1)

            for t in range(TILES + 1):
                if t < TILES:
                    attend0(t, range(4) if t < 2 else range(1, 4))
                if t == 0:
                    output_weights0()
                if t >= 1:
                    values0(t - 1)

            far_ids(pe, general_tensor)

            def keys(s, c, bnk, between=None):
                a, n = CH[c]
                for k in range(FC):
                    if k >= 1 and between:
                        between(4 * n)
                    last = mm(bank(bnk)[:, 0:n], wkvT[:, k, (s % 2) * P:(s % 2 + 1) * P], ctxT[:, k, a:a + n],
                              start=k == 0, stop=k == FC - 1)
                last.then_inc(k_mm, 1)

            def values(b, j, bnk, between=None):
                for i in range(2 * j, min(2 * j + 2, KT)):
                    n = P if i < KT - 1 else KLAST
                    for k in range(FC):
                        if i % 2 + k >= 1 and between:
                            between(4 * D)
                        last = mm(bank(bnk)[0:n, (i % 2) * D:(i % 2 + 1) * D], ctxT[:, k, i * P:i * P + n],
                                  wkvT[:, k, D:2 * D], start=k == 0, stop=k == FC - 1)
                last.then_inc(v_mm, 1)

            NV = (KT + 1) // 2
            pe.wait_ge(ld_ctx, 16)
            pe.wait_ge(x1_rdy, TILES)
            def turn_h(t):
                pe.wait_ge(f_rdy, t + 1)
                if t >= 1:
                    pe.wait_ge(lg_rdy, t)
                for c in range(FC):
                    last = nc.tensor.transpose(bank(3)[:, c * P:(c + 1) * P], xn[0][:, c * P:(c + 1) * P], ident[:, :])
                last.then_inc(hT_mm, 1)

            def route(t):
                pe.wait_ge(hT_ev, t + 1)
                for k in range(FC):
                    last = mm(bank(3)[:, 0:E], hT[t % 2][:, k, :], router[:, k, :], start=k == 0, stop=k == FC - 1)
                last.then_inc(rt_mm, 1)

            done = []
            for s in range(2):
                for c in range(len(CH)):
                    if len(done) >= 2:
                        pe.wait_ge(*done[-2])
                    keys(s, c, 6 + len(done) % 2)
                    done.append((k_ev, len(CH) * s + c + 1))
                if s == 0:
                    turn_h(0)
                else:
                    route(0)
            for j in range(NV):
                pe.wait_ge(*done[-2])
                values(0, j, 6 + len(done) % 2)
                done.append((v_ev, j + 1))

            def gate_up(t, c):
                n = 5 * t + c
                if c == 0:
                    pe.wait_ge(hT_ev, t + 1)
                if n >= 3:
                    pe.wait_ge(hid_rdy, n - 2)
                w = gu[:, :, c * 512:(c + 1) * 512] if c < 4 else sgu
                for k in range(FC):
                    last = mm(bank(n % 3)[:, 0:w.shape[2]], hT[t % 2][:, k, :], w[:, k, :], start=k == 0,
                              stop=k == FC - 1)
                last.then_inc(gu_mm, 1)

            def turn_hidden(t, g):
                n = 3 * t + g
                pe.wait_ge(hid_rdy, 5 * t + (2, 4, 5)[g])
                if n >= 2:
                    pe.wait_ge(ht_ev, n - 1)
                for e in range(4 * g, min(4 * g + 4, HB)):
                    last = nc.tensor.transpose(bank(4 + n % 2)[:, (e % 4) * P:(e % 4 + 1) * P], hid[t % 2][:, e, :],
                                               ident[:, :])
                last.then_inc(ht_mm, 1)

            def combine(t):
                if t >= 1:
                    pe.wait_ge(x2_rdy, t)
                for e in range(HB):
                    if e % 4 == 0:
                        pe.wait_ge(ht_ev, 3 * t + e // 4 + 1)
                    last = mm(bank(6)[:, 0:D], hidT[:, e, :], down[:, e, :], start=e == 0, stop=e == HB - 1)
                last.then_inc(dn_mm, 1)

            def turn_xq(t):
                pe.wait_ge(xq_rdy, t + 1)
                if t >= 1:
                    pe.wait_ge(q1T_ev, t)
                for c in range(FC):
                    last = nc.tensor.transpose(bank(7).bitcast(BF16)[:, c * P:(c + 1) * P],
                                               xq[t % 2][:, c * P:(c + 1) * P], identb[:, :])
                last.then_inc(xqT_mm, 1)

            def project_q(t):
                pe.wait_ge(xqT_ev, t + 1)
                for k in range(FC):
                    last = mm(bank(7)[:, 0:D], xqT[:, k, :], wintT[:, 0, k, :], start=k == 0, stop=k == FC - 1)
                last.then_inc(q1_mm, 1)

            def turn_q(t):
                pe.wait_ge(q1_rdy, t + 1)
                for c in range(FC):
                    last = nc.tensor.transpose(bank(7)[:, c * P:(c + 1) * P], qtok[:, c * P:(c + 1) * P], ident[:, :])
                last.then_inc(q1T_mm, 1)

            def max_scores(quad, n):
                b, s, u, c = quad // 4, quad // 2, n // len(CH), n % len(CH)
                h = 4 * (quad % 4) + u // 2
                ca = 8 * len(CH) * quad + n
                if n == 0:
                    pe.wait_ge(k_stk[s % 2], 96 * (s // 2 + 1))
                    pe.wait_ge(q_stk[b], 96)
                if ca >= 2:
                    pe.wait_ge(mx_rdy, ca - 1)
                a, m = CH[c]
                q0 = b * LQ + (u % 2) * P
                mm(bank(ca % 2)[:, 0:m], qst[0:SROWS, h, q0:q0 + P], kst[0:SROWS, s % 2, h % HALF, a:a + m],
                   start=True, stop=True).then_inc(mx_mm, 1)

            def first_maxima(t, third):
                chunks = list(first_chunks(t, third))

                def next_chunk(columns=0):
                    if chunks:
                        max_scores(0, chunks.pop(0))

                j = 3 * (t - TILES) + third
                pe.wait_ge(ld_ctx, 32)
                if j < 5:
                    pe.wait_ge(*((v_ev, NV + j - 1) if j >= 2 else (ht_ev, 3 * TILES)))
                    next_chunk()
                    values(1, j, 4 + j % 2, next_chunk)
                while chunks:
                    next_chunk()

            pe.wait_ge(ld_ffn, 64)
            for t in range(TILES + 2):
                if t < TILES:
                    gate_up(t, 0)
                if t >= 3:
                    turn_q(t - 3)
                if 1 <= t <= TILES:
                    turn_hidden(t - 1, 0)
                    turn_hidden(t - 1, 1)
                if t < TILES:
                    gate_up(t, 1)
                if 1 <= t <= TILES:
                    turn_hidden(t - 1, 2)
                if t < TILES:
                    gate_up(t, 2)
                else:
                    first_maxima(t, 0)
                if 1 <= t <= TILES:
                    combine(t - 1)
                if t + 1 < TILES:
                    turn_h(t + 1)
                if t >= 2:
                    turn_xq(t - 2)
                if t < TILES:
                    gate_up(t, 3)
                else:
                    first_maxima(t, 1)
                if t + 1 < TILES:
                    route(t + 1)
                if t >= 2:
                    project_q(t - 2)
                if t < TILES:
                    gate_up(t, 4)
                else:
                    first_maxima(t, 2)
            turn_q(TILES - 1)
            pe.wait_ge(v_ev, NV + 4)
            values(1, 5, 5)

            taken = [(q1T_ev, TILES)]

            def bank7(reader, value):
                pe.wait_ge(*taken[0])
                taken[0] = (reader, value)

            def shift(quad):
                bank7(sh_rdy, quad + 1)
                pe.wait_ge(nst_rdy, quad + 1)
                tb = bank(7).bitcast(BF16)
                for u in range(8):
                    last = nc.tensor.transpose(tb[SROWS:SROWS + 3, u * P:(u + 1) * P], nst[quad % 2][:, u, :],
                                               identb[:, :])
                last.then_inc(sh_mm, 1)

            def scores(quad, kt, first):
                i, b, s = KT * quad + kt, quad // 4, quad // 2
                n = P if kt < KT - 1 else KLAST
                if first == 0:
                    if kt == 0:
                        pe.wait_ge(sh_rdy, quad + 1)
                    if i == 0:
                        pe.wait_ge(ld_ones, 16)
                    if i == 1:
                        pe.wait_ge(v_ev, 2 * NV)
                    if i >= 2:
                        pe.wait_ge(ex_rdy, i - 1)
                for k in (first, first + 1):
                    h = 4 * (quad % 4) + k
                    last = mm(bank(2 + 2 * (i % 2), 2)[0:n, k * LQ:(k + 1) * LQ],
                              kst[0:SROWS + 3, s % 2, h % HALF, kt * P:kt * P + n],
                              qst[0:SROWS + 3, h, b * LQ:(b + 1) * LQ], start=True, stop=True)
                if first == 2:
                    last.then_inc(sc_mm, 1)

            def weigh(i):
                quad, kt = i // KT, i % KT
                b = quad // 4
                n = P if kt < KT - 1 else KLAST
                pe.wait_ge(ex_rdy, i + 1)
                if kt == 0:
                    pe.wait_ge(v_ev, NV * (b + 1))
                    if quad >= 1:
                        pe.wait_ge(po_rdy, quad)
                if i == 0:
                    pe.wait_ge(vone_rdy, 1)
                    pe.wait_ge(po_zero, 1)
                for k in range(4):
                    h = 4 * (quad % 4) + k
                    last = mm(bank(6)[32 * k:32 * k + VW, 0:LQ], vx[0:n, b % 2, kt, h, :],
                              pr[i % 3][0:n, k * LQ:(k + 1) * LQ], start=kt == 0, stop=kt == KT - 1,
                              skip_group_check=True)
                last.then_inc(av_mm, 1)

            def turn_out(quad):
                bank7(o_rdy, quad + 1)
                pe.wait_ge(po_rdy, quad + 1)
                for q in range(2):
                    last = nc.tensor.transpose(bank(7)[:, q * P:(q + 1) * P], poS[quad % 2][:, q * P:(q + 1) * P],
                                               ident[:, :])
                last.then_inc(ot_mm, 1)

            def tail(b, part, between):
                tiles = range(2)
                at = tail_bank(b, part)
                take = bank7 if b + 1 < B else (lambda reader, value: None)
                if b + 1 == B and part in ("turn_o", "turn_x"):
                    for _ in range({"turn_o": 10, "turn_x": 17}[part]):
                        mm(bank(4), wintT[:, 1, 0, 0:P], wintT[:, 1].rearrange("p c n -> p (c n)"), start=True,
                           stop=True)
                if part == "turn_o":
                    bank7(oiT_ev, b + 1)
                    pe.wait_ge(oi_rdy, b + 1)
                    for i in tiles:
                        for c in range(FC):
                            at = (i * FC + c) * P
                            last = nc.tensor.transpose(bank(7).bitcast(BF16)[:, at:at + P],
                                                       xq[i][:, c * P:(c + 1) * P], identb[:, :])
                    last.then_inc(oiT_mm, 1)
                elif part == "project":
                    bank7(wp_ev, b + 1)
                    pe.wait_ge(oiT_ev, b + 1)
                    for i in tiles:
                        for k in range(FC):
                            last = mm(bank(7)[:, i * D:(i + 1) * D], xqT2[:, i, k, :], wintT[:, 1, k, :],
                                      start=k == 0, stop=k == FC - 1)
                    last.then_inc(wp_mm, 1)
                elif part == "turn_x":
                    take(x3T_ev, b + 1)
                    pe.wait_ge(n3_rdy, b + 1)
                    for i in tiles:
                        for c in range(FC):
                            col0 = (i * FC + c) * P
                            last = nc.tensor.transpose(bank(at)[:, col0:col0 + P], xn[i][:, c * P:(c + 1) * P],
                                                       ident[:, :])
                    last.then_inc(x3T_mm, 1)
                elif part == "up":
                    take(up_rdy, b + 1)
                    pe.wait_ge(x3T_ev, b + 1)
                    if b == 0:
                        pe.wait_ge(ld_ffn1, 64)
                    for f in range(FC):
                        for k in range(FC):
                            if f + k >= 1:
                                between(4 * D)
                            last = mm(bank(at)[:, f * 2 * P:(f + 1) * 2 * P], wup[:, k, f * P:(f + 1) * P],
                                      hT2[:, :, k, :], start=k == 0, stop=k == FC - 1)
                    last.then_inc(up_mm, 1)
                elif part == "gate":
                    take(lg1_rdy, b + 1)
                    for i in tiles:
                        for k in range(FC):
                            last = mm(bank(at)[:, i * E:(i + 1) * E], hT[i][:, k, :], wg[:, k, :], start=k == 0,
                                      stop=k == FC - 1)
                    last.then_inc(rt_mm, 1)
                elif part == "down":
                    take(d_rdy, b + 1)
                    pe.wait_ge(up_rdy, b + 1)
                    for i in tiles:
                        for k in range(FC):
                            if i + k >= 1:
                                between(4 * D)
                            last = mm(bank(at)[:, i * D:(i + 1) * D], upT[:, k, i * P:(i + 1) * P], wdn[:, k, :],
                                      start=k == 0, stop=k == FC - 1)
                    last.then_inc(d_mm, 1)
                elif part == "expert":
                    take(y_rdy, 2 * b + 2)
                    for i in tiles:
                        for k in range(FC):
                            if i + k >= 1:
                                between(4 * D)
                            last = mm(bank(at)[:, i * D:(i + 1) * D], hT[i][:, k, :], wex[:, k, :], start=k == 0,
                                      stop=k == FC - 1)
                    last.then_inc(y_mm, 1)

            def beside(jobs, between):
                for what, *a in jobs:
                    if what == "shift":
                        shift(*a)
                    elif what == "k":
                        s, c = a
                        bank7(k_ev, len(CH) * s + c + 1)
                        if c == 0:
                            pe.wait_ge(ld_ctx, 16 * (s // 2 + 1))
                        keys(s, c, 7, between)
                    elif what == "v":
                        b, j = a
                        bank7(v_ev, NV * b + j + 1)
                        if j == 0:
                            pe.wait_ge(ld_ctx, 16 * (b + 1))
                        values(b, j, 7, between)
                    elif what == "out":
                        turn_out(*a)
                    elif what == "tail":
                        tail(*a, between)

            shift(0)
            pe.wait_ge(v_ev, NV + 5)
            values(1, 6, 4)
            for quad in range(QUADS + 2):
                for kt in range(KT):
                    jobs = BESIDE.get((quad, kt), [])
                    maxima = [j for j in jobs if j[0] == "max"]
                    others = [j for j in jobs if j[0] != "max"]

                    total, count = step_work(others), len(maxima)
                    passed = [0]

                    def pace(columns):
                        passed[0] += columns
                        while maxima and (count - len(maxima)) * total < count * passed[0]:
                            max_scores(*maxima.pop(0)[1:])

                    if quad < QUADS:
                        pace(1)
                        scores(quad, kt, 0)
                        pace(2 * LQ)
                        scores(quad, kt, 2)
                        pace(2 * LQ)
                        if quad or kt:
                            weigh(KT * quad + kt - 1)
                        pace(4 * LQ)
                    elif quad == QUADS and kt == 0:
                        weigh(STEPS - 1)
                    beside(others, pace)
                    while maxima:
                        max_scores(*maxima.pop(0)[1:])

        @block.scalar
        def _(act):
            fn = nc.scalar.activation

            act.wait_ge(kv_mm, 1)
            fn(kf0[1][0:KVC, :], bank(6)[0:KVC, :], ACT.Copy).then_inc(kv_ev, 1)
            fn(kf0[0][KVC:P, :], bank(6)[KVC:P, :], ACT.Copy).then_inc(kv_ev, 1)
            act.wait_ge(kvt_mm, 1)
            fn(kvtok, bank(5)[:, 0:B * KVC].rearrange("p (b n) -> p b n", b=B), ACT.Copy).then_inc(kvt_ev, 1)
            for t in range(TILES):
                act.wait_ge(xnT_mm, t + 1)
                fn(xnT[:, :, t * P:(t + 1) * P], bank(2 + t % 2)[:, 0:D].rearrange("p (c t) -> p c t", c=FC),
                   ACT.Copy).then_inc(xnT_ev, 1)
            act.wait_ge(ld_q, 96)
            for g in range(2):
                act.wait_ge(m_mm, g + 1)
                src = bank(g)[0:QC, :].rearrange("p (h n) -> p h n", h=8)
                fn(weff[:, 8 * g:8 * g + 8:2, R:P], src[:, 0::2, :], ACT.Copy)
                fn(weff[:, 8 * g + 1:8 * g + 8:2, 0:KVC], src[:, 1::2, :], ACT.Copy).then_inc(m_ev, 1)
            for hf in range(2):
                act.wait_ge(qc_mm, hf + 1)
                fn(qcT[:, hf * 512:(hf + 1) * 512], bank(4 - hf)[0:QC, :], ACT.Copy).then_inc(qc_ev, 1)
            for m in range(2):
                act.wait_ge(wt_mm, m + 1)
                fn(wintT[:, m], bank(6 + m).bitcast(BF16)[:, 0:2 * D].rearrange("p (c n) -> p c n", c=FC),
                   ACT.Copy).then_inc(wt_ev, 1)
            act.wait_ge(sw_mm, 1)
            act.wait_ge(ld_w1, 96)
            fn(rows[:, 3:5, :], bank(5).rearrange("p (r d) -> p r d", r=2), ACT.Copy).then_inc(sw_ev, 1)
            for t in range(TILES + 1):
                if t >= 1:
                    for g in range(4):
                        act.wait_ge(pt_mm, 4 * (t - 1) + g + 1)
                        if t >= 2 and g == 0:
                            act.wait_ge(pv_mm, 2 * (t - 1))
                        elif t == 1 and g == 0:
                            act.wait_ge(kv_mm, 1)
                        fn(pT[:, 4 * g:4 * g + 4, :], bank(4 + g % 2).rearrange("p (h n) -> p h n", h=4), ACT.Copy)\
                            .then_inc(pt_ev, 1)
                    for j in range(2):
                        act.wait_ge(pv_mm, 2 * (t - 1) + j + 1)
                        if t >= 2 and j == 0:
                            act.wait_ge(ao_mm, t - 1)
                        fn(olat[:, 4 * j:4 * j + 4, :], bank(6).rearrange("p (h n) -> p h n", h=4), ACT.Copy)\
                            .then_inc(pv_ev, 1)
                if t < TILES:
                    for j in range(2):
                        act.wait_ge(s_sub, 2 * t + j + 1)
                        half = sm[t % 2][:, j * H // 2:(j + 1) * H // 2, :]
                        fn(half, half, ACT.Exp, scale=SCALE0).then_inc(s_exp, 1)
                if t == 0:
                    for g in range(4):
                        act.wait_ge(m_mm, 3 + g)
                        fn(wuvo[:, 2 * g:2 * g + 2, :], bank(4 + g).rearrange("p (h n) -> p h n", h=2), ACT.Copy)\
                            .then_inc(m_ev, 1)

            far_ids(act, general_scalar)

            def keys_bias(s, c, bnk):
                a, n = CH[c]
                act.wait_ge(k_mm, len(CH) * s + c + 1)
                if c == 0 and s == 0:
                    act.wait_ge(pt_mm, 4 * TILES)
                elif c == 0 and s >= 2:
                    act.wait_ge(kpart_rdy, s)
                    act.wait_ge(k_wr, 48 * s)
                fn(kf[s][:, a:a + n], bank(bnk)[:, 0:n], ACT.Identity, bias=bk[:, s % 2:s % 2 + 1])
                fn(kpart[s][0][:, a:a + n], bank(bnk)[:, 0:n], ACT.Identity, bias=bk[:, s % 2:s % 2 + 1])\
                    .then_inc(k_ev, 1)

            NV = (KT + 1) // 2

            def values_copy(b, j, bnk):
                act.wait_ge(v_mm, NV * b + j + 1)
                if b >= 2 and j == 0:
                    act.wait_ge(av_mm, 4 * KT * (b - 1))
                n = P if j < NV - 1 else KLAST
                tiles = 2 if 2 * j + 2 <= KT else 1
                fn(vx[0:n, b % 2, 2 * j:2 * j + tiles, :, 0:DH],
                   bank(bnk)[0:n, 0:tiles * D].rearrange("p (k h n) -> p k h n", k=tiles, h=H), ACT.Copy)\
                    .then_inc(v_ev, 1)

            def turned_h(t):
                act.wait_ge(hT_mm, t + 1)
                if t >= 2:
                    act.wait_ge(gu_mm, 5 * (t - 1))
                fn(hT[t % 2], bank(3)[:, 0:D].rearrange("p (c t) -> p c t", c=FC), ACT.Copy).then_inc(hT_ev, 1)

            n = 0
            for s in range(2):
                for c in range(len(CH)):
                    keys_bias(s, c, 6 + n % 2)
                    n += 1
                if s == 0:
                    turned_h(0)
            act.wait_ge(x1_rdy, TILES)
            for j in range(NV):
                values_copy(0, j, 6 + n % 2)
                n += 1

            def silu(t, c):
                n = 5 * t + c
                act.wait_ge(gu_mm, n + 1)
                if c == 0:
                    act.wait_ge(p_rdy, t + 1)
                if n >= 2:
                    act.wait_ge(hid_rdy, n - 1)
                src = bank(n % 3)
                if c < 4:
                    for e in range(2):
                        fn(sg[n % 2][:, e, :], src[:, e * 2 * I:e * 2 * I + I], ACT.Silu,
                           scale=probs[t % 2][:, 2 * c + e:2 * c + e + 1]).then_inc(silu_rdy, 1)
                else:
                    fn(sg[n % 2][:, 0, :], src[:, 0:I], ACT.Silu).then_inc(silu_rdy, 1)

            def turned_hidden(t, g):
                n = 3 * t + g
                act.wait_ge(ht_mm, n + 1)
                if g == 0 and t >= 1:
                    act.wait_ge(dn_mm, t)
                e = min(4, HB - 4 * g)
                fn(hidT[:, 4 * g:4 * g + e, :], bank(4 + n % 2)[:, 0:e * P].rearrange("p (e n) -> p e n", e=e),
                   ACT.Copy).then_inc(ht_ev, 1)

            def turned_xq(t):
                act.wait_ge(xqT_mm, t + 1)
                if t >= 1:
                    act.wait_ge(q1_mm, t)
                fn(xqT, bank(7).bitcast(BF16)[:, 0:D].rearrange("p (c t) -> p c t", c=FC), ACT.Copy)\
                    .then_inc(xqT_ev, 1)

            def turned_q(t):
                act.wait_ge(q1T_mm, t + 1)
                if t >= 1:
                    act.wait_ge(qpart_rdy, t)
                if t >= 2:
                    act.wait_ge(q_wr[t % 2], 48 * (t // 2))
                fn(qTf[:, :], bank(7)[:, 0:D], ACT.Copy)
                fn(qpart[t % 2][:, 0, :], bank(7)[:, 0:D], ACT.Copy).then_inc(q1T_ev, 1)

            def first_values(t, third):
                j = 3 * (t - TILES) + third
                if j < 5:
                    values_copy(1, j, 4 + j % 2)

            for t in range(TILES + 2):
                if t < TILES:
                    silu(t, 0)
                if t >= 3:
                    turned_q(t - 3)
                if 1 <= t <= TILES:
                    turned_hidden(t - 1, 0)
                    turned_hidden(t - 1, 1)
                if t < TILES:
                    silu(t, 1)
                if 1 <= t <= TILES:
                    turned_hidden(t - 1, 2)
                if t < TILES:
                    silu(t, 2)
                else:
                    first_values(t, 0)
                if t + 1 < TILES:
                    turned_h(t + 1)
                if t >= 2:
                    turned_xq(t - 2)
                if t < TILES:
                    silu(t, 3)
                    silu(t, 4)
                else:
                    first_values(t, 1)
                    first_values(t, 2)
            turned_q(TILES - 1)
            values_copy(1, 5, 5)

            def beside(quad, kt):
                for what, *a in BESIDE.get((quad, kt), []):
                    if what == "shift":
                        shift_rows(*a)
                    elif what == "k":
                        keys_bias(*a, 7)
                    elif what == "v":
                        values_copy(*a, 7)
                    elif what == "tail":
                        b, part = a
                        if part == "turn_o":
                            act.wait_ge(oiT_mm, b + 1)
                            if b == 0:
                                act.wait_ge(q1_mm, TILES)
                            fn(xqT2, bank(7).bitcast(BF16)[:, 0:2 * D].rearrange("p (t c n) -> p t c n", t=2, c=FC),
                               ACT.Copy).then_inc(oiT_ev, 1)
                        elif part == "turn_x":
                            act.wait_ge(x3T_mm, b + 1)
                            fn(hT2, bank(tail_bank(b, part)).rearrange("p (t c n) -> p t c n", t=2, c=FC), ACT.Copy)\
                                .then_inc(x3T_ev, 1)
                        elif part == "route":
                            act.wait_ge(dtop_rdy, b + 1)
                            fn(etop, dtop, ACT.Exp).then_inc(etop_rdy, 1)

            def shift_rows(quad):
                act.wait_ge(sh_mm, quad + 1)
                h, b = 4 * (quad % 4), quad // 4
                if quad == 0:
                    act.wait_ge(m_mm, 6)
                fn(qst[SROWS:SROWS + 3, h:h + 4, b * LQ:(b + 1) * LQ],
                   bank(7).bitcast(BF16)[SROWS:SROWS + 3, :].rearrange("p (h t) -> p h t", h=4), ACT.Copy)\
                    .then_inc(sh_rdy, 1)

            def out_copy(quad):
                act.wait_ge(av_mm, KT * (quad + 1))
                if quad >= 2:
                    act.wait_ge(ot_mm, quad - 1)
                fn(poS[quad % 2], bank(6)[:, 0:LQ], ACT.Copy).then_inc(po_rdy, 1)

            shift_rows(0)
            values_copy(1, 6, 4)
            act.wait_ge(dn_mm, TILES)
            for quad in range(QUADS + 2):
                for kt in range(KT):
                    if quad < QUADS:
                        i = KT * quad + kt
                        n = P if kt < KT - 1 else KLAST
                        act.wait_ge(sc_mm, i + 1)
                        if i >= 3:
                            act.wait_ge(av_mm, i - 2)
                        fn(pr[i % 3][0:n, :], bank(2 + 2 * (i % 2), 2)[0:n, :], ACT.Exp, scale=SCALE1)\
                            .then_inc(ex_rdy, 1)
                    if kt == 0 and 1 <= quad <= QUADS:
                        out_copy(quad - 1)
                    beside(quad, kt)

        @block.vector
        def _(dve):
            v = nc.vector
            chain = [0]

            def link(ins):
                chain[0] += 1
                ins.then_inc(dve_chain, 1)
                dve.wait_ge(dve_chain, chain[0])

            norms = [0]

            def normalise_a(t):
                n = norms[0]
                norms[0] += 1
                link(v.bn_stats(stats, x[:, t, :]))
                link(v.bn_aggr(mv[n % 2], stats))
                v.tensor_scalar(mv[n % 2][:, 1:2], mv[n % 2][:, 1:2], LN_EPS, None, ALU.add).then_inc(eps_rdy, 1)
                return n

            def normalise_b(t, n, into):
                dve.wait_ge(rstd_rdy, n + 1)
                return v.tensor_scalar(into, x[:, t, :], mv[n % 2][:, 0:1], rstd[n % 2], ALU.subtract, ALU.mult)

            def quantise(src, amax, rscale, scale, mag, into, done):
                link(v.tensor_reduce(amax, src, AX_X, ALU.max, apply_absolute_value=True))
                link(v.tensor_scalar(scale, amax, float(np.float32(1) / np.float32(127)), 1e-8, ALU.mult, ALU.max))
                link(v.reciprocal(rscale, scale))
                link(v.tensor_scalar(mag, src, rscale, 127.0, ALU.mult, ALU.min))
                link(v.tensor_scalar(mag, mag, -127.0, MAGIC, ALU.max, ALU.add))
                v.tensor_scalar(into, mag, -MAGIC, None, ALU.add).then_inc(done, 1)

            v.memset(zeros[:, :], 0.0).then_inc(zero_rdy, 1)
            link(v.memset(neghalf, -0.5))
            link(v.memset(eul, float(np.exp(np.float64(1.0)))))
            dve.wait_ge(ld_x, 48)
            link(v.tensor_copy(identb[:, :], ident[:, :]))
            link(v.tensor_copy(segf, segi[:, :]))
            link(v.tensor_scalar(seglo, segf, float(-LOOKBACK), None, ALU.add))
            normalise_a(0)
            for t in range(TILES):
                if t + 1 < TILES:
                    normalise_a(t + 1)
                if t >= 2:
                    dve.wait_ge(xnT_mm, t - 1)
                normalise_b(t, t, xn[t % 2]).then_inc(xn_rdy, 1)
                dve.wait_ge(xn_rdy, t + 1)
            dve.wait_ge(ld_const, 32)
            cosr, sinr = (tabs[:, i, 0:K0].unsqueeze(1).to_broadcast([P, B, K0]) for i in (2, 3))
            as_b = "p (b k) -> p b k"
            dve.wait_ge(rope_mm, 1)
            link(v.tensor_tensor(ropet[0].rearrange(as_b, b=B), bank(7).rearrange(as_b, b=B), cosr, ALU.mult))
            dve.wait_ge(rope_mm, 2)
            link(v.tensor_tensor(ropet[1].rearrange(as_b, b=B), bank(6).rearrange(as_b, b=B), sinr, ALU.mult))
            link(v.tensor_tensor(kf0[1][KVC:P, :], ropet[0][KVC:P, :], ropet[1][KVC:P, :], ALU.add))
            v.tensor_tensor(kf0[0][0:R, :], ropet[0][0:R, :], ropet[1][0:R, :], ALU.add).then_inc(rope_done, 1)
            dve.wait_ge(rope_done, 1)
            dve.wait_ge(ld_seg, 16)
            link(v.tensor_copy(segrowf, segrow))
            link(v.tensor_reduce(far[0:1], segrowf, AX_X, ALU.max))
            link(v.tensor_reduce(g_mx[0:1], segrowf, AX_X, ALU.min))
            link(v.tensor_scalar(far[0:1], far[0:1], float(K0 - 1), None, ALU.is_gt))
            link(v.tensor_scalar(g_mx[0:1], g_mx[0:1], 0.0, far[0:1], ALU.is_lt, ALU.max))
            v.tensor_copy(fari[0:1, :], g_mx[0:1]).then_inc(far_rdy, 1)

            def mask(t):
                if t >= 2:
                    dve.wait_ge(s_mm, 2 * (t - 1))
                link(v.tensor_scalar(xmag[:, 0:K0], kk[:, :], segf[:, t:t + 1], MASK, ALU.is_le, ALU.mult))
                link(v.tensor_scalar(xmag[:, K0:2 * K0], kk[:, :], seglo[:, t:t + 1], MASK, ALU.is_ge, ALU.mult))
                v.scalar_tensor_tensor(out=maskb[t % 2], in0=xmag[:, 0:K0], scalar=-2 * MASK, in1=xmag[:, K0:2 * K0],
                                       op0=ALU.add, op1=ALU.add).then_inc(mask_rdy, 1)
                dve.wait_ge(mask_rdy, t + 1)

            mask(0)
            mask(1)

            def round_weights(n):
                m, o = n // FC, n % FC
                if n == 0:
                    dve.wait_ge(ld_w1, 96)
                quantise(wnat[:, m, o, :], wam[:, n:n + 1], wrs[:, n:n + 1], wsc[:, n:n + 1], wmag[:, m, o, :],
                         (wint, wint2)[m][:, o, :], wint_rdy if o == FC - 1 else dve_chain)
                if o < FC - 1:
                    chain[0] += 1

            for hf in range(2):
                for h in range(H):
                    n = hf * H + h
                    q = qf(h)[:, hf * 512:(hf + 1) * 512].rearrange(as_b, b=2)
                    cosq = tabs[:, h % 2, :].unsqueeze(1).to_broadcast([P, 2, LQ])
                    dve.wait_ge(qa_mm, n + 1)
                    v.tensor_tensor(q, bank(n % 4).rearrange(as_b, b=2), cosq, ALU.mult).then_inc(qa_ev, 1)
                    if h % 2 == 1:
                        k = hf * (H // 2) + h // 2
                        dve.wait_ge(qb_mm, k + 1)
                        if k >= 2:
                            dve.wait_ge(q_rdy, 2 * k - 2)
                        sinq = tabs[:, 3, :].unsqueeze(1).to_broadcast([P, 2, LQ])
                        v.tensor_tensor(ropet[k % 2].rearrange(as_b, b=2),
                                        bank(4 + k % 2).rearrange(as_b, b=2), sinq, ALU.mult).then_inc(qb_ev, 1)
                    if n in ROUND_AFTER:
                        round_weights(ROUND_AFTER.index(n))

            for t in range(TILES + 1):
                if t < TILES:
                    if t >= 2:
                        dve.wait_ge(pt_mm, 4 * (t - 1))
                    elif t == 0:
                        dve.wait_ge(qb_mm, H)
                        dve.wait_ge(qb_ev, H)
                    for j in range(2):
                        dve.wait_ge(s_mm, 2 * t + j + 1)
                        heads = slice(j * H // 2, (j + 1) * H // 2)
                        s4 = bank(2 * j, 2).rearrange("p (h n) -> p h n", h=H // 2)
                        link(v.tensor_reduce(mx0[:, heads], s4, AX_X, ALU.max))
                        v.tensor_tensor(sm[t % 2][:, heads, :], s4,
                                        mx0[:, heads].unsqueeze(2).to_broadcast([P, H // 2, K0]), ALU.subtract)\
                            .then_inc(s_sub, 1)
                    if t + 2 < TILES:
                        mask(t + 2)
                if t < TILES:
                    for j in range(2):
                        heads = slice(j * H // 2, (j + 1) * H // 2)
                        dve.wait_ge(s_exp, 2 * t + j + 1)
                        link(v.tensor_reduce(den0[:, heads], sm[t % 2][:, heads, :], AX_X, ALU.add))
                        v.reciprocal(rec0[t % 2][:, heads], den0[:, heads]).then_inc(s_rec, 1)
                if t >= 1:
                    dve.wait_ge(ao_mm, t)
                    v.tensor_tensor(x[:, t - 1, :], x[:, t - 1, :], bank(7)[:, 0:D], ALU.add).then_inc(x1_rdy, 1)
            dve.wait_ge(x1_rdy, TILES)
            far_ids(dve, general_vector)
            v.memset(vx[:, :, :, :, DH:VW].rearrange("p r k h n -> p (r k) (h n)"), 1.0).then_inc(vone_rdy, 1)

            def top_two(t):
                dve.wait_ge(rt_mm, t + 1)
                v.tensor_copy(lg, bank(3)[:, 0:E]).then_inc(lg_rdy, 1)
                dve.wait_ge(lg_rdy, t + 1)
                link(v.max(top8, lg))
                link(v.max_index(top8i[:, :], top8, lg))
                link(v.tensor_copy(idf, top8i[:, :]))
                v.tensor_scalar(ntop, top8[:, 0:2], -1.0, 80.0, ALU.mult, ALU.min).then_inc(ntop_rdy, 1)

            def place_probs(t):
                dve.wait_ge(pow_rdy, t + 1)
                link(v.tensor_scalar(sigd, sig[t % 2], 1.0, None, ALU.add))
                link(v.reciprocal(sigr, sigd))
                link(v.tensor_scalar(pe0, kk[:, 0:E], idf[:, 0:1], sigr[:, 0:1], ALU.is_equal, ALU.mult))
                link(v.tensor_scalar(pe1, kk[:, 0:E], idf[:, 1:2], sigr[:, 1:2], ALU.is_equal, ALU.mult))
                v.tensor_tensor(probs[t % 2], pe0, pe1, ALU.add).then_inc(p_rdy, 1)
                dve.wait_ge(p_rdy, t + 1)

            def hidden(t, c):
                n = 5 * t + c
                dve.wait_ge(silu_rdy, 9 * t + min(2 * c + 2, HB))
                if c == 0 and t >= 2:
                    dve.wait_ge(ht_mm, 3 * (t - 1))
                src = bank(n % 3)
                if c < 4:
                    for e in range(2):
                        k = 2 * c + e
                        last = v.scalar_tensor_tensor(out=hid[t % 2][:, k, :], in0=src[:, (2 * e + 1) * I:(2 * e + 2) * I],
                                                      scalar=probs[t % 2][:, k:k + 1], in1=sg[n % 2][:, e, :],
                                                      op0=ALU.mult, op1=ALU.mult)
                else:
                    last = v.tensor_tensor(hid[t % 2][:, E, :], src[:, I:2 * I], sg[n % 2][:, 0, :], ALU.mult)
                last.then_inc(hid_rdy, 1)

            def max_chunk(quad, n):
                m = CH[n % len(CH)][1]
                ca = 8 * len(CH) * quad + n
                dve.wait_ge(mx_mm, ca + 1)
                v.tensor_reduce(mxc[quad % 2][:, n:n + 1], bank(ca % 2)[:, 0:m], AX_X, ALU.max).then_inc(mx_rdy, 1)
                if n == 8 * len(CH) - 1:
                    dve.wait_ge(mx_rdy, ca + 1)
                    link(v.tensor_reduce(mx1, mxc[quad % 2].rearrange("p (u c) -> p u c", u=8), AX_X, ALU.max))
                    if quad >= 2:
                        dve.wait_ge(sh_mm, quad - 1)
                    s3 = nst[quad % 2]
                    link(v.tensor_scalar(s3[:, :, 0], mx1, -1.0, None, ALU.mult))
                    link(v.scalar_tensor_tensor(out=nrem, in0=mx1, scalar=-1.0, in1=s3[:, :, 0], op0=ALU.mult,
                                                op1=ALU.subtract))
                    link(v.tensor_copy(s3[:, :, 1], nrem))
                    v.tensor_tensor(s3[:, :, 2], nrem, s3[:, :, 1], ALU.subtract).then_inc(nst_rdy, 1)

            def first_maxima(t, third):
                for n in first_chunks(t, third):
                    max_chunk(0, n)

            def norm_f_b(t, n):
                if t >= 1:
                    dve.wait_ge(hT_mm, t)
                normalise_b(t, n, xn[0]).then_inc(f_rdy, 1)
                dve.wait_ge(f_rdy, t + 1)

            n0, n1 = normalise_a(0), normalise_a(1)
            norm_f_b(0, n0)
            norm_f_b(1, n1)
            top_two(0)
            place_probs(0)
            for t in range(TILES + 2):
                if t < TILES:
                    hidden(t, 0)
                    hidden(t, 1)
                    hidden(t, 2)
                else:
                    first_maxima(t, 0)
                if 1 <= t <= TILES:
                    dve.wait_ge(dn_mm, t)
                    v.tensor_tensor(x[:, t - 1, :], x[:, t - 1, :], bank(6)[:, 0:D], ALU.add).then_inc(x2_rdy, 1)
                    dve.wait_ge(x2_rdy, t)
                    nq = normalise_a(t - 1)
                if t + 2 < TILES:
                    nf = normalise_a(t + 2)
                if t + 1 < TILES:
                    top_two(t + 1)
                if 1 <= t <= TILES:
                    link(normalise_b(t - 1, nq, xn[1]))
                if t + 2 < TILES:
                    norm_f_b(t + 2, nf)
                if t < TILES:
                    hidden(t, 3)
                else:
                    first_maxima(t, 1)
                if t >= 2:
                    dve.wait_ge(q1_mm, t - 1)
                    if t >= 3:
                        dve.wait_ge(q1T_mm, t - 2)
                    link(v.scalar_tensor_tensor(out=qtok, in0=bank(7)[:, 0:D], scalar=xsc[(t - 2) % 3],
                                                in1=SWQ, op0=ALU.mult, op1=ALU.mult))
                    v.tensor_tensor(qtok, qtok, BQ, ALU.add).then_inc(q1_rdy, 1)
                if t + 1 < TILES:
                    place_probs(t + 1)
                if 1 <= t <= TILES:
                    if t >= 3:
                        dve.wait_ge(xqT_mm, t - 2)
                    quantise(xn[1], xam, xrs, xsc[(t - 1) % 3], xmag, xq[(t - 1) % 2], xq_rdy)
                if t < TILES:
                    hidden(t, 4)
                else:
                    first_maxima(t, 2)

            def out_norm(quad):
                dve.wait_ge(ot_mm, quad + 1)
                o4 = bank(7)[:, 0:2 * P].rearrange("p (t h n) -> p t h n", t=2, h=4)
                r8 = recd.rearrange("p (t h) -> p t h", t=2)
                link(v.reciprocal(r8, o4[:, :, :, DH]))
                g = quad % 4
                dst = otok[quad // 4 % 2][:, :, g * 64:(g + 1) * 64]
                v.tensor_tensor(dst.rearrange("p t (h n) -> p t h n", h=4), o4[:, :, :, 0:DH],
                                r8.unsqueeze(3).to_broadcast([P, 2, 4, DH]), ALU.mult).then_inc(o_rdy, 1)

            def value_bias(quad, between):
                g, b = quad % 4, quad // 4
                dst = otok[b % 2][:, :, g * 64:(g + 1) * 64]
                dve.wait_ge(o_rdy, quad + 1)
                link(v.tensor_tensor(dst, dst, BV[:, g * 64:(g + 1) * 64].unsqueeze(1).to_broadcast([P, 2, 64]),
                                     ALU.add))
                between()
                v.tensor_reduce(qam[:, :, g], dst, AX_X, ALU.max, apply_absolute_value=True).then_inc(qam_rdy, 1)
                if g == 2:
                    x2 = x[:, 2 * b:2 * b + 2, :]
                    link(v.tensor_tensor(x2, x2, BP.unsqueeze(1).to_broadcast([P, 2, D]), ALU.add))

            def tail(b, part, between):
                tiles = range(2)
                o2, x2 = otok[b % 2], x[:, 2 * b:2 * b + 2, :]
                if part == "scale":
                    dve.wait_ge(qam_rdy, 4 * (b + 1))
                    link(v.tensor_reduce(oam, qam, AX_X, ALU.max))
                    link(v.tensor_scalar(osc[b % 2], oam, float(np.float32(1) / np.float32(127)), 1e-8, ALU.mult,
                                         ALU.max))
                    link(v.reciprocal(ors, osc[b % 2]))
                    between()
                    for i in tiles:
                        link(v.tensor_scalar(o2[:, i, :], o2[:, i, :], ors[:, i:i + 1], 127.0, ALU.mult, ALU.min))
                elif part == "round":
                    link(v.tensor_scalar(o2, o2, -127.0, MAGIC, ALU.max, ALU.add))
                    between()
                    v.tensor_scalar(xq2, o2, -MAGIC, None, ALU.add).then_inc(oi_rdy, 1)
                elif part == "project":
                    dve.wait_ge(wp_mm, b + 1)
                    for i in tiles:
                        last = v.scalar_tensor_tensor(out=mag2[:, i, :], in0=bank(7)[:, i * D:(i + 1) * D],
                                                      scalar=osc[b % 2][:, i:i + 1], in1=SWP, op0=ALU.mult,
                                                      op1=ALU.mult)
                    last.then_inc(wp_ev, 1)
                elif part == "residual":
                    dve.wait_ge(wp_ev, b + 1)
                    v.tensor_tensor(x2, x2, mag2, ALU.add).then_inc(x3_rdy, 1)
                elif part == "moments":
                    dve.wait_ge(x3_rdy, b + 1)
                    for i in tiles:
                        last = v.bn_stats(stats3[:, i, :], x2[:, i, :])
                    link(last)
                elif part == "variance":
                    for i in tiles:
                        last = v.bn_aggr(mv3[:, i, :], stats3[:, i, :])
                    link(last)
                    v.tensor_scalar(mv3[:, :, 1], mv3[:, :, 1], LN_EPS, None, ALU.add).then_inc(n3_eps, 1)
                elif part == "norm":
                    dve.wait_ge(n3_rstd, b + 1)
                    for i in tiles:
                        last = v.tensor_scalar(xn[i], x2[:, i, :], mv3[:, i, 0:1], rstd3[:, i:i + 1], ALU.subtract,
                                               ALU.mult)
                    last.then_inc(n3_rdy, 1)
                elif part == "up":
                    dve.wait_ge(up_mm, b + 1)
                    v.tensor_scalar(upT, bank(tail_bank(b, part)).rearrange("p (c t) -> p c t", c=FC), 0.0, None, ALU.max)\
                        .then_inc(up_rdy, 1)
                elif part == "gate":
                    dve.wait_ge(rt_mm, TILES + b + 1)
                    v.tensor_copy(lg1, bank(tail_bank(b, part))[:, 0:2 * E].rearrange("p (t e) -> p t e", t=2)).then_inc(lg1_rdy, 1)
                    dve.wait_ge(lg1_rdy, b + 1)
                    for i in tiles:
                        last = v.max(top1[:, i, :], lg1[:, i, :])
                    link(last)
                    v.tensor_tensor(dtop, top1[:, :, 1], top1[:, :, 0], ALU.subtract).then_inc(dtop_rdy, 1)
                elif part == "down":
                    dve.wait_ge(d_mm, b + 1)
                    v.tensor_tensor(mag2, x2, bank(tail_bank(b, part)).rearrange("p (t d) -> p t d", t=2), ALU.add)\
                        .then_inc(d_rdy, 1)
                    between()
                    dve.wait_ge(etop_rdy, b + 1)
                    link(v.tensor_scalar(rden, etop, 1.0, None, ALU.add))
                    link(v.reciprocal(rden, rden))
                    link(v.tensor_tensor(rsum, etop, rden, ALU.mult))
                    link(v.tensor_tensor(rsum, rsum, rden, ALU.add))
                elif part == "expert":
                    dve.wait_ge(y_mm, b + 1)
                    dve.wait_ge(d_rdy, b + 1)
                    for i in tiles:
                        if b >= 1:
                            dve.wait_ge(stored[i], 16 * b)
                        v.scalar_tensor_tensor(out=y[i][:, :], in0=bank(tail_bank(b, part))[:, i * D:(i + 1) * D],
                                               scalar=rsum[:, i:i + 1], in1=mag2[:, i, :], op0=ALU.mult,
                                               op1=ALU.add).then_inc(y_rdy, 1)

            dve.wait_ge(x2_rdy, TILES)
            v.memset(bank(6), 0.0).then_inc(po_zero, 1)
            for quad in range(QUADS + 2):
                for kt in range(KT):
                    jobs = BESIDE.get((quad, kt), [])
                    maxima = [j for j in jobs if j[0] == "max"]

                    def next_max():
                        if maxima:
                            max_chunk(*maxima.pop(0)[1:])

                    next_max()
                    while maxima and not any(kind(j) in ALONE for j in jobs):
                        next_max()
                    for what, *a in jobs:
                        if what == "out":
                            out_norm(*a)
                        elif what == "bias":
                            value_bias(*a, next_max)
                        elif what == "tail":
                            tail(*a, next_max)
                    while maxima:
                        next_max()


def kernel(**inputs):
    import concourse.bacc as _bacc
    from concourse.bass_utils import run_bass_kernel_spmd as _run

    def chunks(w):
        return w.reshape(w.shape[0] // P, P, -1).transpose(1, 0, 2)

    a = {k: np.asarray(v) for k, v in inputs.items()}
    ctx = a["ctx_2048"]
    ctxT = ctx.transpose(0, 2, 1).reshape(B, FC, P, KEYS).transpose(0, 2, 1, 3)
    ctx0 = ctx[:, :K0].transpose(2, 0, 1).reshape(FC, P, B * K0).transpose(1, 0, 2)
    half = R // 2
    swap = np.r_[half:R, 0:half]
    wkr = a["L0_xattn_W_kr"]
    wqr = a["L0_xattn_W_qr"].reshape(QC, H, R)
    inv = (1.0 / 10000.0 ** (np.arange(half, dtype=np.float32) / np.float32(half))).astype(np.float32)
    ang = (np.arange(KEYS, dtype=np.float32)[:, None] * inv).T
    cos, sin = np.cos(ang).astype(np.float32), np.sin(ang).astype(np.float32)
    keyrope = np.concatenate([np.concatenate([cos] * 4), np.concatenate([-sin, sin] * 2)], 1)
    cos, sin = cos[:, 0:LQ], sin[:, 0:LQ]
    cos2, sin2, one = np.concatenate([cos, cos]), np.concatenate([-sin, sin]), np.ones((KVC, LQ), np.float32)
    tabs = np.stack([np.concatenate(z) for z in ((cos2, one), (one, cos2), (cos2, cos2), (sin2, sin2))], 1)
    gu = a["L0_ffn_gate_up_w"].transpose(1, 0, 2).reshape(D, E * 2 * I)
    rows = np.stack([a["L1_xattn_bq"], a["L1_xattn_bkv"][D:], a["L1_xattn_bp"]])
    vals = {
        "x": a["x"].reshape(TOK, D), "ctx": ctxT, "ctx0": ctx0,
        "seg": a["itok_BxS_0_1023"].reshape(TILES, P).T,
        "ident": np.eye(P, dtype=np.float32), "tabs": tabs,
        "kk": np.broadcast_to(np.arange(P, dtype=np.float32), (P, P)),
        "ones": np.ones((3, 2, HALF, KEYS), mybir.dt.np(BF16)),
        "wkvc": chunks(np.concatenate([a["L0_xattn_W_kvc"]] * 2, 1)),
        "wkr": np.concatenate([wkr, wkr], 1), "wkrs": np.concatenate([wkr[:, swap]] * 2, 1),
        "wdq": chunks(a["L0_xattn_W_dq"]),
        "wuq": a["L0_xattn_W_uq"].reshape(QC, H, HD).transpose(2, 1, 0),
        "wuk": a["L0_xattn_W_uk"].reshape(KVC, H, HD).transpose(2, 1, 0),
        "wqr": wqr, "wqrs": wqr[:, :, swap].reshape(QC, H // 2, 2 * R),
        "wuv": a["L0_xattn_W_uv"].reshape(KVC, H, HD).transpose(2, 1, 0),
        "wo": a["L0_xattn_W_o"].reshape(H, HD, D).transpose(1, 0, 2),
        "router": chunks(a["L0_ffn_router_w"]), "gu": chunks(gu),
        "sgu": chunks(np.concatenate([a["L0_ffn_shared_gate_w"], a["L0_ffn_shared_up_w"]], 1)),
        "down": a["L0_ffn_down_w"].transpose(1, 0, 2), "sdown": a["L0_ffn_shared_down_w"],
        "wq": chunks(a["L1_xattn_wq"]), "wp": chunks(a["L1_xattn_wp"]), "wkv": chunks(a["L1_xattn_wkv"].T),
        "bk": a["L1_xattn_bkv"][:D].reshape(FC, P).T,
        "rows": np.broadcast_to(rows, (P, 3, D)),
        "wup": chunks(a["L1_ffn_W_up"].T), "wdn": chunks(a["L1_ffn_W_down"].T), "wex": chunks(a["L1_ffn_W_expert"]),
        "wg": chunks(a["L1_ffn_W_gate"].T),
        "segrow": a["itok_BxS_0_1023"].reshape(1, TOK), "keyrope": keyrope,
        "keyid": np.broadcast_to(np.arange(KEYS, dtype=np.float32), (P, KEYS)),
    }
    nc = _bacc.Bacc("TRN2", target_bir_lowering=False, num_devices=1)
    arrays, args = {}, []
    for name, val in vals.items():
        val = np.ascontiguousarray(val)
        arrays[f"in_{name}_dram"] = val
        args.append(nc.dram_tensor(f"in_{name}_dram", val.shape, mybir.dt.from_np(val.dtype),
                                   kind="ExternalInput").ap())
    args.append(nc.dram_tensor("out_0_dram", (TOK, D), F32, kind="ExternalOutput").ap())
    program(nc, *args)
    r = _run(nc, [arrays], core_ids=[0])
    return r.results[0]["out_0_dram"].reshape(B, LQ, D)
```
